# Optimizing a Trainium2 kernel written in Bass

```python
import numpy as np
import jax
import jax.numpy as jnp

def _softmax(x, axis=-1):
    return jax.nn.softmax(x, axis=axis)

def _gelu(x):
    return jax.nn.gelu(x, approximate=True)

def _silu(x):
    return jax.nn.silu(x)

def _sigmoid(x):
    return jax.nn.sigmoid(x)

def _layernorm(x, axis=-1, eps=1e-05):
    m = jnp.mean(x, axis=axis, keepdims=True)
    v = jnp.var(x, axis=axis, keepdims=True)
    return (x - m) / jnp.sqrt(v + eps)

def _scatter_add(tgt, idx, src, axis=0):
    return tgt.at[idx].add(src)

def _segment_sum(src, seg, n):
    return jax.ops.segment_sum(src, seg, n)
kernel_name = 'mk_perceiver_d1_seqx_r8_c248aa'

def setup_inputs(seed: int=0):
    np.random.seed(seed)
    _w = jnp.asarray

    def _rec_inputs():
        import jax
        import jax.numpy as jnp
        _rk = jax.random.key(seed)
        x = -0.0003929 + 0.9999 * jax.random.normal(jax.random.fold_in(_rk, 1), (1, 64, 512), jnp.float32)
        _lenS = 64 - jax.random.randint(jax.random.fold_in(_rk, 7), (1,), 0, max(1, 64 // 4) + 1, jnp.int32)
        _lenS2 = 6272 - jax.random.randint(jax.random.fold_in(_rk, 8), (1,), 0, max(1, 6272 // 4) + 1, jnp.int32)
        _ctx_4096P = jax.random.normal(jax.random.fold_in(_rk, 11), (1, 16, 512), jnp.float32)
        _ctx_4096c = jax.random.dirichlet(jax.random.fold_in(_rk, 511), 0.3 * jnp.ones((16,), jnp.float32), (1, 6272))
        _ctx_4096t = jnp.einsum('bsk,bkd->bsd', _ctx_4096c, _ctx_4096P)
        _ctx_4096t = _ctx_4096t * jax.lax.rsqrt(jnp.mean(jnp.square(_ctx_4096t)) + 1e-12) * 0.953939
        ctx_4096 = 2.81802e-05 + 1.00001 * (_ctx_4096t + 0.3 * jax.random.normal(jax.random.fold_in(_rk, 611), (1, 6272, 512), jnp.float32))
        _validS = jnp.arange(64)[None, :] < _lenS[:, None]
        _validS2 = jnp.arange(6272)[None, :] < _lenS2[:, None]
        _causal = jnp.tril(jnp.ones((64, 64), dtype=bool))
        mask_BxSxS2_ff0 = jnp.where(jnp.ones((1, 64, 6272), dtype=bool), 0.0, -1000000000.0).astype(jnp.float32)
        return (x, ctx_4096, mask_BxSxS2_ff0)
    x, ctx_4096, mask_BxSxS2_ff0 = _rec_inputs()

    def _L0_xattn_setup():
        import jax, jax.numpy as jnp
        import numpy as np
        B, S, D = (4, 128, 512)
        HQ, HKV, DK, DV = (32, 8, 128, 128)

        def apply_rope(x, positions):
            d = x.shape[-1]
            inv_freq = 1.0 / 10000.0 ** (jnp.arange(0, d, 2, dtype=jnp.float32) / d)
            ang = positions.astype(jnp.float32)[:, None] * inv_freq[None, :]
            cos = jnp.cos(ang)[None, None]
            sin = jnp.sin(ang)[None, None]
            x1, x2 = (x[..., :d // 2], x[..., d // 2:])
            return jnp.concatenate([x1 * cos - x2 * sin, x2 * cos + x1 * sin], axis=-1)
        key = jax.random.key(seed)
        ks = jax.random.split(key, 8)
        return {'query': jax.random.normal(ks[0], (B, S, D), jnp.float32), 'key': jax.random.normal(ks[1], (B, S, D), jnp.float32), 'value': jax.random.normal(ks[2], (B, S, D), jnp.float32), 'mask': jnp.zeros((B, S, S), jnp.float32), 'wq': jax.random.normal(ks[3], (D, HQ * DK), jnp.float32) * 0.02, 'wk': jax.random.normal(ks[4], (D, HKV * DK), jnp.float32) * 0.02, 'wv': jax.random.normal(ks[5], (D, HKV * DV), jnp.float32) * 0.02, 'wo': jax.random.normal(ks[6], (HQ * DV, D), jnp.float32) * 0.02, 'curr_seq_pos': 0}
    _L0_xattn_all = _L0_xattn_setup()
    _L0_xattn_in = {k: v for k, v in _L0_xattn_all.items() if k in ('wq', 'wk', 'wv', 'wo')}
    del _L0_xattn_all

    def _L0_attn_setup():
        import math
        import jax, jax.numpy as jnp
        import numpy as np
        IN_F, OUT_F, HID = (512, 512, 512)
        WINDOW, STRIPES = (6, 3)

        def make_sparse_mask(n_in=IN_F, n_out=OUT_F, window=WINDOW, stripes=STRIPES):
            m = np.zeros((n_in, n_out), dtype=np.float32)
            stride = int(math.sqrt(n_in))
            for k in range(stripes):
                ps = stride * k
                for i in range(0, n_in, window):
                    m[ps + i:ps + i + window, i:i + window] = 1.0
            mb = m.astype(bool)
            return jnp.asarray((mb | mb.T).astype(np.float32))
        key = jax.random.key(seed)
        k1, k2, k3, k4 = jax.random.split(key, 4)
        scale = 1.0 / math.sqrt(IN_F)
        x = jax.random.normal(k1, (8, 96, IN_F), dtype=jnp.float32)
        w1 = jax.random.normal(k2, (HID, IN_F), dtype=jnp.float32) * scale
        w2 = jax.random.normal(k3, (OUT_F, HID), dtype=jnp.float32) * scale
        b2 = jax.random.normal(k4, (OUT_F,), dtype=jnp.float32) * scale
        return {'x': x, 'w1': w1, 'w2': w2, 'b2': b2, 'sparse_mask': make_sparse_mask()}
    _L0_attn_all = _L0_attn_setup()
    _L0_attn_in = {k: v for k, v in _L0_attn_all.items() if k in ('w1', 'w2', 'b2', 'sparse_mask')}
    del _L0_attn_all

    def _L0_ffn_setup():
        import jax, jax.numpy as jnp
        import numpy as np
        N_STREAMS = 4
        DIM = 128
        SINKHORN_ITERS = 50
        SINKHORN_TAU = 0.1
        RMS_EPS = 1.1920929e-07

        def sinkhorn_log(logits, num_iters=SINKHORN_ITERS, tau=SINKHORN_TAU):
            Z = logits / tau
            u0 = jnp.zeros(Z.shape[:-1], Z.dtype)
            v0 = jnp.zeros_like(u0)

            def step(carry, _):
                u, v = carry
                u = -jax.nn.logsumexp(Z + v[..., None, :], axis=-1)
                v = -jax.nn.logsumexp(Z + u[..., :, None], axis=-2)
                return ((u, v), None)
            (u, v), _ = jax.lax.scan(step, (u0, v0), None, length=num_iters)
            return jnp.exp(Z + u[..., :, None] + v[..., None, :])
        key = jax.random.key(seed)
        ks = jax.random.split(key, 6)
        B, T = (4, 256)
        n, C = (N_STREAMS, DIM)
        wd = n * C
        x = jax.random.normal(ks[0], (B, T, wd), dtype=jnp.float32)
        W_res = 0.01 * jax.random.normal(ks[1], (n * n, wd), dtype=jnp.float32)
        W_pre = 0.01 * jax.random.normal(ks[2], (n, wd), dtype=jnp.float32)
        W_post = 0.01 * jax.random.normal(ks[3], (n, wd), dtype=jnp.float32)
        H_res_base = jnp.full((n, n), -0.5, dtype=jnp.float32)
        H_res_base = H_res_base.at[jnp.arange(n), jnp.arange(n)].set(0.0)
        H_pre_base = jnp.zeros((n,), dtype=jnp.float32).at[0].set(1.0)
        H_post_base = jnp.zeros((n,), dtype=jnp.float32)
        gate = jnp.array([5.0], dtype=jnp.float32)
        W_branch = 1.0 / np.sqrt(C) * jax.random.normal(ks[4], (C, C), dtype=jnp.float32)
        return {'x': x, 'W_res': W_res, 'W_pre': W_pre, 'W_post': W_post, 'H_res_base': H_res_base, 'H_pre_base': H_pre_base, 'H_post_base': H_post_base, 'gate': gate, 'W_branch': W_branch}
    _L0_ffn_all = _L0_ffn_setup()
    _L0_ffn_in = {k: v for k, v in _L0_ffn_all.items() if k in ('W_res', 'W_pre', 'W_post', 'H_res_base', 'H_pre_base', 'H_post_base', 'gate', 'W_branch')}
    del _L0_ffn_all
    return {'x': x, 'ctx_4096': ctx_4096, 'mask_BxSxS2_ff0': mask_BxSxS2_ff0, 'L0_xattn_wq': _L0_xattn_in['wq'], 'L0_xattn_wk': _L0_xattn_in['wk'], 'L0_xattn_wv': _L0_xattn_in['wv'], 'L0_xattn_wo': _L0_xattn_in['wo'], 'L0_attn_w1': _L0_attn_in['w1'], 'L0_attn_w2': _L0_attn_in['w2'], 'L0_attn_b2': _L0_attn_in['b2'], 'L0_attn_sparse_mask': _L0_attn_in['sparse_mask'], 'L0_ffn_W_res': _L0_ffn_in['W_res'], 'L0_ffn_W_pre': _L0_ffn_in['W_pre'], 'L0_ffn_W_post': _L0_ffn_in['W_post'], 'L0_ffn_H_res_base': _L0_ffn_in['H_res_base'], 'L0_ffn_H_pre_base': _L0_ffn_in['H_pre_base'], 'L0_ffn_H_post_base': _L0_ffn_in['H_post_base'], 'L0_ffn_gate': _L0_ffn_in['gate'], 'L0_ffn_W_branch': _L0_ffn_in['W_branch']}

def reference(x, ctx_4096, mask_BxSxS2_ff0, L0_xattn_wq, L0_xattn_wk, L0_xattn_wv, L0_xattn_wo, L0_attn_w1, L0_attn_w2, L0_attn_b2, L0_attn_sparse_mask, L0_ffn_W_res, L0_ffn_W_pre, L0_ffn_W_post, L0_ffn_H_res_base, L0_ffn_H_pre_base, L0_ffn_H_post_base, L0_ffn_gate, L0_ffn_W_branch):
    import jax
    import jax.numpy as jnp

    def _L0_xattn_ref(query, key, value, mask, wq, wk, wv, wo, curr_seq_pos):
        import jax, jax.numpy as jnp
        import numpy as np
        B, S, D = (4, 128, 512)
        HQ, HKV, DK, DV = (32, 8, 128, 128)

        def apply_rope(x, positions):
            d = x.shape[-1]
            inv_freq = 1.0 / 10000.0 ** (jnp.arange(0, d, 2, dtype=jnp.float32) / d)
            ang = positions.astype(jnp.float32)[:, None] * inv_freq[None, :]
            cos = jnp.cos(ang)[None, None]
            sin = jnp.sin(ang)[None, None]
            x1, x2 = (x[..., :d // 2], x[..., d // 2:])
            return jnp.concatenate([x1 * cos - x2 * sin, x2 * cos + x1 * sin], axis=-1)
        bs, sq, _ = query.shape
        sk = key.shape[1]
        n_groups = HQ // HKV
        q = (query @ wq).reshape(bs, sq, HQ, DK).transpose(0, 2, 1, 3)
        k = (key @ wk).reshape(bs, sk, HKV, DK)
        v = (value @ wv).reshape(bs, sk, HKV, DV)
        k = jnp.repeat(k, n_groups, axis=2).transpose(0, 2, 1, 3)
        v = jnp.repeat(v, n_groups, axis=2).transpose(0, 2, 1, 3)
        scale = jnp.sqrt(jnp.float32(DK))
        pos = curr_seq_pos + jnp.arange(sq)
        q = apply_rope(q, pos)
        k = apply_rope(k, curr_seq_pos + jnp.arange(sk))
        scores = jnp.einsum('bhqd,bhkd->bhqk', q, k) / scale
        m = jax.lax.dynamic_slice(mask, (0, curr_seq_pos, 0), (bs, sq, sk))
        attn = jax.nn.softmax(scores + m[:, None, :, :], axis=-1)
        out = jnp.einsum('bhqk,bhkd->bhqd', attn, v)
        out = out.transpose(0, 2, 1, 3).reshape(bs, sq, HQ * DV)
        return out @ wo

    def _L0_attn_ref(x, w1, w2, b2, sparse_mask):
        import math
        import jax, jax.numpy as jnp
        import numpy as np
        IN_F, OUT_F, HID = (512, 512, 512)
        WINDOW, STRIPES = (6, 3)

        def make_sparse_mask(n_in=IN_F, n_out=OUT_F, window=WINDOW, stripes=STRIPES):
            m = np.zeros((n_in, n_out), dtype=np.float32)
            stride = int(math.sqrt(n_in))
            for k in range(stripes):
                ps = stride * k
                for i in range(0, n_in, window):
                    m[ps + i:ps + i + window, i:i + window] = 1.0
            mb = m.astype(bool)
            return jnp.asarray((mb | mb.T).astype(np.float32))
        attn = jnp.einsum('ds,td->st', w1, w2) * sparse_mask
        y = jnp.einsum('bds,st->bdt', x, attn) + b2
        return jax.nn.gelu(y, approximate=False)

    def _L0_ffn_ref(x, W_res, W_pre, W_post, H_res_base, H_pre_base, H_post_base, gate, W_branch):
        import jax, jax.numpy as jnp
        import numpy as np
        N_STREAMS = 4
        DIM = 128
        SINKHORN_ITERS = 50
        SINKHORN_TAU = 0.1
        RMS_EPS = 1.1920929e-07

        def sinkhorn_log(logits, num_iters=SINKHORN_ITERS, tau=SINKHORN_TAU):
            Z = logits / tau
            u0 = jnp.zeros(Z.shape[:-1], Z.dtype)
            v0 = jnp.zeros_like(u0)

            def step(carry, _):
                u, v = carry
                u = -jax.nn.logsumexp(Z + v[..., None, :], axis=-1)
                v = -jax.nn.logsumexp(Z + u[..., :, None], axis=-2)
                return ((u, v), None)
            (u, v), _ = jax.lax.scan(step, (u0, v0), None, length=num_iters)
            return jnp.exp(Z + u[..., :, None] + v[..., None, :])
        B, T, nC = x.shape
        n = N_STREAMS
        C = nC // n
        x_norm = x * jax.lax.rsqrt(jnp.mean(x * x, axis=-1, keepdims=True) + RMS_EPS)
        H_res_logits = (x_norm @ W_res.T).reshape(B, T, n, n) + H_res_base
        H_pre_logits = x_norm @ W_pre.T + H_pre_base
        H_post_logits = x_norm @ W_post.T + H_post_base
        H_res = sinkhorn_log(H_res_logits)
        H_pre = jax.nn.softmax(H_pre_logits, axis=-1)
        H_post = jax.nn.softmax(H_post_logits, axis=-1)
        g = jax.nn.sigmoid(gate)[0]
        I = jnp.eye(n, dtype=H_res.dtype)
        H_res = (1.0 - g) * I + g * H_res
        x_streams = x.reshape(B, T, n, C)
        x_pre = jnp.einsum('btnc,btn->btc', x_streams, H_pre)
        y = x_pre @ W_branch
        x_mixed = jnp.einsum('btij,btjc->btic', H_res, x_streams)
        y_distributed = jnp.einsum('btc,btn->btnc', y, H_post)
        return (x_mixed + y_distributed).reshape(B, T, nC)
    x = x + _L0_xattn_ref(_layernorm(x, axis=-1), ctx_4096, ctx_4096, mask_BxSxS2_ff0, L0_xattn_wq, L0_xattn_wk, L0_xattn_wv, L0_xattn_wo, 0)
    x = x + _L0_attn_ref(_layernorm(x, axis=-1), L0_attn_w1, L0_attn_w2, L0_attn_b2, L0_attn_sparse_mask)
    x = x + _L0_ffn_ref(_layernorm(x, axis=-1), L0_ffn_W_res, L0_ffn_W_pre, L0_ffn_W_post, L0_ffn_H_res_base, L0_ffn_H_pre_base, L0_ffn_H_post_base, L0_ffn_gate, L0_ffn_W_branch)
    return x

_drawn_inputs = setup_inputs


def setup_inputs(seed=0):
    import zlib

    import numpy as np

    out = dict(_drawn_inputs(seed))
    spreads = {'L0_ffn_H_post_base': (0.0, 0.8)}
    factors = {'L0_xattn_wq': 7.127,
     'L0_xattn_wk': 7.225,
     'L0_attn_b2': 2.699,
     'L0_ffn_W_pre': 4.395,
     'L0_ffn_W_post': 3.419}
    for name, (base, spread) in spreads.items():
        noise = np.random.default_rng([zlib.crc32(name.encode()), seed]).standard_normal(out[name].shape)
        drawn = base * np.exp(spread * noise) if base else spread * noise
        out[name] = jnp.asarray(drawn.astype(out[name].dtype))
    for name, factor in factors.items():
        out[name] = (out[name] * factor).astype(out[name].dtype)
    return out
```

```python
from contextlib import ExitStack

import concourse.bass as bass
from concourse import mybir

F32 = mybir.dt.float32
F32R = mybir.dt.float32r
ALU = mybir.AluOpType
ACT = mybir.ActivationFunctionType
AX_X = mybir.AxisListType.X

P = 128
D = 512
DC = D // P
TOK = 64
KEYS = 6272
HQ, HKV, DH = 32, 8, 128
HALF = DH // 2
KT = 7
BK = KT * P
NB = KEYS // BK
HB = BK // 2
UNITS = HKV // 2
QC = HQ // HKV * TOK
PIECES = 4
SCALE = float(DH) ** -0.5
EPS = 1e-5
RMS_EPS = 1.1920929e-07
NS = 4
SINK = 50
INV_TAU = 10.0
SINK_UNROLL = 5
Z_SPREAD_MAX = 150.0
SUM_MAX = 1e25
assert NB * BK == KEYS and UNITS == 4


def piece_tiles(p):
    return range(2 * p, min(2 * p + 2, KT))


def need(eng, sem, value):
    if isinstance(value, int) and value <= 0:
        return
    eng.wait_ge(sem, value)


def perceiver(nc, A):
    with ExitStack() as ctx:
        def sb(name, shape, dt=F32):
            return ctx.enter_context(nc.sbuf_tensor(name, shape, dt))

        def ps(name, shape):
            return ctx.enter_context(nc.psum_tensor(name, shape, F32))

        def sem(name):
            return ctx.enter_context(nc.semaphore(name))

        base = -(-nc.sbuf_base // 32) * 32
        at = [base]

        def region(nbytes):
            here = at[0]
            at[0] += nbytes
            return here

        def place(name, shape, dt, where):
            return nc.alloc_sbuf_tensor_at(name, shape, dt, offset=where)

        R_WK_HI, R_WK_LO, R_WV_HI, R_WV_LO = (region(4 * DC * HKV * DH) for _ in range(4))
        R_CT_HI, R_CT_LO = (region(4 * DC * BK) for _ in range(2))
        R_V = region(4 * 2 * KT * 2 * DH)
        R_S = region(4 * 4 * BK)
        R_PT = region(4 * 2 * 2 * 2 * QC)
        R_ACC = region(4 * HKV * QC)
        R_RAW = region(4 * KT * DC * P)
        arena = sb("arena", [P, (at[0] - base) // 4 + 16])
        assert arena is not None

        wk_hi = place("wk_hi", [P, DC, HKV * DH], F32R, R_WK_HI)
        wk_lo = place("wk_lo", [P, DC, HKV * DH], F32R, R_WK_LO)
        wv_hi = place("wv_hi", [P, DC, HKV * DH], F32R, R_WV_HI)
        wv_lo = place("wv_lo", [P, DC, HKV * DH], F32R, R_WV_LO)
        ct_hi = place("ct_hi", [P, DC, BK], F32R, R_CT_HI)
        ct_lo = place("ct_lo", [P, DC, BK], F32R, R_CT_LO)
        v_hi = place("v_hi", [P, KT, 2 * DH], F32R, R_V)
        v_lo = place("v_lo", [P, KT, 2 * DH], F32R, R_V + 4 * KT * 2 * DH)
        scores = place("scores", [P, 4, BK], F32, R_S)
        pt_hi = place("pt_hi", [P, 2, 2, QC], F32R, R_PT)
        pt_lo = place("pt_lo", [P, 2, 2, QC], F32R, R_PT + 4 * 2 * 2 * QC)
        acc = place("acc", [P, HKV, QC], F32, R_ACC)
        ctx_raw = place("ctx_raw", [P, KT, DC, P], F32, R_RAW)
        stage = [place("stage0", [P, DC, 512], F32, R_PT), place("stage1", [P, DC, 512], F32, R_ACC),
                 place("stage2", [P, DC, 512], F32, R_V), place("stage3", [P, DC, 512], F32, R_S)]
        w1_sb = place("w1_sb", [P, DC, D], F32, R_WK_HI)
        w2t_sb = place("w2t_sb", [P, DC, D], F32, R_WK_HI + 4 * DC * D)
        smask_sb = place("smask_sb", [P, DC, D], F32, R_WK_LO)
        mixw = place("mixw", [P, DC, D], F32, R_WK_LO + 4 * DC * D)
        wo_sb = [place("wo0", [P, 8, D], F32, R_WV_HI), place("wo1", [P, 8, D], F32, R_WV_LO),
                 place("wo2", [P, 14, D], F32, R_CT_HI), place("wo3", [P, 2, D], F32, R_RAW)]
        WO_FIRST = [0, 8, 16, 30, 32]
        assert R_CT_LO == R_CT_HI + 4 * 7 * D

        kt_hi = sb("kt_hi", [P, 2, BK], F32R)
        kt_lo = sb("kt_lo", [P, 2, BK], F32R)
        qt_hi = sb("qt_hi", [P, HQ * TOK], F32R)
        qt_lo = sb("qt_lo", [P, HQ * TOK], F32R)
        mask_sb = sb("mask_sb", [P, BK])
        cos_sb = sb("cos_sb", [P, BK])
        sin_sb = sb("sin_sb", [P, BK])
        rc = sb("rc", [P, 2, 512])
        rs = sb("rs", [P, 2, 512])
        ident = sb("ident", [P, P])
        x_sb = sb("x_sb", [TOK, D])
        xn = sb("xn", [TOK, D])
        xnT = sb("xnT", [P, DC, TOK])
        qtab = sb("qtab", [TOK, 2, HALF])
        bnst = sb("bnst", [TOK, 6])
        mv = sb("mv", [TOK, 4])
        m_run = sb("m_run", [P, 16])
        m_old = sb("m_old", [P, 16])
        m_neg = sb("m_neg", [P, 16])
        m_drop = sb("m_drop", [P, 16])
        fac = sb("fac", [P, 16])
        rsum = sb("rsum", [P, 16])
        l_run = sb("l_run", [P, 16])
        l_inv = sb("l_inv", [P, 16])
        b2_sb = sb("b2_sb", [TOK, D])
        wf_sb = sb("wf_sb", [P, DC, 24])
        hb_sb = sb("hb_sb", [TOK, 24])
        gate_sb = sb("gate_sb", [TOK, 1])
        wb_sb = sb("wb_sb", [P, P])
        eye_sb = sb("eye_sb", [TOK, 16])
        half_sb = sb("half_sb", [TOK, 1])
        lg = sb("lg", [TOK, 24])
        zz = sb("zz", [TOK, 16])
        tt = sb("tt", [TOK, 16])
        ee = sb("ee", [TOK, 16])
        uu = sb("uu", [TOK, 4])
        vv = sb("vv", [TOK, 4])
        mx4 = sb("mx4", [TOK, 4])
        sm4 = sb("sm4", [TOK, 4])
        lns = sb("lns", [TOK, 4])
        hres = sb("hres", [TOK, 16])
        hp = sb("hp", [TOK, 16])
        kk = sb("kk", [TOK, 16])
        zlim = sb("zlim", [TOK, 8])
        sums = sb("sums", [TOK, 2 * SINK_UNROLL, NS])
        sums_max = sb("sums_max", [TOK, 2 * SINK_UNROLL, NS])
        sums_min = sb("sums_min", [TOK, 2 * SINK_UNROLL, NS])
        wide = sb("wide", [1, 2])
        wide_flag = sb("wide_flag", [1, 1], mybir.dt.int32)
        x1 = place("x1", [TOK, D], F32, R_S)
        x2 = place("x2", [TOK, D], F32, R_S + 2048)
        xf = place("xf", [TOK, D], F32, R_S + 4096)
        t0 = place("t0", [TOK, D], F32, R_S + 6144)
        ob = place("ob", [TOK, D], F32, R_S + 8192)
        xpre = place("xpre", [TOK, P], F32, R_S + 10240)
        ybr = place("ybr", [TOK, P], F32, R_S + 10752)
        xpT = place("xpT", [P, TOK], F32, R_S + 11264)

        p_s = ps("p_s", [P, 2, 512])
        p_t = [ps(f"p_t{i}", [P, 512]) for i in range(2)]
        p_kv = [ps(f"p_kv{i}", [P, 512]) for i in range(2)]
        p_o = ps("p_o", [P, 512])
        p_f = ps("p_f", [P, 512])

        x_loaded = sem("x_loaded")
        tail_loaded = sem("tail_loaded")
        stage_loaded = [sem(f"stage_loaded{i}") for i in range(4)]
        ctx_loaded = [sem(f"ctx_loaded{t}") for t in range(KT)]
        rope_loaded = sem("rope_loaded")
        mask_loaded = sem("mask_loaded")
        w12_loaded = sem("w12_loaded")
        smask_loaded = sem("smask_loaded")
        wo_loaded = [sem(f"wo_loaded{i}") for i in range(4)]
        w_hi_ready = sem("w_hi_ready")
        w_lo_ready = sem("w_lo_ready")
        ctx_hi_ready = sem("ctx_hi_ready")
        ctx_lo_ready = sem("ctx_lo_ready")
        q_projected = sem("q_projected")
        q_products = sem("q_products")
        q_rotated = sem("q_rotated")
        q_transposed = sem("q_transposed")
        q_hi_ready = sem("q_hi_ready")
        q_lo_ready = sem("q_lo_ready")
        k_projected = sem("k_projected")
        v_projected = sem("v_projected")
        k_products = sem("k_products")
        k_rotated = sem("k_rotated")
        k_hi_ready = sem("k_hi_ready")
        k_lo_ready = sem("k_lo_ready")
        v_hi_ready = sem("v_hi_ready")
        v_lo_ready = sem("v_lo_ready")
        scores_ready = sem("scores_ready")
        scores_masked = sem("scores_masked")
        max_negated = sem("max_negated")
        max_dropped = sem("max_dropped")
        max_kept = sem("max_kept")
        factor_ready = sem("factor_ready")
        probs_ready = sem("probs_ready")
        sums_kept = sem("sums_kept")
        probs_transposed = sem("probs_transposed")
        pt_hi_ready = sem("pt_hi_ready")
        pt_lo_ready = sem("pt_lo_ready")
        pv_done = sem("pv_done")
        factor_spread = sem("factor_spread")
        acc_scaled = sem("acc_scaled")
        acc_added = sem("acc_added")
        acc_cleared = sem("acc_cleared")
        const_ready = sem("const_ready")
        dve_step = sem("dve_step")
        act_step = sem("act_step")
        pool_step = sem("pool_step")
        pe_step = sem("pe_step")
        out_stored = sem("out_stored")

        sk_shifted = sem("sk_shifted")
        sk_exp = sem("sk_exp")
        sk_summed = sem("sk_summed")
        sk_ln = sem("sk_ln")
        sk_state = sem("sk_state")
        sk_linear = sem("sk_linear")
        sk_limits = sem("sk_limits")

        PE_XNT, PE_MIX = 1, 5
        PE_Y, PE_X1T, PE_Z, PE_XNT3, PE_LOGITS, PE_XPT, PE_BR, PE_WIDE = 6, 7, 8, 9, 10, 11, 12, 13
        DVE_VAR, DVE_XN, DVE_XNT = 3, 4, 5
        DVE_MIX = 7
        DVE_LINV = DVE_MIX + 4 + 1
        DVE_X1 = DVE_LINV + 1
        DVE_VAR2, DVE_XN2, DVE_XNT2 = DVE_X1 + 3, DVE_X1 + 4, DVE_X1 + 5
        DVE_Z = DVE_XNT2 + 1
        DVE_X2 = DVE_Z + 1
        DVE_VAR3, DVE_XF = DVE_X2 + 3, DVE_X2 + 4
        DVE_MS, DVE_XRMS, DVE_XNT3 = DVE_XF + 2, DVE_XF + 3, DVE_XF + 4
        DVE_LG = DVE_XNT3 + 1
        DVE_PMAX = DVE_LG + 2
        DVE_ZS = DVE_PMAX + 6
        DVE_PRE = DVE_ZS + 3
        DVE_XPRE = DVE_PRE + 4
        DVE_XPT = DVE_XPRE + 1
        DVE_YBR = DVE_XPT + 1
        DVE_BOUND = DVE_YBR + 9
        DVE_FLAG = DVE_BOUND + 2
        DVE_END = DVE_FLAG + 4 + 5 * NS

        block = ctx.enter_context(nc.Block())

        STAGED = [("wk", 0), ("wv", 0), ("wq", 0), ("wq", 1), ("wk", 1), ("wv", 1)] + [("wq", i) for i in range(2, 8)]
        W_PIECES = [n for n, (k, _) in enumerate(STAGED) if k != "wq"]
        Q_PIECES = [n for n, (k, _) in enumerate(STAGED) if k == "wq"]

        @block.sync
        def _(sp):
            def load_stage(n):
                kind, i = STAGED[n]
                src = {"wk": A["wk"], "wv": A["wv"], "wq": A["wq"]}[kind]
                if n >= 4:
                    if STAGED[n - 4][0] == "wq":
                        sp.wait_ge(q_projected, Q_PIECES.index(n - 4) + 1)
                    else:
                        sp.wait_ge(w_lo_ready, W_PIECES.index(n - 4) + 1)
                        sp.wait_ge(w_hi_ready, W_PIECES.index(n - 4) + 1)
                sp.dma_start(stage[n % 4][:, :, :],
                             src[:, i * 512:(i + 1) * 512].rearrange("(c p) n -> p c n", p=P)
                             ).then_inc(stage_loaded[n % 4], 16)

            def load_rope(b):
                need(sp, k_products, 16 * b)
                sp.dma_start(cos_sb[:, :], A["cosT"][:, bass.ds(b * BK, BK)]).then_inc(rope_loaded, 16)
                sp.dma_start(sin_sb[:, :], A["sinT"][:, bass.ds(b * BK, BK)]).then_inc(rope_loaded, 16)

            def load_ctx(b, t):
                need(sp, ctx_hi_ready, KT * (b - 1) + t + 1)
                need(sp, ctx_lo_ready, KT * (b - 1) + t + 1)
                sp.dma_start(ctx_raw[:, t, :, :],
                             A["ctxT"][:, bass.ds(b * BK + t * P, P)].rearrange("(c p) n -> p c n", p=P)
                             ).then_inc(ctx_loaded[t], 16)

            def load_mask(b):
                need(sp, scores_masked, 16 * b)
                for h in range(2):
                    sp.dma_start(mask_sb[h * TOK:(h + 1) * TOK, :], A["mask"][:, bass.ds(b * BK, BK)]
                                 ).then_inc(mask_loaded, 16)

            sp.dma_start(x_sb[:, :], A["x"]).then_inc(x_loaded, 16)
            sp.dma_start(ident[:, :], A["ident"]).then_inc(x_loaded, 16)
            sp.dma_start(qtab[:, 0, :], A["qcos"]).then_inc(x_loaded, 16)
            sp.dma_start(qtab[:, 1, :], A["qsin"]).then_inc(x_loaded, 16)
            load_stage(0)
            load_ctx(0, 0)
            load_ctx(0, 1)
            load_rope(0)
            load_ctx(0, 2)
            load_ctx(0, 3)
            load_stage(2)
            load_stage(3)
            for t in range(4, KT):
                load_ctx(0, t)
            load_stage(1)
            load_mask(0)
            for n in range(4, len(STAGED)):
                load_stage(n)
            for dst, src in ((b2_sb, "b2"), (hb_sb, "hbase"), (gate_sb, "gate"), (wb_sb, "wbranch"), (eye_sb, "eye")):
                sp.dma_start(dst[:, :], A[src]).then_inc(tail_loaded, 16)
            sp.dma_start(wf_sb[:, :, :], A["wffn"].rearrange("(c p) n -> p c n", p=P)).then_inc(tail_loaded, 16)

            with sp.Fori(1, NB) as b:
                load_rope(b)
                for t in range(KT):
                    load_ctx(b, t)
                load_mask(b)

            sp.wait_ge(k_projected, 16 * NB)
            sp.dma_start(w1_sb[:, :, :], A["w1"].rearrange("(c p) n -> p c n", p=P)).then_inc(w12_loaded, 16)
            sp.dma_start(w2t_sb[:, :, :], A["w2t"].rearrange("(c p) n -> p c n", p=P)).then_inc(w12_loaded, 16)
            sp.dma_start(smask_sb[:, :, :], A["smask"].rearrange("(c p) n -> p c n", p=P)).then_inc(smask_loaded, 16)
            sp.wait_ge(v_projected, 16 * NB)
            for i in range(4):
                a, z = WO_FIRST[i], WO_FIRST[i + 1]
                sp.dma_start(wo_sb[i][:, :, :], A["wo"][a * P:z * P, :].rearrange("(h p) n -> p h n", p=P)
                             ).then_inc(wo_loaded[i], 16)
            sp.wait_ge(dve_step, DVE_END)
            sp.dma_start(A["out"], ob[:, :]).then_inc(out_stored, 16)
            sp.wait_ge(out_stored, 16)

        def split_matmul(out, w_hi, w_lo, x_hi, x_lo, start, stop):
            nc.tensor.matmul(out, w_hi, x_hi, start=start, stop=False)
            nc.tensor.matmul(out, w_hi, x_lo, start=False, stop=False)
            return nc.tensor.matmul(out, w_lo, x_hi, start=False, stop=stop)

        def pe_project_k(pe, b, g, i):
            u = UNITS * b + g
            head, half = 2 * g + i // 2, i % 2
            if i >= 2:
                need(pe, k_products, 4 * u + i - 1)
            else:
                need(pe, v_lo_ready, 4 * (u - 1) + i + 3)
            if i < 2 and g == 0:
                tiles = KT * b + (i + 1) * KT // 2 + 1 - i
                pe.wait_ge(ctx_hi_ready, tiles)
                pe.wait_ge(ctx_lo_ready, tiles)
            cols = slice(half * HB, (half + 1) * HB)
            for c in range(DC):
                w = slice(head * DH, (head + 1) * DH)
                last = split_matmul(p_kv[i % 2][:, 0:HB], wk_hi[:, c, w], wk_lo[:, c, w],
                                    ct_hi[:, c, cols], ct_lo[:, c, cols], c == 0, c == DC - 1)
            last.then_inc(k_projected, 1)

        def pe_project_v(pe, b, g, i):
            u = UNITS * b + g
            if i >= 2:
                need(pe, v_lo_ready, 4 * u + i - 1)
            else:
                need(pe, k_products, 4 * u + i + 3)
            for j, t in enumerate(piece_tiles(i)):
                for c in range(DC):
                    k = slice(t * P, (t + 1) * P)
                    w = slice(g * 2 * DH, (g + 1) * 2 * DH)
                    last = split_matmul(p_kv[i % 2][:, j * 2 * DH:(j + 1) * 2 * DH], ct_hi[:, c, k], ct_lo[:, c, k],
                                        wv_hi[:, c, w], wv_lo[:, c, w], c == 0, c == DC - 1)
            last.then_inc(v_projected, 1)

        def pe_scores(pe, b, g, s, i):
            u = UNITS * b + g
            h = 2 * u + s
            if i == 0:
                pe.wait_ge(k_lo_ready, 4 * u + 2 * s + 2)
            need(pe, scores_masked, 2 * h + i)
            q = slice((2 * g + s) * QC + i * P, (2 * g + s) * QC + (i + 1) * P)
            for f in range(2):
                k = slice(f * HB, (f + 1) * HB)
                last = split_matmul(p_s[:, f, 0:HB], qt_hi[:, q], qt_lo[:, q], kt_hi[:, s, k], kt_lo[:, s, k], True, True)
            last.then_inc(scores_ready, 1)

        def pe_spread(pe, h, s, g, src):
            for i in range(2):
                col = 2 * (2 * g + s) + i
                last = nc.tensor.transpose(p_f[:, i * P:(i + 1) * P], src[:, col:col + 1].to_broadcast([P, P]), ident[:, :])
            last.then_inc(factor_spread, 1)

        def pe_transpose_probs(pe, h, s, p):
            if p == 0:
                pe.wait_ge(probs_ready, 2 * h + 2)
            need(pe, pt_lo_ready, 4 * h + p - 1)
            for j, t in enumerate(piece_tiles(p)):
                for i in range(2):
                    last = nc.tensor.transpose(p_t[p % 2][:, j * QC + i * P:j * QC + (i + 1) * P],
                                               scores[:, 2 * s + i, t * P:(t + 1) * P], ident[:, :])
            last.then_inc(probs_transposed, 1)

        def pe_pv(pe, h, s, p, v_count):
            pe.wait_ge(pt_lo_ready, 4 * h + p + 1)
            if p == 0:
                need(pe, acc_added, h)
            pe.wait_ge(v_lo_ready, v_count + p + 1)
            for j, t in enumerate(piece_tiles(p)):
                w = slice(s * DH, (s + 1) * DH)
                last = split_matmul(p_o[:, 0:QC], v_hi[:, t, w], v_lo[:, t, w], pt_hi[:, p % 2, j, :], pt_lo[:, p % 2, j, :],
                                    t == 0, t == KT - 1)
            last.then_inc(pv_done, 1)

        def pe_slot(pe, b, g, s, prev=True, last=False):
            u = UNITS * b + g
            h = 2 * u + s
            pg, psn = (g, 0) if s else ((g - 1) % UNITS, 1)
            v_count = 4 * u if s else 4 * (u - 1)

            def fill(i):
                if s == 0:
                    pe_project_v(pe, b, g, i)
                elif g < UNITS - 1:
                    pe_project_k(pe, b, g + 1, i)
                elif not last:
                    pe_project_k(pe, b + 1, 0, i)
                else:
                    pe_mix(pe, i)

            if prev:
                pe_transpose_probs(pe, h - 1, psn, 0)
                pe.wait_ge(factor_ready, 2 * h)
                need(pe, acc_scaled, h - 1)
                pe_spread(pe, h - 1, psn, pg, fac)
            pe_scores(pe, b, g, s, 0)
            if prev:
                pe_transpose_probs(pe, h - 1, psn, 1)
                pe_pv(pe, h - 1, psn, 0, v_count)
            fill(0)
            pe_scores(pe, b, g, s, 1)
            if prev:
                pe_transpose_probs(pe, h - 1, psn, 2)
                pe_pv(pe, h - 1, psn, 1, v_count)
            fill(1)
            if prev:
                pe_transpose_probs(pe, h - 1, psn, 3)
                pe_pv(pe, h - 1, psn, 2, v_count)
            fill(2)
            if prev:
                pe_pv(pe, h - 1, psn, 3, v_count)
            fill(3)

        def pe_mix(pe, i):
            if i == 0:
                pe.wait_ge(w12_loaded, 32)
            if i < 2:
                pe.wait_ge(v_lo_ready, 16 * NB)
            else:
                pe.wait_ge(dve_step, DVE_MIX + i - 1)
            for c in range(DC):
                last = nc.tensor.matmul(p_kv[i % 2][:, :], w1_sb[:, c, i * P:(i + 1) * P], w2t_sb[:, c, :],
                                        start=(c == 0), stop=(c == DC - 1))
            last.then_inc(pe_step, 1)

        @block.tensor
        def _(pe):
            pe.wait_ge(dve_step, DVE_XN)
            pe.wait_ge(x_loaded, 64)
            for c in range(DC):
                last = nc.tensor.transpose(p_o[:, c * TOK:(c + 1) * TOK], xn[:, c * P:(c + 1) * P], ident[0:TOK, 0:TOK])
            last.then_inc(pe_step, 1)
            pe.wait_ge(w_hi_ready, 1)
            pe.wait_ge(w_lo_ready, 1)
            for i in range(4):
                pe_project_k(pe, 0, 0, i)
            pe.wait_ge(dve_step, DVE_XNT)

            def q_heads(n):
                pe.wait_ge(q_rotated, n + 1)
                need(pe, q_lo_ready, n)
                for j in range(4):
                    last = nc.tensor.transpose(p_f[:, j * TOK:(j + 1) * TOK], rc[0:TOK, n % 2, j * DH:(j + 1) * DH],
                                               ident[0:TOK, 0:TOK])
                last.then_inc(q_transposed, 1)

            for n in range(8):
                at_stage = Q_PIECES[n]
                pe.wait_ge(stage_loaded[at_stage % 4], 16 * (at_stage // 4 + 1))
                if n < 2:
                    pe.wait_ge(k_products, 4)
                else:
                    pe.wait_ge(q_products, n - 1)
                for c in range(DC):
                    last = nc.tensor.matmul(p_kv[n % 2][0:TOK, :], xnT[:, c, :], stage[at_stage % 4][:, c, :],
                                            start=(c == 0), stop=(c == DC - 1))
                last.then_inc(q_projected, 1)
                if n:
                    q_heads(n - 1)
            q_heads(7)
            pe.wait_ge(q_hi_ready, 8)
            pe.wait_ge(q_lo_ready, 8)
            pe.wait_ge(w_hi_ready, 4)
            pe.wait_ge(w_lo_ready, 4)

            def pe_block(b, first=False, last=False):
                for g in range(UNITS):
                    for s in range(2):
                        pe_slot(pe, b, g, s, prev=not (first and g == 0 and s == 0), last=last)

            pe_block(0, first=True)
            with pe.Fori(1, NB - 1) as b:
                pe_block(b)
            pe_block(NB - 1, last=True)
            h = 8 * NB - 1
            pe_transpose_probs(pe, h, 1, 0)
            pe.wait_ge(factor_ready, 2 * h + 2)
            pe.wait_ge(acc_scaled, h)
            pe_spread(pe, h, 1, UNITS - 1, fac)
            pe_transpose_probs(pe, h, 1, 1)
            pe_pv(pe, h, 1, 0, 16 * NB - 4)
            pe_transpose_probs(pe, h, 1, 2)
            pe_pv(pe, h, 1, 1, 16 * NB - 4)
            pe_transpose_probs(pe, h, 1, 3)
            pe_pv(pe, h, 1, 2, 16 * NB - 4)
            pe_pv(pe, h, 1, 3, 16 * NB - 4)
            pe.wait_ge(dve_step, DVE_LINV)
            for g in range(HKV):
                pe.wait_ge(acc_scaled, 8 * NB + g)
                pe_spread(pe, None, g % 2, g // 2, l_inv)
            for hq in range(HQ):
                i = max(j for j in range(4) if WO_FIRST[j] <= hq)
                if hq == WO_FIRST[i]:
                    pe.wait_ge(wo_loaded[i], 16)
                if hq % 4 == 0:
                    pe.wait_ge(acc_scaled, 8 * NB + hq // 4 + 1)
                last = nc.tensor.matmul(p_o[0:TOK, :], acc[:, hq // 4, (hq % 4) * TOK:(hq % 4 + 1) * TOK],
                                        wo_sb[i][:, hq - WO_FIRST[i], :], start=(hq == 0), stop=(hq == HQ - 1))
            last.then_inc(pe_step, 1)

            def transpose_rows(src):
                for c in range(DC):
                    last = nc.tensor.transpose(p_f[:, c * TOK:(c + 1) * TOK], src[:, c * P:(c + 1) * P], ident[0:TOK, 0:TOK])
                last.then_inc(pe_step, 1)

            pe.wait_ge(dve_step, DVE_XN2)
            transpose_rows(xn)
            pe.wait_ge(dve_step, DVE_XNT2)
            for c in range(DC):
                last = nc.tensor.matmul(p_o[0:TOK, :], xnT[:, c, :], mixw[:, c, :], start=(c == 0), stop=(c == DC - 1))
            last.then_inc(pe_step, 1)
            pe.wait_ge(dve_step, DVE_XRMS)
            transpose_rows(xn)
            pe.wait_ge(dve_step, DVE_XNT3)
            pe.wait_ge(tail_loaded, 96)
            for c in range(DC):
                last = nc.tensor.matmul(p_o[0:TOK, 0:24], xnT[:, c, :], wf_sb[:, c, :], start=(c == 0), stop=(c == DC - 1))
            last.then_inc(pe_step, 1)
            pe.wait_ge(dve_step, DVE_XPRE)
            nc.tensor.transpose(p_f[:, 0:TOK], xpre[:, :], ident[0:TOK, 0:TOK]).then_inc(pe_step, 1)
            pe.wait_ge(dve_step, DVE_XPT)
            nc.tensor.matmul(p_o[0:TOK, 0:P], xpT[:, :], wb_sb[:, :], start=True, stop=True).then_inc(pe_step, 1)
            pe.wait_ge(dve_step, DVE_BOUND)
            nc.tensor.transpose(p_f[0:1, 0:TOK], zlim[:, 2:3], ident[0:TOK, 0:TOK]).then_inc(pe_step, 1)

        def act_v_hi(act, b, g, i):
            u = UNITS * b + g
            act.wait_ge(v_projected, 4 * u + i + 1)
            need(act, pv_done, 4 * (2 * u - 1) + i + 1)
            n = len(piece_tiles(i)) * 2 * DH
            nc.scalar.activation(v_hi[:, 2 * i:2 * i + len(piece_tiles(i)), :].rearrange("p t n -> p (t n)"),
                                 p_kv[i % 2][:, 0:n], ACT.Copy).then_inc(v_hi_ready, 1)

        def act_k_hi(act, b, g, i):
            u = UNITS * b + g
            act.wait_ge(k_rotated, 4 * u + i + 1)
            f = i % 2
            nc.scalar.activation(kt_hi[:, i // 2, f * HB:(f + 1) * HB], rc[:, i % 2, 0:HB], ACT.Copy).then_inc(k_hi_ready, 1)

        def act_pt_hi(act, h, p):
            act.wait_ge(probs_transposed, 4 * h + p + 1)
            need(act, pv_done, 4 * h + p - 1)
            n = len(piece_tiles(p)) * QC
            nc.scalar.activation(pt_hi[:, p % 2, :, :].rearrange("p t n -> p (t n)")[:, 0:n], p_t[p % 2][:, 0:n],
                                 ACT.Copy).then_inc(pt_hi_ready, 1)

        def act_exp(act, b, g, s, i):
            n = 2 * (2 * (UNITS * b + g) + s) + i
            col = 2 * (2 * g + s) + i
            act.wait_ge(max_dropped, n + 1)
            nc.scalar.activation(fac[:, col:col + 1], m_drop[:, col:col + 1], ACT.Exp).then_inc(factor_ready, 1)
            act.wait_ge(max_negated, n + 1)
            nc.scalar.activation(scores[:, 2 * s + i, :], scores[:, 2 * s + i, :], ACT.Exp, bias=m_neg[:, col:col + 1],
                                 accum_out=rsum[:, col:col + 1]).then_inc(probs_ready, 1)

        @block.scalar
        def _(act):
            def split_w(k):
                n = W_PIECES[k]
                kind, i = STAGED[n]
                dst = (wk_hi if kind == "wk" else wv_hi)[:, :, i * 512:(i + 1) * 512]
                act.wait_ge(stage_loaded[n % 4], 16 * (n // 4 + 1))
                nc.scalar.activation(dst, stage[n % 4][:, :, :], ACT.Copy).then_inc(w_hi_ready, 1)

            split_w(0)
            for i in range(4):
                act_k_hi(act, 0, 0, i)
            split_w(1)

            def q_hi(n):
                act.wait_ge(q_transposed, n + 1)
                nc.scalar.activation(qt_hi[:, n * QC:(n + 1) * QC], p_f[:, 0:QC], ACT.Copy, scale=SCALE
                                     ).then_inc(q_hi_ready, 1)

            q_hi(0)
            split_w(2)
            split_w(3)
            for n in range(1, 8):
                q_hi(n)

            def act_slot(b, g, s, prev=True, last=False):
                h = 2 * (UNITS * b + g) + s

                def keys(i):
                    if g < UNITS - 1:
                        act_k_hi(act, b, g + 1, i)
                    elif not last:
                        act_k_hi(act, b + 1, 0, i)

                if prev:
                    act_pt_hi(act, h - 1, 0)
                    if s == 0:
                        act_k_hi(act, b, g, 2)
                    act_pt_hi(act, h - 1, 1)
                act_exp(act, b, g, s, 0)
                if s == 0:
                    act_v_hi(act, b, g, 0)
                if prev:
                    act_pt_hi(act, h - 1, 2)
                    if s == 0:
                        act_k_hi(act, b, g, 3)
                act_exp(act, b, g, s, 1)
                if s == 0:
                    act_v_hi(act, b, g, 1)
                else:
                    keys(0)
                if prev:
                    act_pt_hi(act, h - 1, 3)
                if s == 0:
                    act_v_hi(act, b, g, 2)
                    act_v_hi(act, b, g, 3)
                else:
                    keys(1)

            def act_block(b, first=False, last=False):
                for g in range(UNITS):
                    for s in range(2):
                        act_slot(b, g, s, prev=not (first and g == 0 and s == 0), last=last)

            act_block(0, first=True)
            with act.Fori(1, NB - 1) as b:
                act_block(b)
            act_block(NB - 1, last=True)
            for p in range(PIECES):
                act_pt_hi(act, 8 * NB - 1, p)

            act.wait_ge(dve_step, DVE_Z)
            nc.scalar.activation(x2[:, :], t0[:, :], ACT.Gelu).then_inc(act_step, 1)
            act.wait_ge(tail_loaded, 96)
            nc.scalar.activation(half_sb[:, :], gate_sb[:, :], ACT.Exp, scale=-1.0).then_inc(act_step, 1)
            act.wait_ge(dve_step, DVE_PMAX)
            nc.scalar.activation(hp[:, 0:8], hp[:, 8:16], ACT.Exp).then_inc(act_step, 1)
            act.wait_ge(dve_step, DVE_ZS)
            nc.scalar.activation(kk[:, :], tt[:, :], ACT.Exp).then_inc(act_step, 1)
            act.wait_ge(dve_step, DVE_FLAG)
            again = act.value_load(wide_flag[0:1, 0:1])
            with act.If(again == 1):
                with act.Fori(0, SINK) as it:
                    for r in range(2):
                        act.wait_ge(sk_shifted, 2 * it + r + 1)
                        nc.scalar.activation(ee[:, :], tt[:, :], ACT.Exp).then_inc(sk_exp, 1)
                        act.wait_ge(sk_summed, 2 * it + r + 1)
                        nc.scalar.activation(lns[:, :], sm4[:, :], ACT.Ln).then_inc(sk_ln, 1)
                act.wait_ge(sk_shifted, 2 * SINK + 1)
                nc.scalar.activation(hres[:, :], tt[:, :], ACT.Exp).then_inc(sk_exp, 1)

        @block.gpsimd
        def _(pool):
            def split_w(k):
                n = W_PIECES[k]
                kind, i = STAGED[n]
                cols = slice(i * 512, (i + 1) * 512)
                hi, lo = (wk_hi, wk_lo) if kind == "wk" else (wv_hi, wv_lo)
                pool.wait_ge(stage_loaded[n % 4], 16 * (n // 4 + 1))
                pool.wait_ge(w_hi_ready, k + 1)
                nc.gpsimd.tensor_tensor(lo[:, :, cols], stage[n % 4][:, :, :], hi[:, :, cols].bitcast(F32), ALU.subtract
                                        ).then_inc(w_lo_ready, 1)

            def ctx_lo(b, t):
                pool.wait_ge(ctx_hi_ready, KT * b + t + 1)
                pool.wait_ge(ctx_loaded[t], 16 * (b + 1))
                k = slice(t * P, (t + 1) * P)
                nc.gpsimd.tensor_tensor(ct_lo[:, :, k], ctx_raw[:, t, :, :], ct_hi[:, :, k].bitcast(F32), ALU.subtract
                                        ).then_inc(ctx_lo_ready, 1)

            def rotate(b, g, i):
                u = UNITS * b + g
                pool.wait_ge(k_products, 4 * u + i + 1)
                nc.gpsimd.tensor_tensor(rc[:, i % 2, 0:HB], rc[:, i % 2, 0:HB], rs[:, i % 2, 0:HB], ALU.add
                                        ).then_inc(k_rotated, 1)
                pool.wait_ge(k_rotated, 4 * u + i + 1)
                pool.wait_ge(k_hi_ready, 4 * u + i + 1)
                f = slice((i % 2) * HB, (i % 2 + 1) * HB)
                nc.gpsimd.tensor_tensor(kt_lo[:, i // 2, f], rc[:, i % 2, 0:HB], kt_hi[:, i // 2, f].bitcast(F32),
                                        ALU.subtract).then_inc(k_lo_ready, 1)

            nc.gpsimd.memset(mv[:, 3:4], -0.5).then_inc(pool_step, 1)
            pool.wait_ge(pool_step, 1)
            pool.wait_ge(dve_step, DVE_VAR)
            nc.gpsimd.tensor_tensor(mv[:, 2:3], mv[:, 1:2], mv[:, 3:4], ALU.pow).then_inc(pool_step, 1)
            split_w(0)
            for t in range(KT):
                ctx_lo(0, t)
            for i in range(4):
                rotate(0, 0, i)
            split_w(1)
            for n in range(8):
                pool.wait_ge(q_products, n + 1)
                c4 = rc[0:TOK, n % 2, :].rearrange("p (h two d) -> p h two d", two=2, d=HALF)
                s4 = rs[0:TOK, n % 2, :].rearrange("p (h two d) -> p h two d", two=2, d=HALF)
                nc.gpsimd.tensor_tensor(c4[:, :, 0, :], c4[:, :, 0, :], s4[:, :, 1, :], ALU.subtract).then_inc(pool_step, 1)
                nc.gpsimd.tensor_tensor(c4[:, :, 1, :], c4[:, :, 1, :], s4[:, :, 0, :], ALU.add)\
                    .then_inc(q_rotated, 1)
                if n == 0:
                    split_w(2)
                    split_w(3)

            def pool_block(b, last=False):
                for g in range(UNITS):
                    if g == UNITS - 1 and not last:
                        for t in range(KT):
                            ctx_lo(b + 1, t)
                    if g < UNITS - 1:
                        for i in range(4):
                            rotate(b, g + 1, i)
                    elif not last:
                        for i in range(4):
                            rotate(b + 1, 0, i)

            with pool.Fori(0, NB - 1) as b:
                pool_block(b)
            pool_block(NB - 1, last=True)
            for k in range(3):
                pool.wait_ge(dve_step, (DVE_VAR2, DVE_VAR3, DVE_MS)[k])
                nc.gpsimd.tensor_tensor(mv[:, 2:3], mv[:, 1:2], mv[:, 3:4], ALU.pow).then_inc(pool_step, 1)

        @block.vector
        def _(dve):
            count = [0]

            def step(ins, expect=None):
                count[0] += 1
                ins.then_inc(dve_step, 1)
                dve.wait_ge(dve_step, count[0])
                assert expect is None or expect == count[0], (expect, count[0])

            def layer_stats(src, var_at):
                step(nc.vector.bn_stats(bnst[:, :], src[:, :]))
                step(nc.vector.bn_aggr(mv[:, 0:2], bnst[:, :]))
                step(nc.vector.tensor_scalar(mv[:, 1:2], mv[:, 1:2], EPS, None, ALU.add), var_at)

            def normalise(dst, src, pool_at, at):
                dve.wait_ge(pool_step, pool_at)
                step(nc.vector.tensor_scalar(dst[:, :], src[:, :], mv[:, 0:1], mv[:, 2:3], ALU.subtract, ALU.mult), at)

            def ctx_hi(b, t):
                dve.wait_ge(ctx_loaded[t], 16 * (b + 1))
                need(dve, v_projected, 16 * (b - 1) + 13 + t // 2)
                nc.vector.tensor_copy(ct_hi[:, :, t * P:(t + 1) * P], ctx_raw[:, t, :, :]).then_inc(ctx_hi_ready, 1)

            def k_rope(b, g, i):
                u = UNITS * b + g
                dve.wait_ge(k_projected, 4 * u + i + 1)
                need(dve, k_lo_ready, 4 * u + i - 1)
                if i == 0 and g == 0:
                    dve.wait_ge(rope_loaded, 32 * (b + 1))
                f = slice((i % 2) * HB, (i % 2 + 1) * HB)
                src = p_kv[i % 2]
                nc.vector.tensor_tensor(rc[:, i % 2, 0:HB], src[:, 0:HB], cos_sb[:, f], ALU.mult)
                nc.vector.tensor_tensor(rs[0:HALF, i % 2, 0:HB], src[HALF:P, 0:HB], sin_sb[HALF:P, f], ALU.mult)
                nc.vector.tensor_tensor(rs[HALF:P, i % 2, 0:HB], src[0:HALF, 0:HB], sin_sb[0:HALF, f], ALU.mult)\
                    .then_inc(k_products, 1)

            def v_low(b, g, i):
                u = UNITS * b + g
                dve.wait_ge(v_hi_ready, 4 * u + i + 1)
                n = len(piece_tiles(i))
                tiles = slice(2 * i, 2 * i + n)
                nc.vector.tensor_tensor(v_lo[:, tiles, :].rearrange("p t n -> p (t n)"), p_kv[i % 2][:, 0:n * 2 * DH],
                                        v_hi[:, tiles, :].bitcast(F32).rearrange("p t n -> p (t n)"), ALU.subtract
                                        ).then_inc(v_lo_ready, 1)

            def pt_low(h, p):
                dve.wait_ge(pt_hi_ready, 4 * h + p + 1)
                n = len(piece_tiles(p)) * QC
                nc.vector.tensor_tensor(pt_lo[:, p % 2, :, :].rearrange("p t n -> p (t n)")[:, 0:n], p_t[p % 2][:, 0:n],
                                        pt_hi[:, p % 2, :, :].bitcast(F32).rearrange("p t n -> p (t n)")[:, 0:n],
                                        ALU.subtract).then_inc(pt_lo_ready, 1)

            def mask_scores(b, g, s, i):
                h = 2 * (UNITS * b + g) + s
                n = 2 * h + i
                col = 2 * (2 * g + s) + i
                c = slice(col, col + 1)
                dve.wait_ge(scores_ready, n + 1)
                if i == 0:
                    if g == 0 and s == 0:
                        dve.wait_ge(mask_loaded, 32 * (b + 1))
                    need(dve, probs_transposed, 4 * (h - 1))
                    need(dve, scores_masked, 2 * h)
                nc.vector.tensor_copy(m_old[:, c], m_run[:, c]).then_inc(max_kept, 1)
                nc.vector.tensor_tensor_reduce(out=scores[:, 2 * s + i, :].rearrange("p (f n) -> p f n", f=2),
                                               in0=p_s[:, :, 0:HB], in1=mask_sb[:, :].rearrange("p (f n) -> p f n", f=2),
                                               scale=1.0, scalar=m_run[:, c], op0=ALU.add, op1=ALU.max,
                                               accum_out=m_run[:, c]).then_inc(scores_masked, 1)
                dve.wait_ge(scores_masked, n + 1)
                dve.wait_ge(max_kept, n + 1)
                nc.vector.tensor_tensor(m_drop[:, c], m_old[:, c], m_run[:, c], ALU.subtract).then_inc(max_dropped, 1)
                nc.vector.tensor_scalar(m_neg[:, c], m_run[:, c], -1.0, None, ALU.mult).then_inc(max_negated, 1)

            def keep_sums(h, g, s):
                c = slice(2 * (2 * g + s), 2 * (2 * g + s) + 2)
                dve.wait_ge(probs_ready, 2 * h + 2)
                dve.wait_ge(factor_ready, 2 * h + 2)
                need(dve, sums_kept, 2 * h)
                nc.vector.tensor_tensor(l_run[:, c], l_run[:, c], fac[:, c], ALU.mult).then_inc(sums_kept, 1)
                dve.wait_ge(sums_kept, 2 * h + 1)
                nc.vector.tensor_tensor(l_run[:, c], l_run[:, c], rsum[:, c], ALU.add).then_inc(sums_kept, 1)

            def acc_scale(h, head):
                dve.wait_ge(factor_spread, h + 1)
                need(dve, acc_added, h)
                nc.vector.tensor_tensor(acc[:, head, :], acc[:, head, :], p_f[:, 0:QC], ALU.mult).then_inc(acc_scaled, 1)

            def acc_add(h, head):
                dve.wait_ge(pv_done, 4 * h + 4)
                dve.wait_ge(acc_scaled, h + 1)
                nc.vector.tensor_tensor(acc[:, head, :], acc[:, head, :], p_o[:, 0:QC], ALU.add).then_inc(acc_added, 1)

            dve.wait_ge(x_loaded, 64)
            layer_stats(x_sb, DVE_VAR)
            normalise(xn, x_sb, 2, DVE_XN)
            for t in range(2):
                ctx_hi(0, t)
            dve.wait_ge(pe_step, PE_XNT)
            step(nc.vector.tensor_copy(xnT[:, :, :].rearrange("p c n -> p (c n)"), p_o[:, 0:DC * TOK]), DVE_XNT)
            for t in range(2, KT):
                ctx_hi(0, t)
            for i in range(4):
                k_rope(0, 0, i)
            step(nc.vector.memset(m_run[:, :], -3.0e38))
            step(nc.vector.memset(l_run[:, :], 0.0), DVE_MIX)

            def q_low(n):
                dve.wait_ge(q_hi_ready, n + 1)
                nc.vector.scalar_tensor_tensor(out=qt_lo[:, n * QC:(n + 1) * QC], in0=p_f[:, 0:QC], scalar=SCALE,
                                               in1=qt_hi[:, n * QC:(n + 1) * QC].bitcast(F32), op0=ALU.mult,
                                               op1=ALU.subtract).then_inc(q_lo_ready, 1)

            for n in range(8):
                dve.wait_ge(q_projected, n + 1)
                if n < 2:
                    dve.wait_ge(k_lo_ready, 4)
                else:
                    dve.wait_ge(q_transposed, n - 1)
                src = p_kv[n % 2][0:TOK, :].rearrange("p (r d) -> p r d", d=HALF)
                for k, dst in ((0, rc), (1, rs)):
                    last = nc.vector.tensor_tensor(dst[0:TOK, n % 2, :].rearrange("p (r d) -> p r d", d=HALF), src,
                                                   qtab[:, k:k + 1, :].to_broadcast([TOK, 8, HALF]), ALU.mult)
                last.then_inc(q_products, 1)
                if n:
                    q_low(n - 1)
            q_low(7)
            nc.vector.memset(acc[:, :, :].rearrange("p h n -> p (h n)"), 0.0).then_inc(acc_cleared, 1)
            dve.wait_ge(acc_cleared, 1)

            def dve_slot(b, g, s, prev=True, last=False):
                h = 2 * (UNITS * b + g) + s
                ph = (2 * g + s - 1) % HKV

                def fill(i):
                    if s == 0:
                        v_low(b, g, i)
                    elif g < UNITS - 1:
                        k_rope(b, g + 1, i)
                    elif not last:
                        k_rope(b + 1, 0, i)
                    else:
                        dve.wait_ge(pe_step, PE_XNT + i + 1)
                        if i == 0:
                            dve.wait_ge(smask_loaded, 16)
                        step(nc.vector.tensor_tensor(mixw[:, i, :], p_kv[i % 2][:, :], smask_sb[:, i, :], ALU.mult))

                def split_ctx(i):
                    if s == 0 and g == UNITS - 1 and not last:
                        for t in piece_tiles(i):
                            ctx_hi(b + 1, t)

                if prev:
                    pt_low(h - 1, 0)
                    acc_scale(h - 1, ph)
                mask_scores(b, g, s, 0)
                if prev:
                    pt_low(h - 1, 1)
                    if s == 0:
                        k_rope(b, g, 3)
                fill(0)
                split_ctx(0)
                mask_scores(b, g, s, 1)
                if prev:
                    pt_low(h - 1, 2)
                fill(1)
                split_ctx(1)
                if prev:
                    pt_low(h - 1, 3)
                fill(2)
                split_ctx(2)
                if prev:
                    acc_add(h - 1, ph)
                keep_sums(h, g, s)
                if s == 0 or last and g == UNITS - 1:
                    fill(3)
                split_ctx(3)

            def dve_block(b, first=False, last=False):
                for g in range(UNITS):
                    for s in range(2):
                        dve_slot(b, g, s, prev=not (first and g == 0 and s == 0), last=last)

            dve_block(0, first=True)
            with dve.Fori(1, NB - 1) as b:
                dve_block(b)
            dve_block(NB - 1, last=True)
            h = 8 * NB - 1
            acc_scale(h, HKV - 1)
            for p in range(PIECES):
                pt_low(h, p)
            acc_add(h, HKV - 1)
            dve.wait_ge(sums_kept, 2 * h + 2)
            step(nc.vector.reciprocal(l_inv[:, :], l_run[:, :]), DVE_LINV)
            dve.wait_ge(acc_added, 8 * NB)
            for head in range(HKV):
                dve.wait_ge(factor_spread, 8 * NB + head + 1)
                nc.vector.tensor_tensor(acc[:, head, :], acc[:, head, :], p_f[:, 0:QC], ALU.mult).then_inc(acc_scaled, 1)

            dve.wait_ge(pe_step, PE_Y)
            step(nc.vector.tensor_tensor(x1[:, :], p_o[0:TOK, :], x_sb[:, :], ALU.add), DVE_X1)
            layer_stats(x1, DVE_VAR2)
            normalise(xn, x1, 11, DVE_XN2)
            dve.wait_ge(pe_step, PE_X1T)
            step(nc.vector.tensor_copy(xnT[:, :, :].rearrange("p c n -> p (c n)"), p_f[:, 0:DC * TOK]), DVE_XNT2)
            dve.wait_ge(pe_step, PE_Z)
            dve.wait_ge(tail_loaded, 96)
            step(nc.vector.tensor_tensor(t0[:, :], p_o[0:TOK, :], b2_sb[:, :], ALU.add), DVE_Z)
            dve.wait_ge(act_step, 1)
            step(nc.vector.tensor_tensor(x2[:, :], x2[:, :], x1[:, :], ALU.add), DVE_X2)
            layer_stats(x2, DVE_VAR3)
            normalise(xf, x2, 12, DVE_XF)
            step(nc.vector.tensor_tensor_reduce(out=t0[:, :], in0=xf[:, :], in1=xf[:, :], scale=1.0, scalar=0.0,
                                                op0=ALU.mult, op1=ALU.add, accum_out=mv[:, 0:1]))
            step(nc.vector.tensor_scalar(mv[:, 1:2], mv[:, 0:1], 1.0 / D, RMS_EPS, ALU.mult, ALU.add), DVE_MS)
            dve.wait_ge(pool_step, 13)
            step(nc.vector.tensor_scalar(xn[:, :], xf[:, :], mv[:, 2:3], None, ALU.mult), DVE_XRMS)
            dve.wait_ge(pe_step, PE_XNT3)
            step(nc.vector.tensor_copy(xnT[:, :, :].rearrange("p c n -> p (c n)"), p_f[:, 0:DC * TOK]), DVE_XNT3)
            dve.wait_ge(pe_step, PE_LOGITS)
            step(nc.vector.tensor_tensor(lg[:, :], p_o[0:TOK, 0:24], hb_sb[:, :], ALU.add), DVE_LG)
            step(nc.vector.tensor_reduce(mx4[:, 0:2], lg[:, 16:24].rearrange("p (k n) -> p k n", k=2), AX_X, ALU.max))
            step(nc.vector.tensor_tensor(hp[:, 8:16].rearrange("p (k n) -> p k n", k=2),
                                         lg[:, 16:24].rearrange("p (k n) -> p k n", k=2),
                                         mx4[:, 0:2].unsqueeze(2).to_broadcast([TOK, 2, 4]), ALU.subtract), DVE_PMAX)
            step(nc.vector.tensor_scalar(zz[:, :], lg[:, 0:16], INV_TAU, None, ALU.mult))
            step(nc.vector.tensor_reduce(zlim[:, 0:1], zz[:, :], AX_X, ALU.max))
            step(nc.vector.tensor_reduce(zlim[:, 1:2], zz[:, :], AX_X, ALU.min))
            step(nc.vector.tensor_tensor(zlim[:, 2:3], zlim[:, 0:1], zlim[:, 1:2], ALU.subtract))
            step(nc.vector.scalar_tensor_tensor(out=zlim[:, 3:4], in0=zlim[:, 2:3], scalar=0.5, in1=zlim[:, 1:2],
                                                op0=ALU.mult, op1=ALU.add))
            step(nc.vector.tensor_scalar(tt[:, :], zz[:, :], zlim[:, 3:4], None, ALU.subtract), DVE_ZS)
            dve.wait_ge(act_step, 3)
            step(nc.vector.tensor_reduce(sm4[:, 0:2], hp[:, 0:8].rearrange("p (k n) -> p k n", k=2), AX_X, ALU.add))
            step(nc.vector.reciprocal(sm4[:, 2:4], sm4[:, 0:2]))
            step(nc.vector.tensor_tensor(hp[:, 0:8].rearrange("p (k n) -> p k n", k=2),
                                         hp[:, 0:8].rearrange("p (k n) -> p k n", k=2),
                                         sm4[:, 2:4].unsqueeze(2).to_broadcast([TOK, 2, 4]), ALU.mult), DVE_PRE)
            step(nc.vector.tensor_scalar(xpre[:, :], xf[:, 0:P], hp[:, 0:1], None, ALU.mult))
            for n in range(1, NS):
                step(nc.vector.scalar_tensor_tensor(out=xpre[:, :], in0=xf[:, n * P:(n + 1) * P], scalar=hp[:, n:n + 1],
                                                    in1=xpre[:, :], op0=ALU.mult, op1=ALU.add))
            dve.wait_ge(pe_step, PE_XPT)
            step(nc.vector.tensor_copy(xpT[:, :], p_f[:, 0:TOK]), DVE_XPT)
            def rows_of(x, order):
                return x[:, :].rearrange(f"p (i j) -> p {order}", j=NS)

            def inner(x):
                return x[:, :].unsqueeze(1).to_broadcast([TOK, NS, NS])

            def outer(x):
                return x[:, :].unsqueeze(2).to_broadcast([TOK, NS, NS])

            t_in = rows_of(tt, "i j")
            e_in = rows_of(ee, "i j")
            HALVES = (("i j", vv, uu), ("j i", uu, vv))
            dve.wait_ge(pe_step, PE_BR)
            step(nc.vector.tensor_copy(ybr[:, :], p_o[0:TOK, 0:P]), DVE_YBR)
            step(nc.vector.memset(vv[:, :], 1.0))
            step(nc.vector.memset(sums_max[:, :, :], 1.0))
            step(nc.vector.memset(sums_min[:, :, :], 1.0))
            dve.wait_ge(act_step, 4)
            with dve.Fori(0, SINK // SINK_UNROLL) as it:
                for k in range(2 * SINK_UNROLL):
                    order, other, mine = HALVES[k % 2]
                    done = 3 * (2 * SINK_UNROLL * it + k)
                    dve.wait_ge(sk_linear, done)
                    nc.vector.tensor_tensor(t_in, rows_of(kk, order), inner(other), ALU.mult).then_inc(sk_linear, 1)
                    dve.wait_ge(sk_linear, done + 1)
                    nc.vector.tensor_reduce(sums[:, k, :], t_in, AX_X, ALU.add).then_inc(sk_linear, 1)
                    dve.wait_ge(sk_linear, done + 2)
                    nc.vector.reciprocal(mine[:, :], sums[:, k, :]).then_inc(sk_linear, 1)
                dve.wait_ge(sk_limits, 2 * it)
                nc.vector.tensor_tensor(sums_max[:, :, :], sums_max[:, :, :], sums[:, :, :], ALU.max).then_inc(sk_limits, 1)
                nc.vector.tensor_tensor(sums_min[:, :, :], sums_min[:, :, :], sums[:, :, :], ALU.min).then_inc(sk_limits, 1)
            dve.wait_ge(sk_linear, 6 * SINK)
            dve.wait_ge(sk_limits, 2 * SINK // SINK_UNROLL)
            step(nc.vector.tensor_reduce(zlim[:, 4:5], sums_max[:, :, :].rearrange("p k n -> p (k n)"), AX_X, ALU.max))
            step(nc.vector.tensor_reduce(zlim[:, 5:6], sums_min[:, :, :].rearrange("p k n -> p (k n)"), AX_X, ALU.min))
            step(nc.vector.reciprocal(zlim[:, 6:7], zlim[:, 5:6]))
            step(nc.vector.tensor_tensor(zlim[:, 7:8], zlim[:, 4:5], zlim[:, 6:7], ALU.max))
            step(nc.vector.tensor_scalar(zlim[:, 3:4], zlim[:, 2:3], 1.0 / Z_SPREAD_MAX, None, ALU.mult))
            step(nc.vector.scalar_tensor_tensor(out=zlim[:, 2:3], in0=zlim[:, 7:8], scalar=1.0 / SUM_MAX,
                                                in1=zlim[:, 3:4], op0=ALU.mult, op1=ALU.max), DVE_BOUND)
            nc.vector.tensor_tensor(t_in, rows_of(kk, "i j"), inner(vv), ALU.mult).then_inc(sk_linear, 1)
            dve.wait_ge(sk_linear, 6 * SINK + 1)
            nc.vector.tensor_tensor(rows_of(hres, "i j"), t_in, outer(uu), ALU.mult).then_inc(sk_linear, 1)
            dve.wait_ge(sk_linear, 6 * SINK + 2)
            dve.wait_ge(pe_step, PE_WIDE)
            step(nc.vector.tensor_reduce(wide[:, 0:1], p_f[0:1, 0:TOK], AX_X, ALU.max))
            step(nc.vector.tensor_scalar(wide_flag[:, :], wide[:, 0:1], 1.0, None, ALU.is_gt), DVE_FLAG)
            again = dve.value_load(wide_flag[0:1, 0:1])
            with dve.If(again == 1):
                nc.vector.memset(vv[:, :], 0.0).then_inc(sk_state, 1)
                with dve.Fori(0, SINK) as it:
                    for r, (order, other, mine) in enumerate(HALVES):
                        done = 8 * it + 4 * r + 1
                        dve.wait_ge(sk_state, done)
                        nc.vector.tensor_tensor(t_in, rows_of(zz, order), inner(other), ALU.add).then_inc(sk_state, 1)
                        dve.wait_ge(sk_state, done + 1)
                        nc.vector.tensor_reduce(mx4[:, :], t_in, AX_X, ALU.max).then_inc(sk_state, 1)
                        dve.wait_ge(sk_state, done + 2)
                        nc.vector.tensor_tensor(t_in, t_in, outer(mx4), ALU.subtract).then_inc(sk_shifted, 1)
                        dve.wait_ge(sk_exp, 2 * it + r + 1)
                        nc.vector.tensor_reduce(sm4[:, :], e_in, AX_X, ALU.add).then_inc(sk_summed, 1)
                        dve.wait_ge(sk_ln, 2 * it + r + 1)
                        nc.vector.tensor_tensor(mine[:, :], lns[:, :], mx4[:, :], ALU.add).then_inc(sk_state, 1)
                        dve.wait_ge(sk_state, done + 3)
                        nc.vector.tensor_scalar(mine[:, :], mine[:, :], -1.0, None, ALU.mult).then_inc(sk_state, 1)
                dve.wait_ge(sk_state, 8 * SINK + 1)
                nc.vector.tensor_tensor(t_in, rows_of(zz, "i j"), inner(vv), ALU.add).then_inc(sk_state, 1)
                dve.wait_ge(sk_state, 8 * SINK + 2)
                nc.vector.tensor_tensor(t_in, t_in, outer(uu), ALU.add).then_inc(sk_shifted, 1)
                dve.wait_ge(sk_exp, 2 * SINK + 1)
            step(nc.vector.tensor_scalar(half_sb[:, :], half_sb[:, :], 1.0, None, ALU.add))
            step(nc.vector.reciprocal(gate_sb[:, :], half_sb[:, :]))
            step(nc.vector.tensor_tensor(hres[:, :], hres[:, :], eye_sb[:, :], ALU.subtract))
            step(nc.vector.scalar_tensor_tensor(out=hres[:, :], in0=hres[:, :], scalar=gate_sb[:, :], in1=eye_sb[:, :],
                                                op0=ALU.mult, op1=ALU.add))
            for i in range(NS):
                o = ob[:, i * P:(i + 1) * P]
                step(nc.vector.scalar_tensor_tensor(out=o, in0=ybr[:, :], scalar=hp[:, 4 + i:5 + i],
                                                    in1=x2[:, i * P:(i + 1) * P], op0=ALU.mult, op1=ALU.add))
                for j in range(NS):
                    step(nc.vector.scalar_tensor_tensor(out=o, in0=xf[:, j * P:(j + 1) * P],
                                                        scalar=hres[:, NS * i + j:NS * i + j + 1],
                                                        in1=o, op0=ALU.mult, op1=ALU.add))
            assert count[0] == DVE_END, (count[0], DVE_END)


def rope_tables():
    import numpy as np
    inv = (np.float32(1.0) / np.power(np.float32(10000.0), np.arange(0, DH, 2, dtype=np.float32) / np.float32(DH))).astype(np.float32)
    ang = (np.arange(KEYS, dtype=np.float32)[:, None] * inv[None, :]).astype(np.float64)
    return np.cos(ang).astype(np.float32), np.sin(ang).astype(np.float32)


def kernel(x, ctx_4096, mask_BxSxS2_ff0, L0_xattn_wq, L0_xattn_wk, L0_xattn_wv, L0_xattn_wo, L0_attn_w1, L0_attn_w2,
           L0_attn_b2, L0_attn_sparse_mask, L0_ffn_W_res, L0_ffn_W_pre, L0_ffn_W_post, L0_ffn_H_res_base,
           L0_ffn_H_pre_base, L0_ffn_H_post_base, L0_ffn_gate, L0_ffn_W_branch):
    import numpy as np
    import concourse.bacc as bacc
    from concourse.bass_utils import run_bass_kernel_spmd

    cos, sin = rope_tables()
    rows = lambda a, n: np.broadcast_to(np.asarray(a).reshape(1, -1), (n, np.asarray(a).size))
    arrays = {
        "x": np.asarray(x)[0],
        "ctxT": np.asarray(ctx_4096)[0].T,
        "mask": np.asarray(mask_BxSxS2_ff0)[0],
        "wq": L0_xattn_wq, "wk": L0_xattn_wk, "wv": L0_xattn_wv, "wo": L0_xattn_wo,
        "w1": L0_attn_w1, "w2t": np.asarray(L0_attn_w2).T, "b2": rows(L0_attn_b2, TOK), "smask": L0_attn_sparse_mask,
        "wffn": np.concatenate([np.asarray(L0_ffn_W_res), np.asarray(L0_ffn_W_pre), np.asarray(L0_ffn_W_post)]).T,
        "hbase": rows(np.concatenate([np.asarray(L0_ffn_H_res_base).ravel(), np.asarray(L0_ffn_H_pre_base),
                                      np.asarray(L0_ffn_H_post_base)]), TOK),
        "gate": rows(L0_ffn_gate, TOK), "wbranch": L0_ffn_W_branch,
        "ident": np.eye(P, dtype=np.float32), "eye": rows(np.eye(NS, dtype=np.float32), TOK),
        "cosT": np.concatenate([cos.T, cos.T]), "sinT": np.concatenate([sin.T, -sin.T]),
        "qcos": cos[:TOK], "qsin": sin[:TOK],
    }
    arrays = {k: np.ascontiguousarray(v) for k, v in arrays.items()}
    nc = bacc.Bacc("TRN2", target_bir_lowering=False, num_devices=1, dynamic_dma_scratch_size=4096)
    A = {k: nc.dram_tensor(f"in_{k}", v.shape, mybir.dt.from_np(v.dtype), kind="ExternalInput").ap()
         for k, v in arrays.items()}
    A["out"] = nc.dram_tensor("out_x", (TOK, D), F32, kind="ExternalOutput").ap()
    perceiver(nc, A)
    r = run_bass_kernel_spmd(nc, [{f"in_{k}": v for k, v in arrays.items()}], core_ids=[0])
    return r.results[0]["out_x"].reshape(1, TOK, D)
```

```python
from contextlib import ExitStack

import concourse.bass as bass
from concourse import mybir

F32 = mybir.dt.float32
F32R = mybir.dt.float32r
ALU = mybir.AluOpType
ACT = mybir.ActivationFunctionType
AX_X = mybir.AxisListType.X

P = 128
D = 512
DC = D // P
TOK = 64
KEYS = 6272
HQ, HKV, DH = 32, 8, 128
HALF = DH // 2
KT = 7
BK = KT * P
NB = KEYS // BK
HB = BK // 2
UNITS = HKV // 2
QC = HQ // HKV * TOK
PIECES = 4
SCALE = float(DH) ** -0.5
EPS = 1e-5
RMS_EPS = 1.1920929e-07
NS = 4
SINK = 50
INV_TAU = 10.0
SINK_UNROLL = 5
Z_SPREAD_MAX = 150.0
SUM_MAX = 1e25
assert NB * BK == KEYS and UNITS == 4


def piece_tiles(p):
    return range(2 * p, min(2 * p + 2, KT))


SC = 2 * DH
STAGED = [p for k in range(HKV) for p in (("wv" if k % 2 else "wk", k // 2), ("wq", 2 * k), ("wq", 2 * k + 1))]


def place_of(n):
    return n if n < 6 else 6 + (n - 6) % 3


def turn_of(n):
    return 1 if n < 6 else (n - 6) // 3 + 1


def need(eng, sem, value):
    if isinstance(value, int) and value <= 0:
        return
    eng.wait_ge(sem, value)


def perceiver(nc, A):
    with ExitStack() as ctx:
        def sb(name, shape, dt=F32):
            return ctx.enter_context(nc.sbuf_tensor(name, shape, dt))

        def ps(name, shape):
            return ctx.enter_context(nc.psum_tensor(name, shape, F32))

        def sem(name):
            return ctx.enter_context(nc.semaphore(name))

        base = -(-nc.sbuf_base // 32) * 32
        at = [base]

        def region(nbytes):
            here = at[0]
            at[0] += nbytes
            return here

        def place(name, shape, dt, where):
            return nc.alloc_sbuf_tensor_at(name, shape, dt, offset=where)

        R_WK_HI, R_WK_LO, R_WV_HI, R_WV_LO = (region(4 * DC * HKV * DH) for _ in range(4))
        R_CT_HI, R_CT_LO = (region(4 * DC * BK) for _ in range(2))
        R_V = region(4 * 2 * KT * 2 * DH)
        R_S = region(4 * 4 * BK)
        R_PT = region(4 * 2 * 2 * 2 * QC)
        R_ACC = region(4 * HKV * QC)
        R_RAW = region(4 * KT * DC * P)
        arena = sb("arena", [P, (at[0] - base) // 4 + 16])
        assert arena is not None

        wk_hi = place("wk_hi", [P, DC, HKV * DH], F32R, R_WK_HI)
        wk_lo = place("wk_lo", [P, DC, HKV * DH], F32R, R_WK_LO)
        wv_hi = place("wv_hi", [P, DC, HKV * DH], F32R, R_WV_HI)
        wv_lo = place("wv_lo", [P, DC, HKV * DH], F32R, R_WV_LO)
        ct_hi = place("ct_hi", [P, DC, BK], F32R, R_CT_HI)
        ct_lo = place("ct_lo", [P, DC, BK], F32R, R_CT_LO)
        v_hi = place("v_hi", [P, KT, 2 * DH], F32R, R_V)
        v_lo = place("v_lo", [P, KT, 2 * DH], F32R, R_V + 4 * KT * 2 * DH)
        scores = place("scores", [P, 4, BK], F32, R_S)
        pt_hi = place("pt_hi", [P, 2, 2, QC], F32R, R_PT)
        pt_lo = place("pt_lo", [P, 2, 2, QC], F32R, R_PT + 4 * 2 * 2 * QC)
        acc = place("acc", [P, HKV, QC], F32, R_ACC)
        ctx_raw = place("ctx_raw", [P, KT, DC, P], F32, R_RAW)
        STAGE_AT = [R_V, R_V + 4096, R_V + 8192, R_PT, R_PT + 4096, R_S + 4 * 2 * BK, R_RAW, R_RAW + 4096, R_RAW + 8192]
        stage = [place(f"stage{i}", [P, DC, SC], F32, a) for i, a in enumerate(STAGE_AT)]
        w1_sb = place("w1_sb", [P, DC, D], F32, R_WK_HI)
        w2t_sb = place("w2t_sb", [P, DC, D], F32, R_WK_HI + 4 * DC * D)
        smask_sb = place("smask_sb", [P, DC, D], F32, R_WK_LO)
        mixw = place("mixw", [P, DC, D], F32, R_WK_LO + 4 * DC * D)
        wo_sb = [place("wo0", [P, 8, D], F32, R_WV_HI), place("wo1", [P, 8, D], F32, R_WV_LO),
                 place("wo2", [P, 14, D], F32, R_CT_HI), place("wo3", [P, 2, D], F32, R_RAW)]
        WO_FIRST = [0, 8, 16, 30, 32]
        assert R_CT_LO == R_CT_HI + 4 * 7 * D

        kt_hi = sb("kt_hi", [P, 2, BK], F32R)
        kt_lo = sb("kt_lo", [P, 2, BK], F32R)
        qt_hi = sb("qt_hi", [P, HQ * TOK], F32R)
        qt_lo = sb("qt_lo", [P, HQ * TOK], F32R)
        mask_sb = sb("mask_sb", [P, BK])
        cos_sb = sb("cos_sb", [P, BK])
        sin_sb = sb("sin_sb", [P, BK])
        rc = sb("rc", [P, 2, HB])
        rs = sb("rs", [P, 2, HB])
        rq = sb("rq", [P, QC])
        rqs = sb("rqs", [P, QC])
        ident = sb("ident", [P, P])
        x_sb = sb("x_sb", [TOK, D])
        xn = sb("xn", [TOK, D])
        xnT = sb("xnT", [P, DC, TOK])
        qtab = sb("qtab", [P, 2, TOK])
        bnst = sb("bnst", [TOK, 6])
        mv = sb("mv", [TOK, 4])
        m_run = sb("m_run", [P, 16])
        m_old = sb("m_old", [P, 16])
        m_neg = sb("m_neg", [P, 16])
        m_drop = sb("m_drop", [P, 16])
        fac = sb("fac", [P, 16])
        rsum = sb("rsum", [P, 16])
        l_run = sb("l_run", [P, 16])
        l_inv = sb("l_inv", [P, 16])
        b2_sb = sb("b2_sb", [TOK, D])
        wf_sb = sb("wf_sb", [P, DC, 24])
        hb_sb = sb("hb_sb", [TOK, 24])
        gate_sb = sb("gate_sb", [TOK, 1])
        wb_sb = sb("wb_sb", [P, P])
        eye_sb = sb("eye_sb", [TOK, 16])
        half_sb = sb("half_sb", [TOK, 1])
        lg = sb("lg", [TOK, 24])
        zz = sb("zz", [TOK, 16])
        tt = sb("tt", [TOK, 16])
        ee = sb("ee", [TOK, 16])
        uu = sb("uu", [TOK, 4])
        vv = sb("vv", [TOK, 4])
        mx4 = sb("mx4", [TOK, 4])
        sm4 = sb("sm4", [TOK, 4])
        lns = sb("lns", [TOK, 4])
        hres = sb("hres", [TOK, 16])
        hp = sb("hp", [TOK, 16])
        kk = sb("kk", [TOK, 16])
        zlim = sb("zlim", [TOK, 8])
        sums = sb("sums", [TOK, 2 * SINK_UNROLL, NS])
        sums_max = sb("sums_max", [TOK, 2 * SINK_UNROLL, NS])
        sums_min = sb("sums_min", [TOK, 2 * SINK_UNROLL, NS])
        wide = sb("wide", [1, 2])
        wide_flag = sb("wide_flag", [1, 1], mybir.dt.int32)
        x1 = place("x1", [TOK, D], F32, R_S)
        x2 = place("x2", [TOK, D], F32, R_S + 2048)
        xf = place("xf", [TOK, D], F32, R_S + 4096)
        t0 = place("t0", [TOK, D], F32, R_S + 6144)
        ob = place("ob", [TOK, D], F32, R_S + 8192)
        xpre = place("xpre", [TOK, P], F32, R_S + 10240)
        ybr = place("ybr", [TOK, P], F32, R_S + 10752)
        xpT = place("xpT", [P, TOK], F32, R_S + 11264)

        p_s = ps("p_s", [P, 2, 512])
        p_t = [ps(f"p_t{i}", [P, 512]) for i in range(2)]
        p_kv = [ps(f"p_kv{i}", [P, 512]) for i in range(2)]
        p_o = ps("p_o", [P, 512])
        p_f = ps("p_f", [P, 512])

        x_loaded = sem("x_loaded")
        ident_loaded = sem("ident_loaded")
        qtab_loaded = sem("qtab_loaded")
        tail_loaded = sem("tail_loaded")
        stage_loaded = [sem(f"stage_loaded{i}") for i in range(len(STAGE_AT))]
        ctx_loaded = [sem(f"ctx_loaded{t}") for t in range(KT)]
        rope_loaded = sem("rope_loaded")
        mask_loaded = sem("mask_loaded")
        w12_loaded = sem("w12_loaded")
        smask_loaded = sem("smask_loaded")
        wo_loaded = [sem(f"wo_loaded{i}") for i in range(4)]
        w_hi_ready = sem("w_hi_ready")
        w_lo_ready = sem("w_lo_ready")
        ctx_hi_ready = sem("ctx_hi_ready")
        ctx_lo_ready = sem("ctx_lo_ready")
        q_projected = sem("q_projected")
        q_products = sem("q_products")
        q_rotated = sem("q_rotated")
        q_hi_ready = sem("q_hi_ready")
        q_lo_ready = sem("q_lo_ready")
        k_projected = sem("k_projected")
        v_projected = sem("v_projected")
        k_products = sem("k_products")
        k_rotated = sem("k_rotated")
        k_hi_ready = sem("k_hi_ready")
        k_lo_ready = sem("k_lo_ready")
        v_hi_ready = sem("v_hi_ready")
        v_lo_ready = sem("v_lo_ready")
        scores_ready = sem("scores_ready")
        scores_masked = sem("scores_masked")
        max_negated = sem("max_negated")
        max_dropped = sem("max_dropped")
        max_kept = sem("max_kept")
        factor_ready = sem("factor_ready")
        probs_ready = sem("probs_ready")
        sums_kept = sem("sums_kept")
        probs_transposed = sem("probs_transposed")
        pt_hi_ready = sem("pt_hi_ready")
        pt_lo_ready = sem("pt_lo_ready")
        pv_done = sem("pv_done")
        factor_spread = sem("factor_spread")
        acc_scaled = sem("acc_scaled")
        acc_added = sem("acc_added")
        acc_cleared = sem("acc_cleared")
        const_ready = sem("const_ready")
        dve_step = sem("dve_step")
        act_step = sem("act_step")
        pool_step = sem("pool_step")
        pe_step = sem("pe_step")
        out_stored = sem("out_stored")

        sk_shifted = sem("sk_shifted")
        sk_exp = sem("sk_exp")
        sk_summed = sem("sk_summed")
        sk_ln = sem("sk_ln")
        sk_state = sem("sk_state")
        sk_linear = sem("sk_linear")
        sk_limits = sem("sk_limits")

        PE_XNT, PE_MIX = 1, 5
        PE_Y, PE_X1T, PE_Z, PE_XNT3, PE_LOGITS, PE_XPT, PE_BR, PE_WIDE = 6, 7, 8, 9, 10, 11, 12, 13
        DVE_VAR, DVE_XN, DVE_XNT = 3, 4, 5
        DVE_MIX = 7
        DVE_LINV = DVE_MIX + 4 + 1
        DVE_X1 = DVE_LINV + 1
        DVE_VAR2, DVE_XN2, DVE_XNT2 = DVE_X1 + 3, DVE_X1 + 4, DVE_X1 + 5
        DVE_Z = DVE_XNT2 + 1
        DVE_X2 = DVE_Z + 1
        DVE_VAR3, DVE_XF = DVE_X2 + 3, DVE_X2 + 4
        DVE_MS, DVE_XRMS, DVE_XNT3 = DVE_XF + 2, DVE_XF + 3, DVE_XF + 4
        DVE_LG = DVE_XNT3 + 1
        DVE_PMAX = DVE_LG + 2
        DVE_ZS = DVE_PMAX + 6
        DVE_PRE = DVE_ZS + 3
        DVE_XPRE = DVE_PRE + 4
        DVE_XPT = DVE_XPRE + 1
        DVE_YBR = DVE_XPT + 1
        DVE_BOUND = DVE_YBR + 9
        DVE_FLAG = DVE_BOUND + 2
        DVE_END = DVE_FLAG + 4 + 5 * NS

        block = ctx.enter_context(nc.Block())

        @block.sync
        def _(sp):
            def load_stage(n):
                kind, i = STAGED[n]
                k, r = divmod(n, 3)
                if 6 <= n < 9:
                    sp.wait_ge(ctx_hi_ready, KT)
                    sp.wait_ge(ctx_lo_ready, KT)
                elif n >= 9 and r == 0:
                    sp.wait_ge(w_hi_ready, k)
                    sp.wait_ge(w_lo_ready, k)
                elif n >= 9:
                    sp.wait_ge(q_projected, 2 * (k - 1) + r)
                sp.dma_start(stage[place_of(n)][:, :, :],
                             A[kind][:, i * SC:(i + 1) * SC].rearrange("(c p) n -> p c n", p=P)
                             ).then_inc(stage_loaded[place_of(n)], 16)

            def load_rope(b):
                need(sp, k_products, 16 * b)
                sp.dma_start(cos_sb[:, :], A["cosT"][:, bass.ds(b * BK, BK)]).then_inc(rope_loaded, 16)
                sp.dma_start(sin_sb[:, :], A["sinT"][:, bass.ds(b * BK, BK)]).then_inc(rope_loaded, 16)

            def load_ctx(b, t):
                need(sp, ctx_hi_ready, KT * (b - 1) + t + 1)
                need(sp, ctx_lo_ready, KT * (b - 1) + t + 1)
                sp.dma_start(ctx_raw[:, t, :, :],
                             A["ctxT"][:, bass.ds(b * BK + t * P, P)].rearrange("(c p) n -> p c n", p=P)
                             ).then_inc(ctx_loaded[t], 16)

            def load_mask(b):
                need(sp, scores_masked, 16 * b)
                for h in range(2):
                    sp.dma_start(mask_sb[h * TOK:(h + 1) * TOK, :], A["mask"][:, bass.ds(b * BK, BK)]
                                 ).then_inc(mask_loaded, 16)

            sp.dma_start(x_sb[:, :], A["x"]).then_inc(x_loaded, 16)
            load_stage(0)
            load_ctx(0, 0)
            load_ctx(0, 1)
            sp.dma_start(ident[:, :], A["ident"]).then_inc(ident_loaded, 16)
            load_ctx(0, 2)
            load_ctx(0, 3)
            load_rope(0)
            for t in range(4, KT):
                load_ctx(0, t)
            sp.dma_start(qtab[:, :, :], A["qrope"]).then_inc(qtab_loaded, 16)
            load_stage(1)
            load_stage(2)
            load_stage(3)
            load_mask(0)
            for n in range(4, len(STAGED)):
                load_stage(n)
            for dst, src in ((b2_sb, "b2"), (hb_sb, "hbase"), (gate_sb, "gate"), (wb_sb, "wbranch"), (eye_sb, "eye")):
                sp.dma_start(dst[:, :], A[src]).then_inc(tail_loaded, 16)
            sp.dma_start(wf_sb[:, :, :], A["wffn"].rearrange("(c p) n -> p c n", p=P)).then_inc(tail_loaded, 16)
            load_rope(1)
            load_ctx(1, 6)
            sp.wait_ge(w_hi_ready, HKV)
            sp.wait_ge(w_lo_ready, HKV)
            for t in range(2):
                load_ctx(1, t)
            sp.wait_ge(q_projected, 2 * HKV)
            for t in range(2, 6):
                load_ctx(1, t)
            load_mask(1)

            with sp.Fori(2, NB) as b:
                load_rope(b)
                for t in range(KT):
                    load_ctx(b, t)
                load_mask(b)

            sp.wait_ge(k_projected, 16 * NB)
            sp.dma_start(w1_sb[:, :, :], A["w1"].rearrange("(c p) n -> p c n", p=P)).then_inc(w12_loaded, 16)
            sp.dma_start(w2t_sb[:, :, :], A["w2t"].rearrange("(c p) n -> p c n", p=P)).then_inc(w12_loaded, 16)
            sp.dma_start(smask_sb[:, :, :], A["smask"].rearrange("(c p) n -> p c n", p=P)).then_inc(smask_loaded, 16)
            sp.wait_ge(v_projected, 16 * NB)
            for i in range(4):
                a, z = WO_FIRST[i], WO_FIRST[i + 1]
                sp.dma_start(wo_sb[i][:, :, :], A["wo"][a * P:z * P, :].rearrange("(h p) n -> p h n", p=P)
                             ).then_inc(wo_loaded[i], 16)
            sp.wait_ge(dve_step, DVE_END)
            sp.dma_start(A["out"], ob[:, :]).then_inc(out_stored, 16)
            sp.wait_ge(out_stored, 16)

        def split_matmul(out, w_hi, w_lo, x_hi, x_lo, start, stop):
            nc.tensor.matmul(out, w_hi, x_hi, start=start, stop=False)
            nc.tensor.matmul(out, w_hi, x_lo, start=False, stop=False)
            return nc.tensor.matmul(out, w_lo, x_hi, start=False, stop=stop)

        def pe_project_k(pe, b, g, i):
            u = UNITS * b + g
            head, half = 2 * g + i // 2, i % 2
            if i >= 2:
                need(pe, k_products, 4 * u + i - 1)
            else:
                need(pe, v_lo_ready, 4 * (u - 1) + i + 3)
            if i < 2 and g == 0:
                tiles = KT * b + (i + 1) * KT // 2 + 1 - i
                pe.wait_ge(ctx_hi_ready, tiles)
                pe.wait_ge(ctx_lo_ready, tiles)
            if i == 0 and isinstance(b, int) and b == 0:
                pe.wait_ge(w_lo_ready, 2 * g + 1)
            cols = slice(half * HB, (half + 1) * HB)
            for c in range(DC):
                w = slice(head * DH, (head + 1) * DH)
                last = split_matmul(p_kv[i % 2][:, 0:HB], wk_hi[:, c, w], wk_lo[:, c, w],
                                    ct_hi[:, c, cols], ct_lo[:, c, cols], c == 0, c == DC - 1)
            last.then_inc(k_projected, 1)

        def pe_project_v(pe, b, g, i):
            u = UNITS * b + g
            if i >= 2:
                need(pe, v_lo_ready, 4 * u + i - 1)
            else:
                need(pe, k_products, 4 * u + i + 3)
            if i == 0 and isinstance(b, int) and b == 0:
                pe.wait_ge(w_lo_ready, 2 * g + 2)
            for j, t in enumerate(piece_tiles(i)):
                for c in range(DC):
                    k = slice(t * P, (t + 1) * P)
                    w = slice(g * 2 * DH, (g + 1) * 2 * DH)
                    last = split_matmul(p_kv[i % 2][:, j * 2 * DH:(j + 1) * 2 * DH], ct_hi[:, c, k], ct_lo[:, c, k],
                                        wv_hi[:, c, w], wv_lo[:, c, w], c == 0, c == DC - 1)
            last.then_inc(v_projected, 1)

        def pe_project_q(pe, k):
            need(pe, q_products, k)
            for r in range(2):
                n = 3 * k + 1 + r
                pe.wait_ge(stage_loaded[place_of(n)], 16 * turn_of(n))
                for j in range(2):
                    for c in range(DC):
                        last = nc.tensor.matmul(p_f[:, QC + (2 * r + j) * TOK:QC + (2 * r + j + 1) * TOK],
                                                stage[place_of(n)][:, c, j * DH:(j + 1) * DH], xnT[:, c, :],
                                                start=(c == 0), stop=(c == DC - 1))
                last.then_inc(q_projected, 1)

        def pe_scores(pe, b, g, s, i):
            u = UNITS * b + g
            h = 2 * u + s
            if i == 0:
                pe.wait_ge(k_lo_ready, 4 * u + 2 * s + 2)
                if isinstance(b, int) and b == 0:
                    pe.wait_ge(q_lo_ready, 2 * g + s + 1)
            need(pe, scores_masked, 2 * h + i)
            q = slice((2 * g + s) * QC + i * P, (2 * g + s) * QC + (i + 1) * P)
            for f in range(2):
                k = slice(f * HB, (f + 1) * HB)
                last = split_matmul(p_s[:, f, 0:HB], qt_hi[:, q], qt_lo[:, q], kt_hi[:, s, k], kt_lo[:, s, k], True, True)
            last.then_inc(scores_ready, 1)

        def pe_spread(pe, h, s, g, src):
            for i in range(2):
                col = 2 * (2 * g + s) + i
                last = nc.tensor.transpose(p_f[:, i * P:(i + 1) * P], src[:, col:col + 1].to_broadcast([P, P]), ident[:, :])
            last.then_inc(factor_spread, 1)

        def pe_transpose_probs(pe, h, s, p):
            if p == 0:
                pe.wait_ge(probs_ready, 2 * h + 2)
            need(pe, pt_lo_ready, 4 * h + p - 1)
            for j, t in enumerate(piece_tiles(p)):
                for i in range(2):
                    last = nc.tensor.transpose(p_t[p % 2][:, j * QC + i * P:j * QC + (i + 1) * P],
                                               scores[:, 2 * s + i, t * P:(t + 1) * P], ident[:, :])
            last.then_inc(probs_transposed, 1)

        def pe_pv(pe, h, s, p, v_count):
            pe.wait_ge(pt_lo_ready, 4 * h + p + 1)
            if p == 0:
                need(pe, acc_added, h)
            pe.wait_ge(v_lo_ready, v_count + p + 1)
            for j, t in enumerate(piece_tiles(p)):
                w = slice(s * DH, (s + 1) * DH)
                last = split_matmul(p_o[:, 0:QC], v_hi[:, t, w], v_lo[:, t, w], pt_hi[:, p % 2, j, :], pt_lo[:, p % 2, j, :],
                                    t == 0, t == KT - 1)
            last.then_inc(pv_done, 1)

        def pe_slot(pe, b, g, s, prev=True, last=False):
            u = UNITS * b + g
            h = 2 * u + s
            pg, psn = (g, 0) if s else ((g - 1) % UNITS, 1)
            v_count = 4 * u if s else 4 * (u - 1)

            def fill(i):
                if s == 0:
                    pe_project_v(pe, b, g, i)
                elif g < UNITS - 1:
                    pe_project_k(pe, b, g + 1, i)
                elif not last:
                    pe_project_k(pe, b + 1, 0, i)
                else:
                    pe_mix(pe, i)

            if prev:
                pe_transpose_probs(pe, h - 1, psn, 0)
                pe.wait_ge(factor_ready, 2 * h)
                need(pe, acc_scaled, h - 1)
                if isinstance(b, int) and b == 0:
                    pe.wait_ge(q_products, h + 1)
                pe_spread(pe, h - 1, psn, pg, fac)
            pe_scores(pe, b, g, s, 0)
            if prev:
                pe_transpose_probs(pe, h - 1, psn, 1)
                pe_pv(pe, h - 1, psn, 0, v_count)
            fill(0)
            if isinstance(b, int) and b == 0 and h < HKV - 1:
                need(pe, acc_scaled, h)
                pe_project_q(pe, h + 1)
            pe_scores(pe, b, g, s, 1)
            if prev:
                pe_transpose_probs(pe, h - 1, psn, 2)
                pe_pv(pe, h - 1, psn, 1, v_count)
            fill(1)
            if prev:
                pe_transpose_probs(pe, h - 1, psn, 3)
                pe_pv(pe, h - 1, psn, 2, v_count)
            fill(2)
            if prev:
                pe_pv(pe, h - 1, psn, 3, v_count)
            fill(3)

        def pe_mix(pe, i):
            if i == 0:
                pe.wait_ge(w12_loaded, 32)
            if i < 2:
                pe.wait_ge(v_lo_ready, 16 * NB)
            else:
                pe.wait_ge(dve_step, DVE_MIX + i - 1)
            for c in range(DC):
                last = nc.tensor.matmul(p_kv[i % 2][:, :], w1_sb[:, c, i * P:(i + 1) * P], w2t_sb[:, c, :],
                                        start=(c == 0), stop=(c == DC - 1))
            last.then_inc(pe_step, 1)

        @block.tensor
        def _(pe):
            pe.wait_ge(dve_step, DVE_XN)
            pe.wait_ge(ident_loaded, 16)
            for c in range(DC):
                last = nc.tensor.transpose(p_o[:, c * TOK:(c + 1) * TOK], xn[:, c * P:(c + 1) * P], ident[0:TOK, 0:TOK])
            last.then_inc(pe_step, 1)
            for i in range(2):
                pe_project_k(pe, 0, 0, i)
            pe.wait_ge(dve_step, DVE_XNT)
            pe_project_q(pe, 0)
            for i in range(2, 4):
                pe_project_k(pe, 0, 0, i)

            def pe_block(b, first=False, last=False):
                for g in range(UNITS):
                    for s in range(2):
                        pe_slot(pe, b, g, s, prev=not (first and g == 0 and s == 0), last=last)

            pe_block(0, first=True)
            with pe.Fori(1, NB - 1) as b:
                pe_block(b)
            pe_block(NB - 1, last=True)
            h = 8 * NB - 1
            pe_transpose_probs(pe, h, 1, 0)
            pe.wait_ge(factor_ready, 2 * h + 2)
            pe.wait_ge(acc_scaled, h)
            pe_spread(pe, h, 1, UNITS - 1, fac)
            pe_transpose_probs(pe, h, 1, 1)
            pe_pv(pe, h, 1, 0, 16 * NB - 4)
            pe_transpose_probs(pe, h, 1, 2)
            pe_pv(pe, h, 1, 1, 16 * NB - 4)
            pe_transpose_probs(pe, h, 1, 3)
            pe_pv(pe, h, 1, 2, 16 * NB - 4)
            pe_pv(pe, h, 1, 3, 16 * NB - 4)
            pe.wait_ge(dve_step, DVE_LINV)
            for g in range(HKV):
                pe.wait_ge(acc_scaled, 8 * NB + g)
                pe_spread(pe, None, g % 2, g // 2, l_inv)
            for hq in range(HQ):
                i = max(j for j in range(4) if WO_FIRST[j] <= hq)
                if hq == WO_FIRST[i]:
                    pe.wait_ge(wo_loaded[i], 16)
                if hq % 4 == 0:
                    pe.wait_ge(acc_scaled, 8 * NB + hq // 4 + 1)
                last = nc.tensor.matmul(p_o[0:TOK, :], acc[:, hq // 4, (hq % 4) * TOK:(hq % 4 + 1) * TOK],
                                        wo_sb[i][:, hq - WO_FIRST[i], :], start=(hq == 0), stop=(hq == HQ - 1))
            last.then_inc(pe_step, 1)

            def transpose_rows(src):
                for c in range(DC):
                    last = nc.tensor.transpose(p_f[:, c * TOK:(c + 1) * TOK], src[:, c * P:(c + 1) * P], ident[0:TOK, 0:TOK])
                last.then_inc(pe_step, 1)

            pe.wait_ge(dve_step, DVE_XN2)
            transpose_rows(xn)
            pe.wait_ge(dve_step, DVE_XNT2)
            for c in range(DC):
                last = nc.tensor.matmul(p_o[0:TOK, :], xnT[:, c, :], mixw[:, c, :], start=(c == 0), stop=(c == DC - 1))
            last.then_inc(pe_step, 1)
            pe.wait_ge(dve_step, DVE_XRMS)
            transpose_rows(xn)
            pe.wait_ge(dve_step, DVE_XNT3)
            pe.wait_ge(tail_loaded, 96)
            for c in range(DC):
                last = nc.tensor.matmul(p_o[0:TOK, 0:24], xnT[:, c, :], wf_sb[:, c, :], start=(c == 0), stop=(c == DC - 1))
            last.then_inc(pe_step, 1)
            pe.wait_ge(dve_step, DVE_XPRE)
            nc.tensor.transpose(p_f[:, 0:TOK], xpre[:, :], ident[0:TOK, 0:TOK]).then_inc(pe_step, 1)
            pe.wait_ge(dve_step, DVE_XPT)
            nc.tensor.matmul(p_o[0:TOK, 0:P], xpT[:, :], wb_sb[:, :], start=True, stop=True).then_inc(pe_step, 1)
            pe.wait_ge(dve_step, DVE_BOUND)
            nc.tensor.transpose(p_f[0:1, 0:TOK], zlim[:, 2:3], ident[0:TOK, 0:TOK]).then_inc(pe_step, 1)

        def act_v_hi(act, b, g, i):
            u = UNITS * b + g
            act.wait_ge(v_projected, 4 * u + i + 1)
            need(act, pv_done, 4 * (2 * u - 1) + i + 1)
            n = len(piece_tiles(i)) * 2 * DH
            nc.scalar.activation(v_hi[:, 2 * i:2 * i + len(piece_tiles(i)), :].rearrange("p t n -> p (t n)"),
                                 p_kv[i % 2][:, 0:n], ACT.Copy).then_inc(v_hi_ready, 1)

        def act_k_hi(act, b, g, i):
            u = UNITS * b + g
            act.wait_ge(k_rotated, 4 * u + i + 1)
            f = i % 2
            nc.scalar.activation(kt_hi[:, i // 2, f * HB:(f + 1) * HB], rc[:, i % 2, 0:HB], ACT.Copy).then_inc(k_hi_ready, 1)

        def act_pt_hi(act, h, p):
            act.wait_ge(probs_transposed, 4 * h + p + 1)
            need(act, pv_done, 4 * h + p - 1)
            n = len(piece_tiles(p)) * QC
            nc.scalar.activation(pt_hi[:, p % 2, :, :].rearrange("p t n -> p (t n)")[:, 0:n], p_t[p % 2][:, 0:n],
                                 ACT.Copy).then_inc(pt_hi_ready, 1)

        def act_exp(act, b, g, s, i):
            n = 2 * (2 * (UNITS * b + g) + s) + i
            col = 2 * (2 * g + s) + i
            act.wait_ge(max_dropped, n + 1)
            nc.scalar.activation(fac[:, col:col + 1], m_drop[:, col:col + 1], ACT.Exp).then_inc(factor_ready, 1)
            act.wait_ge(max_negated, n + 1)
            nc.scalar.activation(scores[:, 2 * s + i, :], scores[:, 2 * s + i, :], ACT.Exp, bias=m_neg[:, col:col + 1],
                                 accum_out=rsum[:, col:col + 1]).then_inc(probs_ready, 1)

        @block.scalar
        def _(act):
            def w_hi(k):
                n = 3 * k
                act.wait_ge(stage_loaded[place_of(n)], 16 * turn_of(n))
                dst = (wv_hi if k % 2 else wk_hi)[:, :, k // 2 * SC:(k // 2 + 1) * SC]
                nc.scalar.activation(dst, stage[place_of(n)][:, :, :], ACT.Copy).then_inc(w_hi_ready, 1)

            def ctx_hi(b, t):
                act.wait_ge(ctx_loaded[t], 16 * (b + 1))
                need(act, v_projected, 16 * (b - 1) + 13 + t // 2)
                nc.scalar.activation(ct_hi[:, :, t * P:(t + 1) * P], ctx_raw[:, t, :, :], ACT.Copy).then_inc(ctx_hi_ready, 1)

            def q_hi(k):
                act.wait_ge(q_rotated, k + 1)
                nc.scalar.activation(qt_hi[:, k * QC:(k + 1) * QC], rq[:, :], ACT.Copy).then_inc(q_hi_ready, 1)

            w_hi(0)
            for t in range(KT):
                ctx_hi(0, t)
            for i in range(2):
                act_k_hi(act, 0, 0, i)
            w_hi(1)
            q_hi(0)
            for i in range(2, 4):
                act_k_hi(act, 0, 0, i)

            def act_slot(b, g, s, prev=True, last=False):
                h = 2 * (UNITS * b + g) + s

                def keys(i):
                    if g < UNITS - 1:
                        act_k_hi(act, b, g + 1, i)
                    elif not last:
                        act_k_hi(act, b + 1, 0, i)

                def split_ctx(at, *tiles):
                    if (g, s) == (UNITS - 1, at) and not last:
                        for t in tiles:
                            ctx_hi(b + 1, t)

                if prev:
                    act_pt_hi(act, h - 1, 0)
                    if s == 0:
                        act_k_hi(act, b, g, 2)
                    act_pt_hi(act, h - 1, 1)
                split_ctx(1, 4, 5, 6)
                act_exp(act, b, g, s, 0)
                if s == 0:
                    act_v_hi(act, b, g, 0)
                if prev:
                    act_pt_hi(act, h - 1, 2)
                    if s == 0:
                        act_k_hi(act, b, g, 3)
                act_exp(act, b, g, s, 1)
                if s == 0:
                    act_v_hi(act, b, g, 1)
                    split_ctx(0, 0, 1)
                else:
                    keys(0)
                if prev:
                    act_pt_hi(act, h - 1, 3)
                if s == 0:
                    if isinstance(b, int) and b == 0:
                        q_hi(h + 1)
                    act_v_hi(act, b, g, 2)
                    split_ctx(0, 2, 3)
                    act_v_hi(act, b, g, 3)
                else:
                    keys(1)
                if isinstance(b, int) and b == 0:
                    if s == 1 and h + 1 < HKV:
                        q_hi(h + 1)
                    if h + 2 < HKV:
                        w_hi(h + 2)

            def act_block(b, first=False, last=False):
                for g in range(UNITS):
                    for s in range(2):
                        act_slot(b, g, s, prev=not (first and g == 0 and s == 0), last=last)

            act_block(0, first=True)
            with act.Fori(1, NB - 1) as b:
                act_block(b)
            act_block(NB - 1, last=True)
            for p in range(PIECES):
                act_pt_hi(act, 8 * NB - 1, p)

            act.wait_ge(dve_step, DVE_Z)
            nc.scalar.activation(x2[:, :], t0[:, :], ACT.Gelu).then_inc(act_step, 1)
            act.wait_ge(tail_loaded, 96)
            nc.scalar.activation(half_sb[:, :], gate_sb[:, :], ACT.Exp, scale=-1.0).then_inc(act_step, 1)
            act.wait_ge(dve_step, DVE_PMAX)
            nc.scalar.activation(hp[:, 0:8], hp[:, 8:16], ACT.Exp).then_inc(act_step, 1)
            act.wait_ge(dve_step, DVE_ZS)
            nc.scalar.activation(kk[:, :], tt[:, :], ACT.Exp).then_inc(act_step, 1)
            act.wait_ge(dve_step, DVE_FLAG)
            again = act.value_load(wide_flag[0:1, 0:1])
            with act.If(again == 1):
                with act.Fori(0, SINK) as it:
                    for r in range(2):
                        act.wait_ge(sk_shifted, 2 * it + r + 1)
                        nc.scalar.activation(ee[:, :], tt[:, :], ACT.Exp).then_inc(sk_exp, 1)
                        act.wait_ge(sk_summed, 2 * it + r + 1)
                        nc.scalar.activation(lns[:, :], sm4[:, :], ACT.Ln).then_inc(sk_ln, 1)
                act.wait_ge(sk_shifted, 2 * SINK + 1)
                nc.scalar.activation(hres[:, :], tt[:, :], ACT.Exp).then_inc(sk_exp, 1)

        @block.gpsimd
        def _(pool):
            def w_lo(k):
                n = 3 * k
                cols = slice(k // 2 * SC, (k // 2 + 1) * SC)
                hi, lo = (wv_hi, wv_lo) if k % 2 else (wk_hi, wk_lo)
                pool.wait_ge(stage_loaded[place_of(n)], 16 * turn_of(n))
                pool.wait_ge(w_hi_ready, k + 1)
                nc.gpsimd.tensor_tensor(lo[:, :, cols], stage[place_of(n)][:, :, :], hi[:, :, cols].bitcast(F32),
                                        ALU.subtract).then_inc(w_lo_ready, 1)

            def rotate_q(k):
                pool.wait_ge(q_products, k + 1)
                nc.gpsimd.tensor_tensor(rq[:, :], rq[:, :], rqs[:, :], ALU.add).then_inc(q_rotated, 1)
                pool.wait_ge(q_rotated, k + 1)
                pool.wait_ge(q_hi_ready, k + 1)
                cols = slice(k * QC, (k + 1) * QC)
                nc.gpsimd.tensor_tensor(qt_lo[:, cols], rq[:, :], qt_hi[:, cols].bitcast(F32), ALU.subtract
                                        ).then_inc(q_lo_ready, 1)

            def rotate(b, g, i):
                u = UNITS * b + g
                pool.wait_ge(k_products, 4 * u + i + 1)
                nc.gpsimd.tensor_tensor(rc[:, i % 2, 0:HB], rc[:, i % 2, 0:HB], rs[:, i % 2, 0:HB], ALU.add
                                        ).then_inc(k_rotated, 1)
                pool.wait_ge(k_rotated, 4 * u + i + 1)
                pool.wait_ge(k_hi_ready, 4 * u + i + 1)
                f = slice((i % 2) * HB, (i % 2 + 1) * HB)
                nc.gpsimd.tensor_tensor(kt_lo[:, i // 2, f], rc[:, i % 2, 0:HB], kt_hi[:, i // 2, f].bitcast(F32),
                                        ALU.subtract).then_inc(k_lo_ready, 1)

            nc.gpsimd.memset(mv[:, 3:4], -0.5).then_inc(pool_step, 1)
            pool.wait_ge(pool_step, 1)
            pool.wait_ge(dve_step, DVE_VAR)
            nc.gpsimd.tensor_tensor(mv[:, 2:3], mv[:, 1:2], mv[:, 3:4], ALU.pow).then_inc(pool_step, 1)
            w_lo(0)
            rotate(0, 0, 0)
            rotate(0, 0, 1)
            w_lo(1)
            rotate_q(0)
            rotate(0, 0, 2)
            rotate(0, 0, 3)

            for g in range(UNITS):
                rotate_q(2 * g + 1)
                nb, ng = (0, g + 1) if g < UNITS - 1 else (1, 0)
                if g < UNITS - 1:
                    w_lo(2 * g + 2)
                rotate(nb, ng, 0)
                rotate(nb, ng, 1)
                if g < UNITS - 1:
                    rotate_q(2 * g + 2)
                    w_lo(2 * g + 3)
                rotate(nb, ng, 2)
                rotate(nb, ng, 3)
            with pool.Fori(1, NB - 1) as b:
                for g in range(UNITS):
                    for i in range(4):
                        rotate(b + 1 if g == UNITS - 1 else b, (g + 1) % UNITS, i)
            for g in range(UNITS - 1):
                for i in range(4):
                    rotate(NB - 1, g + 1, i)
            for k in range(3):
                pool.wait_ge(dve_step, (DVE_VAR2, DVE_VAR3, DVE_MS)[k])
                nc.gpsimd.tensor_tensor(mv[:, 2:3], mv[:, 1:2], mv[:, 3:4], ALU.pow).then_inc(pool_step, 1)

        @block.vector
        def _(dve):
            count = [0]

            def step(ins, expect=None):
                count[0] += 1
                ins.then_inc(dve_step, 1)
                dve.wait_ge(dve_step, count[0])
                assert expect is None or expect == count[0], (expect, count[0])

            def layer_stats(src, var_at):
                step(nc.vector.bn_stats(bnst[:, :], src[:, :]))
                step(nc.vector.bn_aggr(mv[:, 0:2], bnst[:, :]))
                step(nc.vector.tensor_scalar(mv[:, 1:2], mv[:, 1:2], EPS, None, ALU.add), var_at)

            def normalise(dst, src, pool_at, at):
                dve.wait_ge(pool_step, pool_at)
                step(nc.vector.tensor_scalar(dst[:, :], src[:, :], mv[:, 0:1], mv[:, 2:3], ALU.subtract, ALU.mult), at)

            def ctx_lo(b, t):
                dve.wait_ge(ctx_hi_ready, KT * b + t + 1)
                dve.wait_ge(ctx_loaded[t], 16 * (b + 1))
                k = slice(t * P, (t + 1) * P)
                nc.vector.tensor_tensor(ct_lo[:, :, k], ctx_raw[:, t, :, :], ct_hi[:, :, k].bitcast(F32), ALU.subtract
                                        ).then_inc(ctx_lo_ready, 1)

            def q_rope(k):
                dve.wait_ge(q_projected, 2 * k + 2)
                need(dve, q_lo_ready, k)
                if k == 0:
                    dve.wait_ge(qtab_loaded, 16)

                def heads(x):
                    return x.rearrange("p (h t) -> p h t", t=TOK)

                for dst, frm, tab in ((rq, slice(0, P), 0), (rqs, slice(0, HALF), 1), (rqs, slice(HALF, P), 1)):
                    src = frm if tab == 0 else slice(HALF - frm.start, P + HALF - frm.stop)
                    last = nc.vector.tensor_tensor(heads(dst[frm, :]), heads(p_f[src, QC:2 * QC]),
                                                   qtab[src, tab:tab + 1, :].to_broadcast([frm.stop - frm.start, 4, TOK]),
                                                   ALU.mult)
                last.then_inc(q_products, 1)

            def k_rope(b, g, i):
                u = UNITS * b + g
                dve.wait_ge(k_projected, 4 * u + i + 1)
                need(dve, k_lo_ready, 4 * u + i - 1)
                if i == 0 and g == 0:
                    dve.wait_ge(rope_loaded, 32 * (b + 1))
                f = slice((i % 2) * HB, (i % 2 + 1) * HB)
                src = p_kv[i % 2]
                nc.vector.tensor_tensor(rc[:, i % 2, 0:HB], src[:, 0:HB], cos_sb[:, f], ALU.mult)
                nc.vector.tensor_tensor(rs[0:HALF, i % 2, 0:HB], src[HALF:P, 0:HB], sin_sb[HALF:P, f], ALU.mult)
                nc.vector.tensor_tensor(rs[HALF:P, i % 2, 0:HB], src[0:HALF, 0:HB], sin_sb[0:HALF, f], ALU.mult)\
                    .then_inc(k_products, 1)

            def v_low(b, g, i):
                u = UNITS * b + g
                dve.wait_ge(v_hi_ready, 4 * u + i + 1)
                n = len(piece_tiles(i))
                tiles = slice(2 * i, 2 * i + n)
                nc.vector.tensor_tensor(v_lo[:, tiles, :].rearrange("p t n -> p (t n)"), p_kv[i % 2][:, 0:n * 2 * DH],
                                        v_hi[:, tiles, :].bitcast(F32).rearrange("p t n -> p (t n)"), ALU.subtract
                                        ).then_inc(v_lo_ready, 1)

            def pt_low(h, p):
                dve.wait_ge(pt_hi_ready, 4 * h + p + 1)
                n = len(piece_tiles(p)) * QC
                nc.vector.tensor_tensor(pt_lo[:, p % 2, :, :].rearrange("p t n -> p (t n)")[:, 0:n], p_t[p % 2][:, 0:n],
                                        pt_hi[:, p % 2, :, :].bitcast(F32).rearrange("p t n -> p (t n)")[:, 0:n],
                                        ALU.subtract).then_inc(pt_lo_ready, 1)

            def mask_scores(b, g, s, i):
                h = 2 * (UNITS * b + g) + s
                n = 2 * h + i
                col = 2 * (2 * g + s) + i
                c = slice(col, col + 1)
                dve.wait_ge(scores_ready, n + 1)
                if i == 0:
                    if g == 0 and s == 0:
                        dve.wait_ge(mask_loaded, 32 * (b + 1))
                    need(dve, probs_transposed, 4 * (h - 1))
                    need(dve, scores_masked, 2 * h)
                nc.vector.tensor_copy(m_old[:, c], m_run[:, c]).then_inc(max_kept, 1)
                nc.vector.tensor_tensor_reduce(out=scores[:, 2 * s + i, :].rearrange("p (f n) -> p f n", f=2),
                                               in0=p_s[:, :, 0:HB], in1=mask_sb[:, :].rearrange("p (f n) -> p f n", f=2),
                                               scale=1.0, scalar=m_run[:, c], op0=ALU.add, op1=ALU.max,
                                               accum_out=m_run[:, c]).then_inc(scores_masked, 1)
                dve.wait_ge(scores_masked, n + 1)
                dve.wait_ge(max_kept, n + 1)
                nc.vector.tensor_tensor(m_drop[:, c], m_old[:, c], m_run[:, c], ALU.subtract).then_inc(max_dropped, 1)
                nc.vector.tensor_scalar(m_neg[:, c], m_run[:, c], -1.0, None, ALU.mult).then_inc(max_negated, 1)

            def keep_sums(h, g, s):
                c = slice(2 * (2 * g + s), 2 * (2 * g + s) + 2)
                dve.wait_ge(probs_ready, 2 * h + 2)
                dve.wait_ge(factor_ready, 2 * h + 2)
                need(dve, sums_kept, 2 * h)
                nc.vector.tensor_tensor(l_run[:, c], l_run[:, c], fac[:, c], ALU.mult).then_inc(sums_kept, 1)
                dve.wait_ge(sums_kept, 2 * h + 1)
                nc.vector.tensor_tensor(l_run[:, c], l_run[:, c], rsum[:, c], ALU.add).then_inc(sums_kept, 1)

            def acc_scale(h, head):
                dve.wait_ge(factor_spread, h + 1)
                need(dve, acc_added, h)
                nc.vector.tensor_tensor(acc[:, head, :], acc[:, head, :], p_f[:, 0:QC], ALU.mult).then_inc(acc_scaled, 1)

            def acc_add(h, head):
                dve.wait_ge(pv_done, 4 * h + 4)
                dve.wait_ge(acc_scaled, h + 1)
                nc.vector.tensor_tensor(acc[:, head, :], acc[:, head, :], p_o[:, 0:QC], ALU.add).then_inc(acc_added, 1)

            dve.wait_ge(x_loaded, 16)
            layer_stats(x_sb, DVE_VAR)
            normalise(xn, x_sb, 2, DVE_XN)
            for t in range(4):
                ctx_lo(0, t)
            dve.wait_ge(pe_step, PE_XNT)
            step(nc.vector.tensor_copy(xnT[:, :, :].rearrange("p c n -> p (c n)"), p_o[:, 0:DC * TOK]), DVE_XNT)
            for t in range(4, KT):
                ctx_lo(0, t)
            k_rope(0, 0, 0)
            k_rope(0, 0, 1)
            q_rope(0)
            k_rope(0, 0, 2)
            step(nc.vector.memset(m_run[:, :], -3.0e38))
            step(nc.vector.memset(l_run[:, :], 0.0), DVE_MIX)
            nc.vector.memset(acc[:, :, :].rearrange("p h n -> p (h n)"), 0.0).then_inc(acc_cleared, 1)
            dve.wait_ge(acc_cleared, 1)
            k_rope(0, 0, 3)

            def dve_slot(b, g, s, prev=True, last=False):
                h = 2 * (UNITS * b + g) + s
                ph = (2 * g + s - 1) % HKV

                def fill(i):
                    if s == 0:
                        v_low(b, g, i)
                    elif g < UNITS - 1:
                        k_rope(b, g + 1, i)
                    elif not last:
                        k_rope(b + 1, 0, i)
                    else:
                        dve.wait_ge(pe_step, PE_XNT + i + 1)
                        if i == 0:
                            dve.wait_ge(smask_loaded, 16)
                        step(nc.vector.tensor_tensor(mixw[:, i, :], p_kv[i % 2][:, :], smask_sb[:, i, :], ALU.mult))

                def split_ctx(at, *tiles):
                    if (g, s) == (UNITS - 1, at) and not last:
                        for t in tiles:
                            ctx_lo(b + 1, t)

                if prev:
                    pt_low(h - 1, 0)
                    acc_scale(h - 1, ph)
                mask_scores(b, g, s, 0)
                if prev:
                    pt_low(h - 1, 1)
                    if s == 0:
                        k_rope(b, g, 3)
                split_ctx(1, 4, 5, 6)
                fill(0)
                if isinstance(b, int) and b == 0 and h + 1 < HKV:
                    q_rope(h + 1)
                mask_scores(b, g, s, 1)
                if prev:
                    pt_low(h - 1, 2)
                fill(1)
                split_ctx(0, 0, 1)
                if prev:
                    pt_low(h - 1, 3)
                fill(2)
                split_ctx(0, 2, 3)
                if prev:
                    acc_add(h - 1, ph)
                keep_sums(h, g, s)
                if s == 0 or last and g == UNITS - 1:
                    fill(3)
            def dve_block(b, first=False, last=False):
                for g in range(UNITS):
                    for s in range(2):
                        dve_slot(b, g, s, prev=not (first and g == 0 and s == 0), last=last)

            dve_block(0, first=True)
            with dve.Fori(1, NB - 1) as b:
                dve_block(b)
            dve_block(NB - 1, last=True)
            h = 8 * NB - 1
            acc_scale(h, HKV - 1)
            for p in range(PIECES):
                pt_low(h, p)
            acc_add(h, HKV - 1)
            dve.wait_ge(sums_kept, 2 * h + 2)
            step(nc.vector.reciprocal(l_inv[:, :], l_run[:, :]), DVE_LINV)
            dve.wait_ge(acc_added, 8 * NB)
            for head in range(HKV):
                dve.wait_ge(factor_spread, 8 * NB + head + 1)
                nc.vector.tensor_tensor(acc[:, head, :], acc[:, head, :], p_f[:, 0:QC], ALU.mult).then_inc(acc_scaled, 1)

            dve.wait_ge(pe_step, PE_Y)
            step(nc.vector.tensor_tensor(x1[:, :], p_o[0:TOK, :], x_sb[:, :], ALU.add), DVE_X1)
            layer_stats(x1, DVE_VAR2)
            normalise(xn, x1, 3, DVE_XN2)
            dve.wait_ge(pe_step, PE_X1T)
            step(nc.vector.tensor_copy(xnT[:, :, :].rearrange("p c n -> p (c n)"), p_f[:, 0:DC * TOK]), DVE_XNT2)
            dve.wait_ge(pe_step, PE_Z)
            dve.wait_ge(tail_loaded, 96)
            step(nc.vector.tensor_tensor(t0[:, :], p_o[0:TOK, :], b2_sb[:, :], ALU.add), DVE_Z)
            dve.wait_ge(act_step, 1)
            step(nc.vector.tensor_tensor(x2[:, :], x2[:, :], x1[:, :], ALU.add), DVE_X2)
            layer_stats(x2, DVE_VAR3)
            normalise(xf, x2, 4, DVE_XF)
            step(nc.vector.tensor_tensor_reduce(out=t0[:, :], in0=xf[:, :], in1=xf[:, :], scale=1.0, scalar=0.0,
                                                op0=ALU.mult, op1=ALU.add, accum_out=mv[:, 0:1]))
            step(nc.vector.tensor_scalar(mv[:, 1:2], mv[:, 0:1], 1.0 / D, RMS_EPS, ALU.mult, ALU.add), DVE_MS)
            dve.wait_ge(pool_step, 5)
            step(nc.vector.tensor_scalar(xn[:, :], xf[:, :], mv[:, 2:3], None, ALU.mult), DVE_XRMS)
            dve.wait_ge(pe_step, PE_XNT3)
            step(nc.vector.tensor_copy(xnT[:, :, :].rearrange("p c n -> p (c n)"), p_f[:, 0:DC * TOK]), DVE_XNT3)
            dve.wait_ge(pe_step, PE_LOGITS)
            step(nc.vector.tensor_tensor(lg[:, :], p_o[0:TOK, 0:24], hb_sb[:, :], ALU.add), DVE_LG)
            step(nc.vector.tensor_reduce(mx4[:, 0:2], lg[:, 16:24].rearrange("p (k n) -> p k n", k=2), AX_X, ALU.max))
            step(nc.vector.tensor_tensor(hp[:, 8:16].rearrange("p (k n) -> p k n", k=2),
                                         lg[:, 16:24].rearrange("p (k n) -> p k n", k=2),
                                         mx4[:, 0:2].unsqueeze(2).to_broadcast([TOK, 2, 4]), ALU.subtract), DVE_PMAX)
            step(nc.vector.tensor_scalar(zz[:, :], lg[:, 0:16], INV_TAU, None, ALU.mult))
            step(nc.vector.tensor_reduce(zlim[:, 0:1], zz[:, :], AX_X, ALU.max))
            step(nc.vector.tensor_reduce(zlim[:, 1:2], zz[:, :], AX_X, ALU.min))
            step(nc.vector.tensor_tensor(zlim[:, 2:3], zlim[:, 0:1], zlim[:, 1:2], ALU.subtract))
            step(nc.vector.scalar_tensor_tensor(out=zlim[:, 3:4], in0=zlim[:, 2:3], scalar=0.5, in1=zlim[:, 1:2],
                                                op0=ALU.mult, op1=ALU.add))
            step(nc.vector.tensor_scalar(tt[:, :], zz[:, :], zlim[:, 3:4], None, ALU.subtract), DVE_ZS)
            dve.wait_ge(act_step, 3)
            step(nc.vector.tensor_reduce(sm4[:, 0:2], hp[:, 0:8].rearrange("p (k n) -> p k n", k=2), AX_X, ALU.add))
            step(nc.vector.reciprocal(sm4[:, 2:4], sm4[:, 0:2]))
            step(nc.vector.tensor_tensor(hp[:, 0:8].rearrange("p (k n) -> p k n", k=2),
                                         hp[:, 0:8].rearrange("p (k n) -> p k n", k=2),
                                         sm4[:, 2:4].unsqueeze(2).to_broadcast([TOK, 2, 4]), ALU.mult), DVE_PRE)
            step(nc.vector.tensor_scalar(xpre[:, :], xf[:, 0:P], hp[:, 0:1], None, ALU.mult))
            for n in range(1, NS):
                step(nc.vector.scalar_tensor_tensor(out=xpre[:, :], in0=xf[:, n * P:(n + 1) * P], scalar=hp[:, n:n + 1],
                                                    in1=xpre[:, :], op0=ALU.mult, op1=ALU.add))
            dve.wait_ge(pe_step, PE_XPT)
            step(nc.vector.tensor_copy(xpT[:, :], p_f[:, 0:TOK]), DVE_XPT)
            def rows_of(x, order):
                return x[:, :].rearrange(f"p (i j) -> p {order}", j=NS)

            def inner(x):
                return x[:, :].unsqueeze(1).to_broadcast([TOK, NS, NS])

            def outer(x):
                return x[:, :].unsqueeze(2).to_broadcast([TOK, NS, NS])

            t_in = rows_of(tt, "i j")
            e_in = rows_of(ee, "i j")
            HALVES = (("i j", vv, uu), ("j i", uu, vv))
            dve.wait_ge(pe_step, PE_BR)
            step(nc.vector.tensor_copy(ybr[:, :], p_o[0:TOK, 0:P]), DVE_YBR)
            step(nc.vector.memset(vv[:, :], 1.0))
            step(nc.vector.memset(sums_max[:, :, :], 1.0))
            step(nc.vector.memset(sums_min[:, :, :], 1.0))
            dve.wait_ge(act_step, 4)
            with dve.Fori(0, SINK // SINK_UNROLL) as it:
                for k in range(2 * SINK_UNROLL):
                    order, other, mine = HALVES[k % 2]
                    done = 3 * (2 * SINK_UNROLL * it + k)
                    dve.wait_ge(sk_linear, done)
                    nc.vector.tensor_tensor(t_in, rows_of(kk, order), inner(other), ALU.mult).then_inc(sk_linear, 1)
                    dve.wait_ge(sk_linear, done + 1)
                    nc.vector.tensor_reduce(sums[:, k, :], t_in, AX_X, ALU.add).then_inc(sk_linear, 1)
                    dve.wait_ge(sk_linear, done + 2)
                    nc.vector.reciprocal(mine[:, :], sums[:, k, :]).then_inc(sk_linear, 1)
                dve.wait_ge(sk_limits, 2 * it)
                nc.vector.tensor_tensor(sums_max[:, :, :], sums_max[:, :, :], sums[:, :, :], ALU.max).then_inc(sk_limits, 1)
                nc.vector.tensor_tensor(sums_min[:, :, :], sums_min[:, :, :], sums[:, :, :], ALU.min).then_inc(sk_limits, 1)
            dve.wait_ge(sk_linear, 6 * SINK)
            dve.wait_ge(sk_limits, 2 * SINK // SINK_UNROLL)
            step(nc.vector.tensor_reduce(zlim[:, 4:5], sums_max[:, :, :].rearrange("p k n -> p (k n)"), AX_X, ALU.max))
            step(nc.vector.tensor_reduce(zlim[:, 5:6], sums_min[:, :, :].rearrange("p k n -> p (k n)"), AX_X, ALU.min))
            step(nc.vector.reciprocal(zlim[:, 6:7], zlim[:, 5:6]))
            step(nc.vector.tensor_tensor(zlim[:, 7:8], zlim[:, 4:5], zlim[:, 6:7], ALU.max))
            step(nc.vector.tensor_scalar(zlim[:, 3:4], zlim[:, 2:3], 1.0 / Z_SPREAD_MAX, None, ALU.mult))
            step(nc.vector.scalar_tensor_tensor(out=zlim[:, 2:3], in0=zlim[:, 7:8], scalar=1.0 / SUM_MAX,
                                                in1=zlim[:, 3:4], op0=ALU.mult, op1=ALU.max), DVE_BOUND)
            nc.vector.tensor_tensor(t_in, rows_of(kk, "i j"), inner(vv), ALU.mult).then_inc(sk_linear, 1)
            dve.wait_ge(sk_linear, 6 * SINK + 1)
            nc.vector.tensor_tensor(rows_of(hres, "i j"), t_in, outer(uu), ALU.mult).then_inc(sk_linear, 1)
            dve.wait_ge(sk_linear, 6 * SINK + 2)
            dve.wait_ge(pe_step, PE_WIDE)
            step(nc.vector.tensor_reduce(wide[:, 0:1], p_f[0:1, 0:TOK], AX_X, ALU.max))
            step(nc.vector.tensor_scalar(wide_flag[:, :], wide[:, 0:1], 1.0, None, ALU.is_gt), DVE_FLAG)
            again = dve.value_load(wide_flag[0:1, 0:1])
            with dve.If(again == 1):
                nc.vector.memset(vv[:, :], 0.0).then_inc(sk_state, 1)
                with dve.Fori(0, SINK) as it:
                    for r, (order, other, mine) in enumerate(HALVES):
                        done = 8 * it + 4 * r + 1
                        dve.wait_ge(sk_state, done)
                        nc.vector.tensor_tensor(t_in, rows_of(zz, order), inner(other), ALU.add).then_inc(sk_state, 1)
                        dve.wait_ge(sk_state, done + 1)
                        nc.vector.tensor_reduce(mx4[:, :], t_in, AX_X, ALU.max).then_inc(sk_state, 1)
                        dve.wait_ge(sk_state, done + 2)
                        nc.vector.tensor_tensor(t_in, t_in, outer(mx4), ALU.subtract).then_inc(sk_shifted, 1)
                        dve.wait_ge(sk_exp, 2 * it + r + 1)
                        nc.vector.tensor_reduce(sm4[:, :], e_in, AX_X, ALU.add).then_inc(sk_summed, 1)
                        dve.wait_ge(sk_ln, 2 * it + r + 1)
                        nc.vector.tensor_tensor(mine[:, :], lns[:, :], mx4[:, :], ALU.add).then_inc(sk_state, 1)
                        dve.wait_ge(sk_state, done + 3)
                        nc.vector.tensor_scalar(mine[:, :], mine[:, :], -1.0, None, ALU.mult).then_inc(sk_state, 1)
                dve.wait_ge(sk_state, 8 * SINK + 1)
                nc.vector.tensor_tensor(t_in, rows_of(zz, "i j"), inner(vv), ALU.add).then_inc(sk_state, 1)
                dve.wait_ge(sk_state, 8 * SINK + 2)
                nc.vector.tensor_tensor(t_in, t_in, outer(uu), ALU.add).then_inc(sk_shifted, 1)
                dve.wait_ge(sk_exp, 2 * SINK + 1)
            step(nc.vector.tensor_scalar(half_sb[:, :], half_sb[:, :], 1.0, None, ALU.add))
            step(nc.vector.reciprocal(gate_sb[:, :], half_sb[:, :]))
            step(nc.vector.tensor_tensor(hres[:, :], hres[:, :], eye_sb[:, :], ALU.subtract))
            step(nc.vector.scalar_tensor_tensor(out=hres[:, :], in0=hres[:, :], scalar=gate_sb[:, :], in1=eye_sb[:, :],
                                                op0=ALU.mult, op1=ALU.add))
            for i in range(NS):
                o = ob[:, i * P:(i + 1) * P]
                step(nc.vector.scalar_tensor_tensor(out=o, in0=ybr[:, :], scalar=hp[:, 4 + i:5 + i],
                                                    in1=x2[:, i * P:(i + 1) * P], op0=ALU.mult, op1=ALU.add))
                for j in range(NS):
                    step(nc.vector.scalar_tensor_tensor(out=o, in0=xf[:, j * P:(j + 1) * P],
                                                        scalar=hres[:, NS * i + j:NS * i + j + 1],
                                                        in1=o, op0=ALU.mult, op1=ALU.add))
            assert count[0] == DVE_END, (count[0], DVE_END)


def rope_tables():
    import numpy as np
    inv = (np.float32(1.0) / np.power(np.float32(10000.0), np.arange(0, DH, 2, dtype=np.float32) / np.float32(DH))).astype(np.float32)
    ang = (np.arange(KEYS, dtype=np.float32)[:, None] * inv[None, :]).astype(np.float64)
    return np.cos(ang).astype(np.float32), np.sin(ang).astype(np.float32)


def kernel(x, ctx_4096, mask_BxSxS2_ff0, L0_xattn_wq, L0_xattn_wk, L0_xattn_wv, L0_xattn_wo, L0_attn_w1, L0_attn_w2,
           L0_attn_b2, L0_attn_sparse_mask, L0_ffn_W_res, L0_ffn_W_pre, L0_ffn_W_post, L0_ffn_H_res_base,
           L0_ffn_H_pre_base, L0_ffn_H_post_base, L0_ffn_gate, L0_ffn_W_branch):
    import numpy as np
    import concourse.bacc as bacc
    from concourse.bass_utils import run_bass_kernel_spmd

    cos, sin = rope_tables()
    rows = lambda a, n: np.broadcast_to(np.asarray(a).reshape(1, -1), (n, np.asarray(a).size))
    arrays = {
        "x": np.asarray(x)[0],
        "ctxT": np.asarray(ctx_4096)[0].T,
        "mask": np.asarray(mask_BxSxS2_ff0)[0],
        "wq": L0_xattn_wq, "wk": L0_xattn_wk, "wv": L0_xattn_wv, "wo": L0_xattn_wo,
        "w1": L0_attn_w1, "w2t": np.asarray(L0_attn_w2).T, "b2": rows(L0_attn_b2, TOK), "smask": L0_attn_sparse_mask,
        "wffn": np.concatenate([np.asarray(L0_ffn_W_res), np.asarray(L0_ffn_W_pre), np.asarray(L0_ffn_W_post)]).T,
        "hbase": rows(np.concatenate([np.asarray(L0_ffn_H_res_base).ravel(), np.asarray(L0_ffn_H_pre_base),
                                      np.asarray(L0_ffn_H_post_base)]), TOK),
        "gate": rows(L0_ffn_gate, TOK), "wbranch": L0_ffn_W_branch,
        "ident": np.eye(P, dtype=np.float32), "eye": rows(np.eye(NS, dtype=np.float32), TOK),
        "cosT": np.concatenate([cos.T, cos.T]), "sinT": np.concatenate([sin.T, -sin.T]),
        "qrope": np.stack([np.concatenate([cos.T, cos.T])[:, :TOK], np.concatenate([sin.T, -sin.T])[:, :TOK]],
                          axis=1) * np.float32(SCALE),
    }
    arrays = {k: np.ascontiguousarray(v) for k, v in arrays.items()}
    nc = bacc.Bacc("TRN2", target_bir_lowering=False, num_devices=1, dynamic_dma_scratch_size=4096)
    A = {k: nc.dram_tensor(f"in_{k}", v.shape, mybir.dt.from_np(v.dtype), kind="ExternalInput").ap()
         for k, v in arrays.items()}
    A["out"] = nc.dram_tensor("out_x", (TOK, D), F32, kind="ExternalOutput").ap()
    perceiver(nc, A)
    r = run_bass_kernel_spmd(nc, [{f"in_{k}": v for k, v in arrays.items()}], core_ids=[0])
    return r.results[0]["out_x"].reshape(1, TOK, D)
```

```python
from contextlib import ExitStack

import concourse.bass as bass
from concourse import mybir

F32 = mybir.dt.float32
F32R = mybir.dt.float32r
ALU = mybir.AluOpType
ACT = mybir.ActivationFunctionType
AX_X = mybir.AxisListType.X

P = 128
D = 512
DC = D // P
TOK = 64
KEYS = 6272
HQ, HKV, DH = 32, 8, 128
HALF = DH // 2
KT = 7
BK = KT * P
NB = KEYS // BK
HB = BK // 2
UNITS = HKV // 2
QC = HQ // HKV * TOK
PIECES = 4
SCALE = float(DH) ** -0.5
EPS = 1e-5
RMS_EPS = 1.1920929e-07
NS = 4
SINK = 50
INV_TAU = 10.0
SINK_UNROLL = 7
assert (SINK - 1) % SINK_UNROLL == 0
SPREAD_MAX = 64.0
SPREAD_FLOOR = 80.0
assert NB * BK == KEYS and UNITS == 4


def piece_tiles(p):
    return range(2 * p, min(2 * p + 2, KT))


SC = 2 * DH
STAGED = [p for k in range(HKV) for p in (("wv" if k % 2 else "wk", k // 2), ("wq", 2 * k), ("wq", 2 * k + 1))]


def place_of(n):
    return n if n < 6 else 6 + (n - 6) % 3


def turn_of(n):
    return 1 if n < 6 else (n - 6) // 3 + 1


def halves():
    return slice(0, D // 2), slice(D // 2, D)


def need(eng, sem, value):
    if isinstance(value, int) and value <= 0:
        return
    eng.wait_ge(sem, value)


def perceiver(nc, A):
    with ExitStack() as ctx:
        def sb(name, shape, dt=F32):
            return ctx.enter_context(nc.sbuf_tensor(name, shape, dt))

        def ps(name, shape):
            return ctx.enter_context(nc.psum_tensor(name, shape, F32))

        def sem(name):
            return ctx.enter_context(nc.semaphore(name))

        base = -(-nc.sbuf_base // 32) * 32
        at = [base]

        def region(nbytes):
            here = at[0]
            at[0] += nbytes
            return here

        def place(name, shape, dt, where):
            return nc.alloc_sbuf_tensor_at(name, shape, dt, offset=where)

        R_WK_HI, R_WK_LO, R_WV_HI, R_WV_LO = (region(4 * DC * HKV * DH) for _ in range(4))
        R_CT_HI, R_CT_LO = (region(4 * DC * BK) for _ in range(2))
        R_V = region(4 * 2 * KT * 2 * DH)
        R_S = region(4 * 4 * BK)
        R_PT = region(4 * 2 * 2 * 2 * QC)
        R_ACC = region(4 * HKV * QC)
        R_RAW = region(4 * KT * DC * P)
        arena = sb("arena", [P, (at[0] - base) // 4 + 16])
        assert arena is not None

        wk_hi = place("wk_hi", [P, DC, HKV * DH], F32R, R_WK_HI)
        wk_lo = place("wk_lo", [P, DC, HKV * DH], F32R, R_WK_LO)
        wv_hi = place("wv_hi", [P, DC, HKV * DH], F32R, R_WV_HI)
        wv_lo = place("wv_lo", [P, DC, HKV * DH], F32R, R_WV_LO)
        ct_hi = place("ct_hi", [P, DC, BK], F32R, R_CT_HI)
        ct_lo = place("ct_lo", [P, DC, BK], F32R, R_CT_LO)
        v_hi = place("v_hi", [P, KT, 2 * DH], F32R, R_V)
        v_lo = place("v_lo", [P, KT, 2 * DH], F32R, R_V + 4 * KT * 2 * DH)
        scores = place("scores", [P, 4, BK], F32, R_S)
        pt_hi = place("pt_hi", [P, 2, 2, QC], F32R, R_PT)
        pt_lo = place("pt_lo", [P, 2, 2, QC], F32R, R_PT + 4 * 2 * 2 * QC)
        acc = place("acc", [P, HKV, QC], F32, R_ACC)
        ctx_raw = place("ctx_raw", [P, KT, DC, P], F32, R_RAW)
        STAGE_AT = [R_V, R_V + 4096, R_V + 8192, R_PT, R_PT + 4096, R_S + 4 * 2 * BK, R_RAW, R_RAW + 4096, R_RAW + 8192]
        stage = [place(f"stage{i}", [P, DC, SC], F32, a) for i, a in enumerate(STAGE_AT)]
        w1_sb = place("w1_sb", [P, DC, D], F32, R_WK_HI)
        w2t_sb = place("w2t_sb", [P, DC, D], F32, R_WK_HI + 4 * DC * D)
        smask_sb = place("smask_sb", [P, DC, D], F32, R_WK_LO)
        mixw = place("mixw", [P, DC, D], F32, R_WK_LO + 4 * DC * D)
        wo_v = [place("wo_v_hi", [P, DC, 2, D], F32, R_WV_HI), place("wo_v_lo", [P, DC, 2, D], F32, R_WV_LO)]
        wo_part = [place("wo_raw", [P, 7, D], F32, R_RAW)[:, :, :]]
        wo_part += [wo_v[k][:, :, half, :] for half in range(2) for k in range(2)]
        wo_part += [place("wo_ct", [P, 9, D], F32, R_CT_HI)[:, :, :]]
        WO_FIRST = [0, 7, 11, 15, 19, 23, 32]
        WO_PARTS = len(wo_part)
        assert R_CT_LO == R_CT_HI + 4 * 7 * D

        kt_hi = sb("kt_hi", [P, 2, BK], F32R)
        kt_lo = sb("kt_lo", [P, 2, BK], F32R)
        qt_hi = sb("qt_hi", [P, HQ * TOK], F32R)
        qt_lo = sb("qt_lo", [P, HQ * TOK], F32R)
        mask_sb = sb("mask_sb", [P, BK])
        cos_sb = sb("cos_sb", [P, BK])
        sin_sb = sb("sin_sb", [P, BK])
        rc = sb("rc", [P, 2, HB])
        rs = sb("rs", [P, 2, HB])
        rq = sb("rq", [P, QC])
        rqs = sb("rqs", [P, QC])
        ident = sb("ident", [P, P])
        x_sb = sb("x_sb", [TOK, D])
        xn = sb("xn", [TOK, D])
        xnT = sb("xnT", [P, DC, TOK])
        qtab = sb("qtab", [P, 2, TOK])
        bnst = sb("bnst", [TOK, 2, 6])
        mv = sb("mv", [TOK, 4])
        m_run = sb("m_run", [P, 16])
        m_old = sb("m_old", [P, 16])
        m_neg = sb("m_neg", [P, 16])
        m_drop = sb("m_drop", [P, 16])
        fac = sb("fac", [P, 16])
        rsum = sb("rsum", [P, 16])
        l_run = sb("l_run", [P, 16])
        l_inv = sb("l_inv", [P, 16])
        b2_sb = sb("b2_sb", [TOK, D])
        wf_sb = sb("wf_sb", [P, DC, 24])
        hb_sb = sb("hb_sb", [TOK, 24])
        gate_sb = sb("gate_sb", [TOK, 1])
        wb_sb = sb("wb_sb", [P, P])
        lg = sb("lg", [TOK, 24])
        zz = sb("zz", [TOK, 16])
        tt = sb("tt", [TOK, 16])
        ee = sb("ee", [TOK, 16])
        uu = sb("uu", [TOK, 4])
        vv = sb("vv", [TOK, 4])
        mx6 = sb("mx6", [TOK, 6])
        mx4 = sb("mx4", [TOK, 4])
        sm4 = sb("sm4", [TOK, 4])
        lns = sb("lns", [TOK, 4])
        sh = sb("sh", [TOK, 24])
        hp = sb("hp", [TOK, 8])
        hres = sb("hres", [TOK, 16])
        hsum = sb("hsum", [TOK, 4])
        kk = sb("kk", [TOK, 16])
        hg = sb("hg", [TOK, 16])
        gg = sb("gg", [TOK, 4])
        zlim = sb("zlim", [TOK, 4])
        sums = sb("sums", [TOK, NS])
        wide = sb("wide", [1, 2])
        wide_flag = sb("wide_flag", [1, 1], mybir.dt.int32)
        x1 = place("x1", [TOK, D], F32, R_S)
        x2 = place("x2", [TOK, D], F32, R_S + 2048)
        xf = place("xf", [TOK, D], F32, R_S + 4096)
        t0 = place("t0", [TOK, D], F32, R_S + 6144)
        ob = place("ob", [TOK, D], F32, R_S + 8192)
        xpre = place("xpre", [TOK, P], F32, R_S + 10240)
        ybr = place("ybr", [TOK, P], F32, R_S + 10752)
        xpT = place("xpT", [P, TOK], F32, R_S + 11264)
        t1 = place("t1", [TOK, D], F32, R_S + 11520)

        p_s = ps("p_s", [P, 2, 512])
        p_t = [ps(f"p_t{i}", [P, 512]) for i in range(2)]
        p_kv = [ps(f"p_kv{i}", [P, 512]) for i in range(2)]
        p_o = ps("p_o", [P, 512])
        p_f = ps("p_f", [P, 512])

        x_loaded = sem("x_loaded")
        ident_loaded = sem("ident_loaded")
        qtab_loaded = sem("qtab_loaded")
        tail_loaded = sem("tail_loaded")
        stage_loaded = [sem(f"stage_loaded{i}") for i in range(len(STAGE_AT))]
        ctx_loaded = [sem(f"ctx_loaded{t}") for t in range(KT)]
        rope_loaded = sem("rope_loaded")
        mask_loaded = sem("mask_loaded")
        w12_loaded = sem("w12_loaded")
        smask_loaded = sem("smask_loaded")
        wo_loaded = [sem(f"wo_loaded{i}") for i in range(WO_PARTS)]
        w_hi_ready = sem("w_hi_ready")
        w_lo_ready = sem("w_lo_ready")
        ctx_hi_ready = sem("ctx_hi_ready")
        ctx_lo_ready = sem("ctx_lo_ready")
        q_projected = sem("q_projected")
        q_products = sem("q_products")
        q_rotated = sem("q_rotated")
        q_hi_ready = sem("q_hi_ready")
        q_lo_ready = sem("q_lo_ready")
        k_projected = sem("k_projected")
        v_projected = sem("v_projected")
        k_products = sem("k_products")
        k_rotated = sem("k_rotated")
        k_hi_ready = sem("k_hi_ready")
        k_lo_ready = sem("k_lo_ready")
        v_hi_ready = sem("v_hi_ready")
        v_lo_ready = sem("v_lo_ready")
        scores_ready = sem("scores_ready")
        scores_masked = sem("scores_masked")
        max_negated = sem("max_negated")
        max_dropped = sem("max_dropped")
        max_kept = sem("max_kept")
        factor_ready = sem("factor_ready")
        probs_ready = sem("probs_ready")
        sums_kept = sem("sums_kept")
        probs_transposed = sem("probs_transposed")
        pt_hi_ready = sem("pt_hi_ready")
        pt_lo_ready = sem("pt_lo_ready")
        pv_done = sem("pv_done")
        factor_spread = sem("factor_spread")
        acc_scaled = sem("acc_scaled")
        acc_added = sem("acc_added")
        acc_cleared = sem("acc_cleared")
        dve_step = sem("dve_step")
        act_step = sem("act_step")
        pool_step = sem("pool_step")
        pe_step = sem("pe_step")
        out_stored = sem("out_stored")

        sk_shifted = sem("sk_shifted")
        sk_exp = sem("sk_exp")
        sk_summed = sem("sk_summed")
        sk_ln = sem("sk_ln")
        sk_state = sem("sk_state")
        sk_linear = sem("sk_linear")
        inv_spread = sem("inv_spread")
        acc_normal = sem("acc_normal")

        PE_XNT = 1
        PE_Y, PE_X1T, PE_Z, PE_XNT3, PE_LOGITS, PE_WIDE, PE_XPT, PE_BR = 6, 8, 9, 11, 12, 13, 14, 15
        DVE_VAR, DVE_XN, DVE_XNT = 4, 5, 6
        DVE_MIX = DVE_XNT + 2
        DVE_LINV = DVE_MIX + 4 + 1
        DVE_VAR2, DVE_XN2, DVE_XNT2 = DVE_LINV + 6, DVE_LINV + 7, DVE_LINV + 8
        DVE_Z = DVE_XNT2 + 1
        DVE_VAR3, DVE_XF = DVE_Z + 1 + 6, DVE_Z + 1 + 7
        DVE_SQ, DVE_XNT3, DVE_MS = DVE_XF + 1, DVE_XF + 2, DVE_XF + 3
        DVE_GATE = DVE_MS + 3
        DVE_LG = DVE_GATE + 1
        DVE_SHIFT = DVE_LG + 3
        DVE_SPREAD = DVE_SHIFT + 3
        DVE_HP = DVE_SPREAD + 3
        DVE_FLAG = DVE_HP + 2
        DVE_HG = DVE_FLAG + 1
        DVE_END = DVE_HG + 3 * NS
        ACT_GELU, ACT_GATE, ACT_K, ACT_HP, ACT_XPT, ACT_YBR = 1, 3, 4, 5, 6, 7
        POOL_RSTD1, POOL_RSTD2, POOL_RSTD3, POOL_RRMS, POOL_XPRE, POOL_BASE, POOL_END = 2, 3, 4, 5, 8, 12, 16

        block = ctx.enter_context(nc.Block())

        @block.sync
        def _(sp):
            def load_stage(n):
                kind, i = STAGED[n]
                k, r = divmod(n, 3)
                if 6 <= n < 9:
                    sp.wait_ge(ctx_hi_ready, KT)
                    sp.wait_ge(ctx_lo_ready, KT)
                elif n >= 9 and r == 0:
                    sp.wait_ge(w_hi_ready, k)
                    sp.wait_ge(w_lo_ready, k)
                elif n >= 9:
                    sp.wait_ge(q_projected, 2 * (k - 1) + r)
                sp.dma_start(stage[place_of(n)][:, :, :],
                             A[kind][:, i * SC:(i + 1) * SC].rearrange("(c p) n -> p c n", p=P)
                             ).then_inc(stage_loaded[place_of(n)], 16)

            def load_rope(b):
                need(sp, k_products, 16 * b)
                sp.dma_start(cos_sb[:, :], A["cosT"][:, bass.ds(b * BK, BK)]).then_inc(rope_loaded, 16)
                sp.dma_start(sin_sb[:, :], A["sinT"][:, bass.ds(b * BK, BK)]).then_inc(rope_loaded, 16)

            def load_ctx(b, t):
                need(sp, ctx_hi_ready, KT * (b - 1) + t + 1)
                need(sp, ctx_lo_ready, KT * (b - 1) + t + 1)
                sp.dma_start(ctx_raw[:, t, :, :],
                             A["ctxT"][:, bass.ds(b * BK + t * P, P)].rearrange("(c p) n -> p c n", p=P)
                             ).then_inc(ctx_loaded[t], 16)

            def load_mask(b):
                need(sp, scores_masked, 16 * b)
                for h in range(2):
                    sp.dma_start(mask_sb[h * TOK:(h + 1) * TOK, :], A["mask"][:, bass.ds(b * BK, BK)]
                                 ).then_inc(mask_loaded, 16)

            sp.dma_start(x_sb[:, :], A["x"]).then_inc(x_loaded, 16)
            sp.dma_start(ident[:, :], A["ident"]).then_inc(ident_loaded, 16)
            load_stage(0)
            load_ctx(0, 0)
            load_ctx(0, 1)
            load_ctx(0, 2)
            load_ctx(0, 3)
            load_rope(0)
            for t in range(4, KT):
                load_ctx(0, t)
            sp.dma_start(qtab[:, :, :], A["qrope"]).then_inc(qtab_loaded, 16)
            load_stage(3)
            load_stage(1)
            load_stage(2)
            load_mask(0)
            for n in range(4, len(STAGED)):
                load_stage(n)
            for dst, src in ((b2_sb, "b2"), (hb_sb, "hbase"), (gate_sb, "gate"), (wb_sb, "wbranch")):
                sp.dma_start(dst[:, :], A[src]).then_inc(tail_loaded, 16)
            sp.dma_start(wf_sb[:, :, :], A["wffn"].rearrange("(c p) n -> p c n", p=P)).then_inc(tail_loaded, 16)
            load_rope(1)
            load_ctx(1, 6)
            sp.wait_ge(w_hi_ready, HKV)
            sp.wait_ge(w_lo_ready, HKV)
            for t in range(2):
                load_ctx(1, t)
            sp.wait_ge(q_projected, 2 * HKV)
            for t in range(2, 6):
                load_ctx(1, t)
            load_mask(1)

            with sp.Fori(2, NB) as b:
                load_rope(b)
                for t in range(KT):
                    load_ctx(b, t)
                load_mask(b)

            def load_wo(i):
                a, z = WO_FIRST[i], WO_FIRST[i + 1]
                sp.dma_start(wo_part[i], A["wo"][a * P:z * P, :].rearrange("(h p) n -> p h n", p=P)
                             ).then_inc(wo_loaded[i], 16)

            sp.wait_ge(ctx_hi_ready, KT * NB)
            sp.wait_ge(ctx_lo_ready, KT * NB)
            load_wo(0)
            sp.wait_ge(v_projected, 16 * NB - 4)
            load_wo(1)
            load_wo(2)
            sp.wait_ge(k_projected, 16 * NB)
            sp.dma_start(w1_sb[:, :, :], A["w1"].rearrange("(c p) n -> p c n", p=P)).then_inc(w12_loaded, 16)
            sp.dma_start(w2t_sb[:, :, :], A["w2t"].rearrange("(c p) n -> p c n", p=P)).then_inc(w12_loaded, 16)
            sp.dma_start(smask_sb[:, :, :], A["smask"].rearrange("(c p) n -> p c n", p=P)).then_inc(smask_loaded, 16)
            sp.wait_ge(v_projected, 16 * NB)
            for i in range(3, WO_PARTS):
                load_wo(i)
            sp.wait_ge(pool_step, POOL_END)
            sp.wait_ge(dve_step, DVE_END)
            sp.dma_start(A["out"], ob[:, :]).then_inc(out_stored, 16)
            sp.wait_ge(out_stored, 16)

        def split_matmul(out, w_hi, w_lo, x_hi, x_lo, start, stop):
            nc.tensor.matmul(out, w_hi, x_hi, start=start, stop=False)
            nc.tensor.matmul(out, w_hi, x_lo, start=False, stop=False)
            return nc.tensor.matmul(out, w_lo, x_hi, start=False, stop=stop)

        def pe_project_k(pe, b, g, i):
            u = UNITS * b + g
            head, half = 2 * g + i // 2, i % 2
            if i >= 2:
                need(pe, k_products, 4 * u + i - 1)
            else:
                need(pe, v_lo_ready, 4 * (u - 1) + i + 3)
            if i < 2 and g == 0:
                tiles = KT * b + (i + 1) * KT // 2 + 1 - i
                pe.wait_ge(ctx_hi_ready, tiles)
                pe.wait_ge(ctx_lo_ready, tiles)
            if i == 0 and isinstance(b, int) and b == 0:
                pe.wait_ge(w_lo_ready, 2 * g + 1)
            cols = slice(half * HB, (half + 1) * HB)
            for c in range(DC):
                w = slice(head * DH, (head + 1) * DH)
                last = split_matmul(p_kv[i % 2][:, 0:HB], wk_hi[:, c, w], wk_lo[:, c, w],
                                    ct_hi[:, c, cols], ct_lo[:, c, cols], c == 0, c == DC - 1)
            last.then_inc(k_projected, 1)

        def pe_project_v(pe, b, g, i):
            u = UNITS * b + g
            if i >= 2:
                need(pe, v_lo_ready, 4 * u + i - 1)
            else:
                need(pe, k_products, 4 * u + i + 3)
            if i == 0 and isinstance(b, int) and b == 0:
                pe.wait_ge(w_lo_ready, 2 * g + 2)
            for j, t in enumerate(piece_tiles(i)):
                for c in range(DC):
                    k = slice(t * P, (t + 1) * P)
                    w = slice(g * 2 * DH, (g + 1) * 2 * DH)
                    last = split_matmul(p_kv[i % 2][:, j * 2 * DH:(j + 1) * 2 * DH], ct_hi[:, c, k], ct_lo[:, c, k],
                                        wv_hi[:, c, w], wv_lo[:, c, w], c == 0, c == DC - 1)
            last.then_inc(v_projected, 1)

        def pe_project_q(pe, k):
            need(pe, q_products, k)
            for r in range(2):
                n = 3 * k + 1 + r
                pe.wait_ge(stage_loaded[place_of(n)], 16 * turn_of(n))
                for j in range(2):
                    for c in range(DC):
                        last = nc.tensor.matmul(p_f[:, QC + (2 * r + j) * TOK:QC + (2 * r + j + 1) * TOK],
                                                stage[place_of(n)][:, c, j * DH:(j + 1) * DH], xnT[:, c, :],
                                                start=(c == 0), stop=(c == DC - 1))
                last.then_inc(q_projected, 1)

        def pe_scores(pe, b, g, s, i):
            u = UNITS * b + g
            h = 2 * u + s
            if i == 0:
                pe.wait_ge(k_lo_ready, 4 * u + 2 * s + 2)
                if isinstance(b, int) and b == 0:
                    pe.wait_ge(q_lo_ready, 2 * g + s + 1)
            need(pe, scores_masked, 2 * h + i)
            q = slice((2 * g + s) * QC + i * P, (2 * g + s) * QC + (i + 1) * P)
            for f in range(2):
                k = slice(f * HB, (f + 1) * HB)
                last = split_matmul(p_s[:, f, 0:HB], qt_hi[:, q], qt_lo[:, q], kt_hi[:, s, k], kt_lo[:, s, k], True, True)
            last.then_inc(scores_ready, 1)

        def pe_spread(pe, h, s, g, src):
            for i in range(2):
                col = 2 * (2 * g + s) + i
                last = nc.tensor.transpose(p_f[:, i * P:(i + 1) * P], src[:, col:col + 1].to_broadcast([P, P]), ident[:, :])
            last.then_inc(factor_spread, 1)

        def pe_transpose_probs(pe, h, s, p):
            if p == 0:
                pe.wait_ge(probs_ready, 2 * h + 2)
            need(pe, pt_lo_ready, 4 * h + p - 1)
            for j, t in enumerate(piece_tiles(p)):
                for i in range(2):
                    last = nc.tensor.transpose(p_t[p % 2][:, j * QC + i * P:j * QC + (i + 1) * P],
                                               scores[:, 2 * s + i, t * P:(t + 1) * P], ident[:, :])
            last.then_inc(probs_transposed, 1)

        def pe_pv(pe, h, s, p, v_count):
            pe.wait_ge(pt_lo_ready, 4 * h + p + 1)
            if p == 0:
                need(pe, acc_added, h)
            pe.wait_ge(v_lo_ready, v_count + p + 1)
            for j, t in enumerate(piece_tiles(p)):
                w = slice(s * DH, (s + 1) * DH)
                last = split_matmul(p_o[:, 0:QC], v_hi[:, t, w], v_lo[:, t, w], pt_hi[:, p % 2, j, :], pt_lo[:, p % 2, j, :],
                                    t == 0, t == KT - 1)
            last.then_inc(pv_done, 1)

        def pe_slot(pe, b, g, s, prev=True, last=False):
            u = UNITS * b + g
            h = 2 * u + s
            pg, psn = (g, 0) if s else ((g - 1) % UNITS, 1)
            v_count = 4 * u if s else 4 * (u - 1)

            def fill(i):
                if s == 0:
                    pe_project_v(pe, b, g, i)
                elif g < UNITS - 1:
                    pe_project_k(pe, b, g + 1, i)
                elif not last:
                    pe_project_k(pe, b + 1, 0, i)
                else:
                    pe_mix(pe, i)

            if prev:
                pe_transpose_probs(pe, h - 1, psn, 0)
                pe.wait_ge(factor_ready, 2 * h)
                need(pe, acc_scaled, h - 1)
                if isinstance(b, int) and b == 0:
                    pe.wait_ge(q_products, h + 1)
                pe_spread(pe, h - 1, psn, pg, fac)
            pe_scores(pe, b, g, s, 0)
            if prev:
                pe_transpose_probs(pe, h - 1, psn, 1)
                pe_pv(pe, h - 1, psn, 0, v_count)
            fill(0)
            if isinstance(b, int) and b == 0 and h < HKV - 1:
                need(pe, acc_scaled, h)
                pe_project_q(pe, h + 1)
            pe_scores(pe, b, g, s, 1)
            if prev:
                pe_transpose_probs(pe, h - 1, psn, 2)
                pe_pv(pe, h - 1, psn, 1, v_count)
            fill(1)
            if prev:
                pe_transpose_probs(pe, h - 1, psn, 3)
                pe_pv(pe, h - 1, psn, 2, v_count)
            fill(2)
            if prev:
                pe_pv(pe, h - 1, psn, 3, v_count)
            fill(3)

        def pe_mix(pe, i):
            if i == 0:
                pe.wait_ge(w12_loaded, 32)
            if i < 2:
                pe.wait_ge(v_lo_ready, 16 * NB)
            else:
                pe.wait_ge(dve_step, DVE_MIX + i - 1)
            for c in range(DC):
                last = nc.tensor.matmul(p_kv[i % 2][:, :], w1_sb[:, c, i * P:(i + 1) * P], w2t_sb[:, c, :],
                                        start=(c == 0), stop=(c == DC - 1))
            last.then_inc(pe_step, 1)

        @block.tensor
        def _(pe):
            def keep_awake(n):
                for _ in range(n):
                    nc.tensor.transpose(p_s[:, 0, 0:P], ident[:, :], ident[:, :])

            pe.wait_ge(ident_loaded, 16)
            pe.wait_ge(dve_step, DVE_XN)
            for c in range(DC):
                last = nc.tensor.transpose(p_o[:, c * TOK:(c + 1) * TOK], xn[:, c * P:(c + 1) * P], ident[0:TOK, 0:TOK])
            last.then_inc(pe_step, 1)
            for i in range(2):
                pe_project_k(pe, 0, 0, i)
            pe.wait_ge(dve_step, DVE_XNT)
            pe_project_q(pe, 0)
            for i in range(2, 4):
                pe_project_k(pe, 0, 0, i)

            def pe_block(b, first=False, last=False):
                for g in range(UNITS):
                    for s in range(2):
                        pe_slot(pe, b, g, s, prev=not (first and g == 0 and s == 0), last=last)

            pe_block(0, first=True)
            with pe.Fori(1, NB - 1) as b:
                pe_block(b)
            pe_block(NB - 1, last=True)
            def inv_spread_pair(k):
                if k < 2:
                    pe.wait_ge(dve_step, DVE_LINV)
                    pe.wait_ge(scores_masked, 16 * NB)
                else:
                    pe.wait_ge(acc_normal, k - 1)
                for i in range(4):
                    col = 4 * k + i
                    last = nc.tensor.transpose(p_s[:, k % 2, i * P:(i + 1) * P],
                                               l_inv[:, col:col + 1].to_broadcast([P, P]), ident[:, :])
                last.then_inc(inv_spread, 1)

            def project_out(first, end, which=(0, 1)):
                for hq in range(first, end):
                    i = max(j for j in range(WO_PARTS) if WO_FIRST[j] <= hq)
                    if hq == 0:
                        pe.wait_ge(dve_step, DVE_MIX + 4)
                    if hq == WO_FIRST[i]:
                        pe.wait_ge(wo_loaded[i], 16)
                    if hq % 8 == 0:
                        pe.wait_ge(acc_normal, hq // 8 + 1)
                    for k in which:
                        last = nc.tensor.matmul(p_kv[k][0:TOK, 0:D // 2], acc[:, hq // 4, (hq % 4) * TOK:(hq % 4 + 1) * TOK],
                                                wo_part[i][:, hq - WO_FIRST[i], halves()[k]], start=(hq == 0),
                                                stop=(hq == HQ - 1))
                return last

            h = 8 * NB - 1
            v_count = 16 * NB - 4
            pe_transpose_probs(pe, h, 1, 0)
            pe.wait_ge(factor_ready, 2 * h + 2)
            pe.wait_ge(acc_scaled, h)
            pe_spread(pe, h, 1, UNITS - 1, fac)
            pe_transpose_probs(pe, h, 1, 1)
            inv_spread_pair(0)
            inv_spread_pair(1)
            pe_pv(pe, h, 1, 0, v_count)
            pe_transpose_probs(pe, h, 1, 2)
            project_out(0, 2)
            pe_pv(pe, h, 1, 1, v_count)
            pe_transpose_probs(pe, h, 1, 3)
            project_out(2, 4)
            pe_pv(pe, h, 1, 2, v_count)
            pe_pv(pe, h, 1, 3, v_count)
            inv_spread_pair(2)
            project_out(4, 8)
            inv_spread_pair(3)
            project_out(8, 24)
            for k in range(2):
                project_out(24, HQ, (k,)).then_inc(pe_step, 1)
            keep_awake(20)

            def transpose_rows(src):
                for c in range(DC):
                    last = nc.tensor.transpose(p_f[:, c * TOK:(c + 1) * TOK], src[:, c * P:(c + 1) * P], ident[0:TOK, 0:TOK])
                last.then_inc(pe_step, 1)

            pe.wait_ge(dve_step, DVE_XN2)
            transpose_rows(xn)
            keep_awake(4)
            pe.wait_ge(dve_step, DVE_XNT2)
            for bank, half in zip((p_o, p_t[1]), halves()):
                for c in range(DC):
                    last = nc.tensor.matmul(bank[0:TOK, 0:D // 2], xnT[:, c, :], mixw[:, c, half], start=(c == 0),
                                            stop=(c == DC - 1))
                last.then_inc(pe_step, 1)
            pe.wait_ge(dve_step, DVE_XF)
            transpose_rows(xf)
            pe.wait_ge(dve_step, DVE_XNT3)
            pe.wait_ge(tail_loaded, 80)
            for c in range(DC):
                last = nc.tensor.matmul(p_o[0:TOK, 0:24], xnT[:, c, :], wf_sb[:, c, :], start=(c == 0), stop=(c == DC - 1))
            last.then_inc(pe_step, 1)
            pe.wait_ge(dve_step, DVE_SPREAD)
            nc.tensor.transpose(p_t[0][0:1, 0:TOK], zlim[:, 2:3], ident[0:TOK, 0:TOK]).then_inc(pe_step, 1)
            pe.wait_ge(pool_step, POOL_XPRE)
            nc.tensor.transpose(p_f[:, 0:TOK], xpre[:, :], ident[0:TOK, 0:TOK]).then_inc(pe_step, 1)
            pe.wait_ge(act_step, ACT_XPT)
            nc.tensor.matmul(p_t[1][0:TOK, 0:P], xpT[:, :], wb_sb[:, :], start=True, stop=True).then_inc(pe_step, 1)

        def act_v_hi(act, b, g, i):
            u = UNITS * b + g
            act.wait_ge(v_projected, 4 * u + i + 1)
            need(act, pv_done, 4 * (2 * u - 1) + i + 1)
            n = len(piece_tiles(i)) * 2 * DH
            nc.scalar.activation(v_hi[:, 2 * i:2 * i + len(piece_tiles(i)), :].rearrange("p t n -> p (t n)"),
                                 p_kv[i % 2][:, 0:n], ACT.Copy).then_inc(v_hi_ready, 1)

        def act_k_hi(act, b, g, i):
            u = UNITS * b + g
            act.wait_ge(k_rotated, 4 * u + i + 1)
            f = i % 2
            nc.scalar.activation(kt_hi[:, i // 2, f * HB:(f + 1) * HB], rc[:, i % 2, 0:HB], ACT.Copy).then_inc(k_hi_ready, 1)

        def act_pt_hi(act, h, p):
            act.wait_ge(probs_transposed, 4 * h + p + 1)
            need(act, pv_done, 4 * h + p - 1)
            n = len(piece_tiles(p)) * QC
            nc.scalar.activation(pt_hi[:, p % 2, :, :].rearrange("p t n -> p (t n)")[:, 0:n], p_t[p % 2][:, 0:n],
                                 ACT.Copy).then_inc(pt_hi_ready, 1)

        def act_exp(act, b, g, s, i):
            n = 2 * (2 * (UNITS * b + g) + s) + i
            col = 2 * (2 * g + s) + i
            act.wait_ge(max_dropped, n + 1)
            nc.scalar.activation(fac[:, col:col + 1], m_drop[:, col:col + 1], ACT.Exp).then_inc(factor_ready, 1)
            act.wait_ge(max_negated, n + 1)
            nc.scalar.activation(scores[:, 2 * s + i, :], scores[:, 2 * s + i, :], ACT.Exp, bias=m_neg[:, col:col + 1],
                                 accum_out=rsum[:, col:col + 1]).then_inc(probs_ready, 1)

        @block.scalar
        def _(act):
            def w_hi(k):
                n = 3 * k
                act.wait_ge(stage_loaded[place_of(n)], 16 * turn_of(n))
                dst = (wv_hi if k % 2 else wk_hi)[:, :, k // 2 * SC:(k // 2 + 1) * SC]
                nc.scalar.activation(dst, stage[place_of(n)][:, :, :], ACT.Copy).then_inc(w_hi_ready, 1)

            def ctx_hi(b, t):
                act.wait_ge(ctx_loaded[t], 16 * (b + 1))
                need(act, v_projected, 16 * (b - 1) + 13 + t // 2)
                nc.scalar.activation(ct_hi[:, :, t * P:(t + 1) * P], ctx_raw[:, t, :, :], ACT.Copy).then_inc(ctx_hi_ready, 1)

            def q_hi(k):
                act.wait_ge(q_rotated, k + 1)
                nc.scalar.activation(qt_hi[:, k * QC:(k + 1) * QC], rq[:, :], ACT.Copy).then_inc(q_hi_ready, 1)

            w_hi(0)
            for t in range(KT):
                ctx_hi(0, t)
            w_hi(1)
            for i in range(2):
                act_k_hi(act, 0, 0, i)
            q_hi(0)
            for i in range(2, 4):
                act_k_hi(act, 0, 0, i)

            def act_slot(b, g, s, prev=True, last=False):
                h = 2 * (UNITS * b + g) + s

                def keys(i):
                    if g < UNITS - 1:
                        act_k_hi(act, b, g + 1, i)
                    elif not last:
                        act_k_hi(act, b + 1, 0, i)

                def split_ctx(at, *tiles):
                    if (g, s) == (UNITS - 1, at) and not last:
                        for t in tiles:
                            ctx_hi(b + 1, t)

                if prev:
                    act_pt_hi(act, h - 1, 0)
                    if s == 0:
                        act_k_hi(act, b, g, 2)
                    act_pt_hi(act, h - 1, 1)
                split_ctx(1, 4, 5, 6)
                act_exp(act, b, g, s, 0)
                if isinstance(b, int) and b == 0 and h + 2 < HKV:
                    w_hi(h + 2)
                if s == 0:
                    act_v_hi(act, b, g, 0)
                if prev:
                    act_pt_hi(act, h - 1, 2)
                    if s == 0:
                        act_k_hi(act, b, g, 3)
                act_exp(act, b, g, s, 1)
                if s == 0:
                    act_v_hi(act, b, g, 1)
                    split_ctx(0, 0, 1)
                else:
                    keys(0)
                    if isinstance(b, int) and b == 0 and h + 1 < HKV:
                        q_hi(h + 1)
                if prev:
                    act_pt_hi(act, h - 1, 3)
                if s == 0:
                    if isinstance(b, int) and b == 0:
                        q_hi(h + 1)
                    act_v_hi(act, b, g, 2)
                    split_ctx(0, 2, 3)
                    act_v_hi(act, b, g, 3)
                else:
                    keys(1)

            def act_block(b, first=False, last=False):
                for g in range(UNITS):
                    for s in range(2):
                        act_slot(b, g, s, prev=not (first and g == 0 and s == 0), last=last)

            act_block(0, first=True)
            with act.Fori(1, NB - 1) as b:
                act_block(b)
            act_block(NB - 1, last=True)
            for p in range(PIECES):
                act_pt_hi(act, 8 * NB - 1, p)

            for k, half in enumerate(halves()):
                act.wait_ge(dve_step, DVE_Z + k)
                nc.scalar.activation(x2[:, half], t0[:, half], ACT.Gelu).then_inc(act_step, 1)
            act.wait_ge(tail_loaded, 80)
            nc.scalar.activation(gg[:, 0:1], gate_sb[:, :], ACT.Exp, scale=-1.0).then_inc(act_step, 1)
            act.wait_ge(dve_step, DVE_SHIFT)
            nc.scalar.activation(kk[:, :], sh[:, 0:16], ACT.Exp, scale=INV_TAU).then_inc(act_step, 1)
            nc.scalar.activation(hp[:, :], sh[:, 16:24], ACT.Exp).then_inc(act_step, 1)
            act.wait_ge(pe_step, PE_XPT)
            nc.scalar.activation(xpT[:, :], p_f[:, 0:TOK], ACT.Copy).then_inc(act_step, 1)
            act.wait_ge(pe_step, PE_BR)
            nc.scalar.activation(ybr[:, :], p_t[1][0:TOK, 0:P], ACT.Copy).then_inc(act_step, 1)
            act.wait_ge(dve_step, DVE_FLAG)
            again = act.value_load(wide_flag[0:1, 0:1])
            with act.If(again == 1):
                with act.Fori(0, SINK) as it:
                    for r in range(2):
                        act.wait_ge(sk_shifted, 2 * it + r + 1)
                        nc.scalar.activation(ee[:, :], tt[:, :], ACT.Exp).then_inc(sk_exp, 1)
                        act.wait_ge(sk_summed, 2 * it + r + 1)
                        nc.scalar.activation(lns[:, :], sm4[:, :], ACT.Ln).then_inc(sk_ln, 1)
                act.wait_ge(sk_shifted, 2 * SINK + 1)
                nc.scalar.activation(hres[:, :], tt[:, :], ACT.Exp).then_inc(sk_exp, 1)

        @block.gpsimd
        def _(pool):
            def w_lo(k):
                n = 3 * k
                cols = slice(k // 2 * SC, (k // 2 + 1) * SC)
                hi, lo = (wv_hi, wv_lo) if k % 2 else (wk_hi, wk_lo)
                pool.wait_ge(stage_loaded[place_of(n)], 16 * turn_of(n))
                pool.wait_ge(w_hi_ready, k + 1)
                nc.gpsimd.tensor_tensor(lo[:, :, cols], stage[place_of(n)][:, :, :], hi[:, :, cols].bitcast(F32),
                                        ALU.subtract).then_inc(w_lo_ready, 1)

            def rotate_q(k):
                pool.wait_ge(q_products, k + 1)
                nc.gpsimd.tensor_tensor(rq[:, :], rq[:, :], rqs[:, :], ALU.add).then_inc(q_rotated, 1)
                pool.wait_ge(q_rotated, k + 1)
                pool.wait_ge(q_hi_ready, k + 1)
                cols = slice(k * QC, (k + 1) * QC)
                nc.gpsimd.tensor_tensor(qt_lo[:, cols], rq[:, :], qt_hi[:, cols].bitcast(F32), ALU.subtract
                                        ).then_inc(q_lo_ready, 1)

            def rotate(b, g, i):
                u = UNITS * b + g
                pool.wait_ge(k_products, 4 * u + i + 1)
                nc.gpsimd.tensor_tensor(rc[:, i % 2, 0:HB], rc[:, i % 2, 0:HB], rs[:, i % 2, 0:HB], ALU.add
                                        ).then_inc(k_rotated, 1)
                pool.wait_ge(k_rotated, 4 * u + i + 1)
                pool.wait_ge(k_hi_ready, 4 * u + i + 1)
                f = slice((i % 2) * HB, (i % 2 + 1) * HB)
                nc.gpsimd.tensor_tensor(kt_lo[:, i // 2, f], rc[:, i % 2, 0:HB], kt_hi[:, i // 2, f].bitcast(F32),
                                        ALU.subtract).then_inc(k_lo_ready, 1)

            nc.gpsimd.memset(mv[:, 3:4], -0.5).then_inc(pool_step, 1)
            pool.wait_ge(pool_step, 1)
            pool.wait_ge(dve_step, DVE_VAR)
            nc.gpsimd.tensor_tensor(mv[:, 2:3], mv[:, 1:2], mv[:, 3:4], ALU.pow).then_inc(pool_step, 1)
            w_lo(0)
            rotate(0, 0, 0)
            rotate(0, 0, 1)
            rotate_q(0)
            w_lo(1)
            rotate(0, 0, 2)
            rotate(0, 0, 3)

            for g in range(UNITS):
                rotate_q(2 * g + 1)
                nb, ng = (0, g + 1) if g < UNITS - 1 else (1, 0)
                if g < UNITS - 1:
                    w_lo(2 * g + 2)
                rotate(nb, ng, 0)
                if g < UNITS - 1:
                    rotate_q(2 * g + 2)
                rotate(nb, ng, 1)
                if g < UNITS - 1:
                    w_lo(2 * g + 3)
                rotate(nb, ng, 2)
                rotate(nb, ng, 3)
            with pool.Fori(1, NB - 1) as b:
                for g in range(UNITS):
                    for i in range(4):
                        rotate(b + 1 if g == UNITS - 1 else b, (g + 1) % UNITS, i)
            for g in range(UNITS - 1):
                for i in range(4):
                    rotate(NB - 1, g + 1, i)
            for at in (DVE_VAR2, DVE_VAR3, DVE_MS):
                pool.wait_ge(dve_step, at)
                nc.gpsimd.tensor_tensor(mv[:, 2:3], mv[:, 1:2], mv[:, 3:4], ALU.pow).then_inc(pool_step, 1)

            steps = [POOL_RRMS]

            def pool_op(out, a, b, op):
                pool.wait_ge(pool_step, steps[0])
                nc.gpsimd.tensor_tensor(out, a, b, op).then_inc(pool_step, 1)
                steps[0] += 1

            def streams(x):
                return x[:, :].rearrange("p (n c) -> p n c", n=NS)

            def each(x):
                return x.unsqueeze(2).to_broadcast([TOK, NS, P])

            def stream_sum(x, out, plus=None):
                pool_op(x[:, 0:2 * P], x[:, 0:2 * P], x[:, 2 * P:4 * P], ALU.add)
                if plus is not None:
                    pool_op(x[:, 0:P], x[:, 0:P], x[:, P:2 * P], ALU.add)
                    pool_op(out, x[:, 0:P], plus, ALU.add)
                else:
                    pool_op(out, x[:, 0:P], x[:, P:2 * P], ALU.add)

            pool.wait_ge(dve_step, DVE_HP)
            pool_op(streams(t1), streams(xf), each(hp[:, 0:NS]), ALU.mult)
            stream_sum(t1, xpre[:, :])
            assert steps[0] == POOL_XPRE
            pool_op(t0[:, :], xf[:, :], gg[:, 3:4].to_broadcast([TOK, D]), ALU.mult)
            pool_op(t0[:, :], t0[:, :], x2[:, :], ALU.add)
            pool.wait_ge(act_step, ACT_YBR)
            pool_op(streams(t1), ybr[:, :].unsqueeze(1).to_broadcast([TOK, NS, P]), each(hp[:, NS:2 * NS]), ALU.mult)
            pool_op(ob[:, :], t0[:, :], t1[:, :], ALU.add)
            assert steps[0] == POOL_BASE
            pool.wait_ge(dve_step, DVE_HG)
            pool_op(streams(t1), streams(xf), each(hg[:, 3 * NS:4 * NS]), ALU.mult)
            stream_sum(t1, ob[:, 3 * P:4 * P], plus=ob[:, 3 * P:4 * P])
            assert steps[0] == POOL_END
        @block.vector
        def _(dve):
            count = [0]

            def step(ins, expect=None, wait=True):
                count[0] += 1
                ins.then_inc(dve_step, 1)
                if wait:
                    dve.wait_ge(dve_step, count[0])
                assert expect is None or expect == count[0], (expect, count[0])

            def half_stats(src, k, half):
                step(nc.vector.bn_stats(bnst[:, k, :], src[:, half]))

            def layer_stats(var_at):
                step(nc.vector.bn_aggr(mv[:, 0:2], bnst[:, :, :]))
                step(nc.vector.tensor_scalar(mv[:, 1:2], mv[:, 1:2], EPS, None, ALU.add), var_at)

            def normalise(dst, src, pool_at, at):
                dve.wait_ge(pool_step, pool_at)
                step(nc.vector.tensor_scalar(dst[:, :], src[:, :], mv[:, 0:1], mv[:, 2:3], ALU.subtract, ALU.mult), at)

            def ctx_lo(b, t):
                dve.wait_ge(ctx_hi_ready, KT * b + t + 1)
                dve.wait_ge(ctx_loaded[t], 16 * (b + 1))
                k = slice(t * P, (t + 1) * P)
                nc.vector.tensor_tensor(ct_lo[:, :, k], ctx_raw[:, t, :, :], ct_hi[:, :, k].bitcast(F32), ALU.subtract
                                        ).then_inc(ctx_lo_ready, 1)

            def q_rope(k):
                dve.wait_ge(q_projected, 2 * k + 2)
                need(dve, q_lo_ready, k)
                if k == 0:
                    dve.wait_ge(qtab_loaded, 16)

                def heads(x):
                    return x.rearrange("p (h t) -> p h t", t=TOK)

                for dst, frm, tab in ((rq, slice(0, P), 0), (rqs, slice(0, HALF), 1), (rqs, slice(HALF, P), 1)):
                    src = frm if tab == 0 else slice(HALF - frm.start, P + HALF - frm.stop)
                    last = nc.vector.tensor_tensor(heads(dst[frm, :]), heads(p_f[src, QC:2 * QC]),
                                                   qtab[src, tab:tab + 1, :].to_broadcast([frm.stop - frm.start, 4, TOK]),
                                                   ALU.mult)
                last.then_inc(q_products, 1)

            def k_rope(b, g, i):
                u = UNITS * b + g
                dve.wait_ge(k_projected, 4 * u + i + 1)
                need(dve, k_lo_ready, 4 * u + i - 1)
                if i == 0 and g == 0:
                    dve.wait_ge(rope_loaded, 32 * (b + 1))
                f = slice((i % 2) * HB, (i % 2 + 1) * HB)
                src = p_kv[i % 2]
                nc.vector.tensor_tensor(rc[:, i % 2, 0:HB], src[:, 0:HB], cos_sb[:, f], ALU.mult)
                nc.vector.tensor_tensor(rs[0:HALF, i % 2, 0:HB], src[HALF:P, 0:HB], sin_sb[HALF:P, f], ALU.mult)
                nc.vector.tensor_tensor(rs[HALF:P, i % 2, 0:HB], src[0:HALF, 0:HB], sin_sb[0:HALF, f], ALU.mult)\
                    .then_inc(k_products, 1)

            def v_low(b, g, i):
                u = UNITS * b + g
                dve.wait_ge(v_hi_ready, 4 * u + i + 1)
                n = len(piece_tiles(i))
                tiles = slice(2 * i, 2 * i + n)
                nc.vector.tensor_tensor(v_lo[:, tiles, :].rearrange("p t n -> p (t n)"), p_kv[i % 2][:, 0:n * 2 * DH],
                                        v_hi[:, tiles, :].bitcast(F32).rearrange("p t n -> p (t n)"), ALU.subtract
                                        ).then_inc(v_lo_ready, 1)

            def pt_low(h, p):
                dve.wait_ge(pt_hi_ready, 4 * h + p + 1)
                n = len(piece_tiles(p)) * QC
                nc.vector.tensor_tensor(pt_lo[:, p % 2, :, :].rearrange("p t n -> p (t n)")[:, 0:n], p_t[p % 2][:, 0:n],
                                        pt_hi[:, p % 2, :, :].bitcast(F32).rearrange("p t n -> p (t n)")[:, 0:n],
                                        ALU.subtract).then_inc(pt_lo_ready, 1)

            def mask_scores(b, g, s, i):
                h = 2 * (UNITS * b + g) + s
                n = 2 * h + i
                col = 2 * (2 * g + s) + i
                c = slice(col, col + 1)
                dve.wait_ge(scores_ready, n + 1)
                if i == 0:
                    if g == 0 and s == 0:
                        dve.wait_ge(mask_loaded, 32 * (b + 1))
                    need(dve, probs_transposed, 4 * (h - 1))
                    need(dve, scores_masked, 2 * h)
                nc.vector.tensor_copy(m_old[:, c], m_run[:, c]).then_inc(max_kept, 1)
                nc.vector.tensor_tensor_reduce(out=scores[:, 2 * s + i, :].rearrange("p (f n) -> p f n", f=2),
                                               in0=p_s[:, :, 0:HB], in1=mask_sb[:, :].rearrange("p (f n) -> p f n", f=2),
                                               scale=1.0, scalar=m_run[:, c], op0=ALU.add, op1=ALU.max,
                                               accum_out=m_run[:, c]).then_inc(scores_masked, 1)
                dve.wait_ge(scores_masked, n + 1)
                dve.wait_ge(max_kept, n + 1)
                nc.vector.tensor_tensor(m_drop[:, c], m_old[:, c], m_run[:, c], ALU.subtract).then_inc(max_dropped, 1)
                nc.vector.tensor_scalar(m_neg[:, c], m_run[:, c], -1.0, None, ALU.mult).then_inc(max_negated, 1)

            def keep_sums(h, g, s):
                c = slice(2 * (2 * g + s), 2 * (2 * g + s) + 2)
                dve.wait_ge(probs_ready, 2 * h + 2)
                dve.wait_ge(factor_ready, 2 * h + 2)
                need(dve, sums_kept, 2 * h)
                nc.vector.tensor_tensor(l_run[:, c], l_run[:, c], fac[:, c], ALU.mult).then_inc(sums_kept, 1)
                dve.wait_ge(sums_kept, 2 * h + 1)
                nc.vector.tensor_tensor(l_run[:, c], l_run[:, c], rsum[:, c], ALU.add).then_inc(sums_kept, 1)

            def acc_scale(h, head):
                dve.wait_ge(factor_spread, h + 1)
                need(dve, acc_added, h)
                nc.vector.tensor_tensor(acc[:, head, :], acc[:, head, :], p_f[:, 0:QC], ALU.mult).then_inc(acc_scaled, 1)

            def acc_add(h, head):
                dve.wait_ge(pv_done, 4 * h + 4)
                dve.wait_ge(acc_scaled, h + 1)
                nc.vector.tensor_tensor(acc[:, head, :], acc[:, head, :], p_o[:, 0:QC], ALU.add).then_inc(acc_added, 1)

            dve.wait_ge(x_loaded, 16)
            for k, half in enumerate(halves()):
                half_stats(x_sb, k, half)
            layer_stats(DVE_VAR)
            normalise(xn, x_sb, POOL_RSTD1, DVE_XN)
            for t in range(4):
                ctx_lo(0, t)
            dve.wait_ge(pe_step, PE_XNT)
            step(nc.vector.tensor_copy(xnT[:, :, :].rearrange("p c n -> p (c n)"), p_o[:, 0:DC * TOK]), DVE_XNT)
            for t in range(4, KT):
                ctx_lo(0, t)
            k_rope(0, 0, 0)
            k_rope(0, 0, 1)
            q_rope(0)
            k_rope(0, 0, 2)
            step(nc.vector.memset(m_run[:, :], -3.0e38))
            step(nc.vector.memset(l_run[:, :], 0.0), DVE_MIX)
            nc.vector.memset(acc[:, :, :].rearrange("p h n -> p (h n)"), 0.0).then_inc(acc_cleared, 1)
            dve.wait_ge(acc_cleared, 1)
            k_rope(0, 0, 3)

            def dve_slot(b, g, s, prev=True, last=False):
                h = 2 * (UNITS * b + g) + s
                ph = (2 * g + s - 1) % HKV

                def fill(i):
                    if s == 0:
                        v_low(b, g, i)
                    elif g < UNITS - 1:
                        k_rope(b, g + 1, i)
                    elif not last:
                        k_rope(b + 1, 0, i)
                    else:
                        dve.wait_ge(pe_step, PE_XNT + i + 1)
                        if i == 0:
                            dve.wait_ge(smask_loaded, 16)
                        step(nc.vector.tensor_tensor(mixw[:, i, :], p_kv[i % 2][:, :], smask_sb[:, i, :], ALU.mult))

                def split_ctx(at, *tiles):
                    if (g, s) == (UNITS - 1, at) and not last:
                        for t in tiles:
                            ctx_lo(b + 1, t)

                if prev:
                    pt_low(h - 1, 0)
                    acc_scale(h - 1, ph)
                mask_scores(b, g, s, 0)
                if prev:
                    pt_low(h - 1, 1)
                    if s == 0:
                        k_rope(b, g, 3)
                split_ctx(1, 4, 5, 6)
                fill(0)
                if isinstance(b, int) and b == 0 and h + 1 < HKV:
                    q_rope(h + 1)
                mask_scores(b, g, s, 1)
                if prev:
                    pt_low(h - 1, 2)
                fill(1)
                split_ctx(0, 0, 1)
                if prev:
                    pt_low(h - 1, 3)
                fill(2)
                split_ctx(0, 2, 3)
                if prev:
                    acc_add(h - 1, ph)
                keep_sums(h, g, s)
                if s == 0 or last and g == UNITS - 1:
                    fill(3)
            def dve_block(b, first=False, last=False):
                for g in range(UNITS):
                    for s in range(2):
                        dve_slot(b, g, s, prev=not (first and g == 0 and s == 0), last=last)

            dve_block(0, first=True)
            with dve.Fori(1, NB - 1) as b:
                dve_block(b)
            dve_block(NB - 1, last=True)
            h = 8 * NB - 1
            dve.wait_ge(sums_kept, 2 * h + 2)
            step(nc.vector.reciprocal(l_inv[:, :], l_run[:, :]), DVE_LINV)

            def acc_normalise(k):
                dve.wait_ge(inv_spread, k + 1)
                dve.wait_ge(acc_added, min(8 * (NB - 1) + 2 * k + 2, 8 * NB))
                nc.vector.tensor_tensor(acc[:, 2 * k:2 * k + 2, :], acc[:, 2 * k:2 * k + 2, :],
                                        p_s[:, k % 2, :].rearrange("p (h n) -> p h n", h=2), ALU.mult).then_inc(acc_normal, 1)

            pt_low(h, 0)
            acc_scale(h, HKV - 1)
            pt_low(h, 1)
            acc_normalise(0)
            acc_normalise(1)
            pt_low(h, 2)
            pt_low(h, 3)
            acc_normalise(2)
            acc_add(h, HKV - 1)
            acc_normalise(3)

            for k, half in enumerate(halves()):
                dve.wait_ge(pe_step, PE_Y + k)
                step(nc.vector.tensor_tensor(x1[:, half], p_kv[k][0:TOK, 0:D // 2], x_sb[:, half], ALU.add))
                half_stats(x1, k, half)
            layer_stats(DVE_VAR2)
            normalise(xn, x1, POOL_RSTD2, DVE_XN2)
            dve.wait_ge(pe_step, PE_X1T)
            step(nc.vector.tensor_copy(xnT[:, :, :].rearrange("p c n -> p (c n)"), p_f[:, 0:DC * TOK]), DVE_XNT2)
            dve.wait_ge(tail_loaded, 80)
            for k, half in enumerate(halves()):
                dve.wait_ge(pe_step, PE_Z + k)
                step(nc.vector.tensor_tensor(t0[:, half], (p_o, p_t[1])[k][0:TOK, 0:D // 2], b2_sb[:, half], ALU.add),
                     DVE_Z + k, wait=False)
            for k, half in enumerate(halves()):
                dve.wait_ge(act_step, ACT_GELU + k)
                step(nc.vector.tensor_tensor(x2[:, half], x2[:, half], x1[:, half], ALU.add))
                half_stats(x2, k, half)
            layer_stats(DVE_VAR3)
            normalise(xf, x2, POOL_RSTD3, DVE_XF)
            step(nc.vector.tensor_tensor_reduce(out=t0[:, :], in0=xf[:, :], in1=xf[:, :], scale=1.0, scalar=0.0,
                                                op0=ALU.mult, op1=ALU.add, accum_out=mv[:, 0:1]), DVE_SQ, wait=False)
            dve.wait_ge(pe_step, PE_XNT3)
            step(nc.vector.tensor_copy(xnT[:, :, :].rearrange("p c n -> p (c n)"), p_f[:, 0:DC * TOK]), DVE_XNT3,
                 wait=False)
            dve.wait_ge(dve_step, DVE_SQ)
            step(nc.vector.tensor_scalar(mv[:, 1:2], mv[:, 0:1], 1.0 / D, RMS_EPS, ALU.mult, ALU.add), DVE_MS)
            dve.wait_ge(act_step, ACT_GATE)
            step(nc.vector.tensor_scalar(gg[:, 1:2], gg[:, 0:1], 1.0, None, ALU.add))
            step(nc.vector.reciprocal(gg[:, 2:3], gg[:, 1:2]))
            step(nc.vector.tensor_tensor(gg[:, 3:4], gg[:, 0:1], gg[:, 2:3], ALU.mult), DVE_GATE)
            dve.wait_ge(pe_step, PE_LOGITS)
            dve.wait_ge(pool_step, POOL_RRMS)
            step(nc.vector.scalar_tensor_tensor(out=lg[:, :], in0=p_o[0:TOK, 0:24], scalar=mv[:, 2:3], in1=hb_sb[:, :],
                                                op0=ALU.mult, op1=ALU.add), DVE_LG)

            def fours(x):
                return x.rearrange("p (k n) -> p k n", n=4)

            step(nc.vector.tensor_reduce(mx6[:, :], fours(lg[:, :]), AX_X, ALU.max))
            step(nc.vector.tensor_tensor(fours(sh[:, :]), fours(lg[:, :]), mx6[:, :].unsqueeze(2).to_broadcast([TOK, 6, 4]),
                                         ALU.subtract))
            step(nc.vector.tensor_scalar(sh[:, 0:16], sh[:, 0:16], -SPREAD_FLOOR / INV_TAU, None, ALU.max), DVE_SHIFT,
                 wait=False)
            step(nc.vector.tensor_reduce(zlim[:, 0:1], lg[:, 0:16], AX_X, ALU.max), wait=False)
            step(nc.vector.tensor_reduce(zlim[:, 1:2], lg[:, 0:16], AX_X, ALU.min))
            step(nc.vector.tensor_tensor(zlim[:, 2:3], zlim[:, 0:1], zlim[:, 1:2], ALU.subtract), DVE_SPREAD, wait=False)

            def rows_of(x, order):
                return x[:, :].rearrange(f"p (i j) -> p {order}", j=NS)

            def inner(x):
                return x[:, :].unsqueeze(1).to_broadcast([TOK, NS, NS])

            def outer(x):
                return x[:, :].unsqueeze(2).to_broadcast([TOK, NS, NS])

            HALVES = (("i j", vv, uu), ("j i", uu, vv))

            def sink_weigh(r):
                nc.vector.tensor_tensor(rows_of(tt, "i j"), rows_of(kk, HALVES[r][0]), inner(HALVES[r][1]), ALU.mult
                                        ).then_inc(sk_linear, 1)

            def sink_sum(src):
                nc.vector.tensor_reduce(sums[:, :], rows_of(src, "i j"), AX_X, ALU.add).then_inc(sk_linear, 1)

            def sink_invert(r):
                nc.vector.reciprocal(HALVES[r][2][:, :], sums[:, :]).then_inc(sk_linear, 1)

            dve.wait_ge(act_step, ACT_K)
            sink_sum(kk)
            dve.wait_ge(act_step, ACT_HP)
            step(nc.vector.tensor_reduce(hsum[:, 0:2], fours(hp[:, :]), AX_X, ALU.add), wait=False)
            dve.wait_ge(sk_linear, 1)
            sink_invert(0)
            dve.wait_ge(dve_step, DVE_HP - 2)
            step(nc.vector.reciprocal(hsum[:, 2:4], hsum[:, 0:2]), wait=False)
            dve.wait_ge(sk_linear, 2)
            sink_weigh(1)
            dve.wait_ge(dve_step, DVE_HP - 1)
            step(nc.vector.tensor_tensor(fours(hp[:, :]), fours(hp[:, :]), hsum[:, 2:4].unsqueeze(2).to_broadcast([TOK, 2, 4]),
                                         ALU.mult), DVE_HP, wait=False)
            dve.wait_ge(sk_linear, 3)
            sink_sum(tt)
            dve.wait_ge(sk_linear, 4)
            sink_invert(1)
            dve.wait_ge(pe_step, PE_WIDE)
            step(nc.vector.tensor_reduce(wide[:, 0:1], p_t[0][0:1, 0:TOK], AX_X, ALU.max))
            step(nc.vector.tensor_scalar(wide_flag[:, :], wide[:, 0:1], SPREAD_MAX / INV_TAU, None, ALU.is_gt), DVE_FLAG)
            again = dve.value_load(wide_flag[0:1, 0:1])
            with dve.Fori(0, (SINK - 1) // SINK_UNROLL) as turn:
                for k in range(SINK_UNROLL):
                    for r in range(2):
                        done = 6 * (SINK_UNROLL * turn + k) + 3 * r + 5
                        dve.wait_ge(sk_linear, done)
                        sink_weigh(r)
                        dve.wait_ge(sk_linear, done + 1)
                        sink_sum(tt)
                        dve.wait_ge(sk_linear, done + 2)
                        sink_invert(r)
            dve.wait_ge(sk_linear, 6 * SINK - 1)
            nc.vector.tensor_tensor(rows_of(tt, "i j"), rows_of(kk, "i j"), inner(vv), ALU.mult).then_inc(sk_linear, 1)
            dve.wait_ge(sk_linear, 6 * SINK)
            nc.vector.tensor_tensor(rows_of(hres, "i j"), rows_of(tt, "i j"), outer(uu), ALU.mult).then_inc(sk_linear, 1)
            dve.wait_ge(sk_linear, 6 * SINK + 1)
            with dve.If(again == 1):
                t_in = rows_of(tt, "i j")
                e_in = rows_of(ee, "i j")
                nc.vector.memset(vv[:, :], 0.0).then_inc(sk_state, 1)
                nc.vector.tensor_scalar(zz[:, :], lg[:, 0:16], INV_TAU, None, ALU.mult).then_inc(sk_state, 1)
                with dve.Fori(0, SINK) as it:
                    for r, (order, other, mine) in enumerate(HALVES):
                        done = 8 * it + 4 * r + 2
                        dve.wait_ge(sk_state, done)
                        nc.vector.tensor_tensor(t_in, rows_of(zz, order), inner(other), ALU.add).then_inc(sk_state, 1)
                        dve.wait_ge(sk_state, done + 1)
                        nc.vector.tensor_reduce(mx4[:, :], t_in, AX_X, ALU.max).then_inc(sk_state, 1)
                        dve.wait_ge(sk_state, done + 2)
                        nc.vector.tensor_tensor(t_in, t_in, outer(mx4), ALU.subtract).then_inc(sk_shifted, 1)
                        dve.wait_ge(sk_exp, 2 * it + r + 1)
                        nc.vector.tensor_reduce(sm4[:, :], e_in, AX_X, ALU.add).then_inc(sk_summed, 1)
                        dve.wait_ge(sk_ln, 2 * it + r + 1)
                        nc.vector.tensor_tensor(mine[:, :], lns[:, :], mx4[:, :], ALU.add).then_inc(sk_state, 1)
                        dve.wait_ge(sk_state, done + 3)
                        nc.vector.tensor_scalar(mine[:, :], mine[:, :], -1.0, None, ALU.mult).then_inc(sk_state, 1)
                dve.wait_ge(sk_state, 8 * SINK + 2)
                nc.vector.tensor_tensor(t_in, rows_of(zz, "i j"), inner(vv), ALU.add).then_inc(sk_state, 1)
                dve.wait_ge(sk_state, 8 * SINK + 3)
                nc.vector.tensor_tensor(t_in, t_in, outer(uu), ALU.add).then_inc(sk_shifted, 1)
                dve.wait_ge(sk_exp, 2 * SINK + 1)
            step(nc.vector.tensor_scalar(hg[:, :], hres[:, :], gg[:, 2:3], None, ALU.mult), DVE_HG)
            dve.wait_ge(pool_step, POOL_BASE)
            for j in range(NS):
                for i in range(NS - 1):
                    o = ob[:, i * P:(i + 1) * P]
                    if j:
                        dve.wait_ge(dve_step, count[0] - 2)
                    step(nc.vector.scalar_tensor_tensor(out=o, in0=xf[:, j * P:(j + 1) * P],
                                                        scalar=hg[:, NS * i + j:NS * i + j + 1],
                                                        in1=o, op0=ALU.mult, op1=ALU.add), wait=False)
            assert count[0] == DVE_END, (count[0], DVE_END)


def rope_tables():
    import numpy as np
    inv = (np.float32(1.0) / np.power(np.float32(10000.0), np.arange(0, DH, 2, dtype=np.float32) / np.float32(DH))).astype(np.float32)
    ang = (np.arange(KEYS, dtype=np.float32)[:, None] * inv[None, :]).astype(np.float64)
    return np.cos(ang).astype(np.float32), np.sin(ang).astype(np.float32)


def kernel(x, ctx_4096, mask_BxSxS2_ff0, L0_xattn_wq, L0_xattn_wk, L0_xattn_wv, L0_xattn_wo, L0_attn_w1, L0_attn_w2,
           L0_attn_b2, L0_attn_sparse_mask, L0_ffn_W_res, L0_ffn_W_pre, L0_ffn_W_post, L0_ffn_H_res_base,
           L0_ffn_H_pre_base, L0_ffn_H_post_base, L0_ffn_gate, L0_ffn_W_branch):
    import numpy as np
    import concourse.bacc as bacc
    from concourse.bass_utils import run_bass_kernel_spmd

    cos, sin = rope_tables()
    rows = lambda a, n: np.broadcast_to(np.asarray(a).reshape(1, -1), (n, np.asarray(a).size))
    arrays = {
        "x": np.asarray(x)[0],
        "ctxT": np.asarray(ctx_4096)[0].T,
        "mask": np.asarray(mask_BxSxS2_ff0)[0],
        "wq": L0_xattn_wq, "wk": L0_xattn_wk, "wv": L0_xattn_wv, "wo": L0_xattn_wo,
        "w1": L0_attn_w1, "w2t": np.asarray(L0_attn_w2).T, "b2": rows(L0_attn_b2, TOK), "smask": L0_attn_sparse_mask,
        "wffn": np.concatenate([np.asarray(L0_ffn_W_res), np.asarray(L0_ffn_W_pre), np.asarray(L0_ffn_W_post)]).T,
        "hbase": rows(np.concatenate([np.asarray(L0_ffn_H_res_base).ravel(), np.asarray(L0_ffn_H_pre_base),
                                      np.asarray(L0_ffn_H_post_base)]), TOK),
        "gate": rows(L0_ffn_gate, TOK), "wbranch": L0_ffn_W_branch,
        "ident": np.eye(P, dtype=np.float32),
        "cosT": np.concatenate([cos.T, cos.T]), "sinT": np.concatenate([sin.T, -sin.T]),
        "qrope": np.stack([np.concatenate([cos.T, cos.T])[:, :TOK], np.concatenate([sin.T, -sin.T])[:, :TOK]],
                          axis=1) * np.float32(SCALE),
    }
    arrays = {k: np.ascontiguousarray(v) for k, v in arrays.items()}
    nc = bacc.Bacc("TRN2", target_bir_lowering=False, num_devices=1, dynamic_dma_scratch_size=4096)
    A = {k: nc.dram_tensor(f"in_{k}", v.shape, mybir.dt.from_np(v.dtype), kind="ExternalInput").ap()
         for k, v in arrays.items()}
    A["out"] = nc.dram_tensor("out_x", (TOK, D), F32, kind="ExternalOutput").ap()
    perceiver(nc, A)
    r = run_bass_kernel_spmd(nc, [{f"in_{k}": v for k, v in arrays.items()}], core_ids=[0])
    return r.results[0]["out_x"].reshape(1, TOK, D)
```
